# Optimizing a Trainium2 kernel written in Bass

```python
import numpy as np
import jax
import jax.numpy as jnp

def _softmax(x, axis=-1):
    return jax.nn.softmax(x, axis=axis)

def _gelu(x):
    return jax.nn.gelu(x, approximate=True)

def _silu(x):
    return jax.nn.silu(x)

def _sigmoid(x):
    return jax.nn.sigmoid(x)

def _layernorm(x, axis=-1, eps=1e-05):
    m = jnp.mean(x, axis=axis, keepdims=True)
    v = jnp.var(x, axis=axis, keepdims=True)
    return (x - m) / jnp.sqrt(v + eps)

def _scatter_add(tgt, idx, src, axis=0):
    return tgt.at[idx].add(src)

def _segment_sum(src, seg, n):
    return jax.ops.segment_sum(src, seg, n)
kernel_name = 'mk_seq_postln_d1_jaxref_r4_94e149'

def setup_inputs(seed: int=0):
    np.random.seed(seed)
    _w = jnp.asarray

    def _L0_attn_setup():
        import jax, jax.numpy as jnp
        import numpy as np
        EMBED_DIM = 256
        NUM_HEADS = 16

        def quat_norm(q, eps=1e-06):
            r, i, j, k = jnp.split(q, 4, axis=-1)
            n = jnp.sqrt(r * r + i * i + j * j + k * k + eps)
            return jnp.concatenate([r / n, i / n, j / n, k / n], axis=-1)

        def quat_linear(x, W, b):
            B, T, D = x.shape
            D4 = D // 4
            xs = x.reshape(B, T, 4, D4)
            A = jnp.einsum('btcd,wdo->btcwo', xs, W) + b
            r = A[:, :, 0, 0] - A[:, :, 1, 1] - A[:, :, 2, 2] - A[:, :, 3, 3]
            i = A[:, :, 1, 0] + A[:, :, 0, 1] + A[:, :, 3, 2] - A[:, :, 2, 3]
            j = A[:, :, 2, 0] - A[:, :, 3, 1] + A[:, :, 0, 2] + A[:, :, 1, 3]
            k = A[:, :, 3, 0] + A[:, :, 2, 1] - A[:, :, 1, 2] + A[:, :, 0, 3]
            return jnp.concatenate([r, i, j, k], axis=-1)
        key = jax.random.key(seed)
        ks = jax.random.split(key, 10)
        B, T, D = (2, 512, EMBED_DIM)
        D4 = D // 4
        s = 0.02
        x = jax.random.normal(ks[0], (B, T, D), dtype=jnp.float32)

        def proj(kw, kb):
            W = jax.random.normal(kw, (4, D4, D4), dtype=jnp.float32) * s
            b = jax.random.normal(kb, (4, D4), dtype=jnp.float32) * s
            return (W, b)
        qW, qb = proj(ks[1], ks[2])
        kW, kb = proj(ks[3], ks[4])
        vW, vb = proj(ks[5], ks[6])
        oW, ob = proj(ks[7], ks[8])
        J = jax.random.normal(ks[9], (D,), dtype=jnp.float32) * 0.01
        return {'x': x, 'qW': qW, 'qb': qb, 'kW': kW, 'kb': kb, 'vW': vW, 'vb': vb, 'oW': oW, 'ob': ob, 'J': J}
    _L0_attn_in = _L0_attn_setup()

    def _L0_ffn_setup():
        import jax, jax.numpy as jnp
        import numpy as np
        E = 16
        G = 4
        EPG = E // G
        K = 4
        TOPK_GROUP = 2
        PER_GROUP_K = K // TOPK_GROUP

        def _route(xf, router_w, correction_bias):
            S = xf.shape[0]
            logits = xf @ router_w.T
            scores = jax.nn.sigmoid(logits)
            sb = scores + correction_bias
            grp_top = jax.lax.top_k(sb.reshape(S, G, EPG), PER_GROUP_K)[0]
            group_scores = grp_top.sum(axis=-1)
            _, group_idx = jax.lax.top_k(group_scores, TOPK_GROUP)
            group_mask = jnp.zeros((S, G), sb.dtype).at[jnp.arange(S)[:, None], group_idx].set(1.0)
            score_mask = jnp.broadcast_to(group_mask[:, :, None], (S, G, EPG)).reshape(S, E)
            masked = jnp.where(score_mask > 0, sb, -jnp.inf)
            _, topk_idx = jax.lax.top_k(masked, K)
            w = jnp.take_along_axis(scores, topk_idx, axis=1)
            w = w / (w.sum(axis=-1, keepdims=True) + 1e-20)
            return (topk_idx, w, scores)
        key = jax.random.key(seed)
        ks = jax.random.split(key, 9)
        B, T, C, H, HS = (2, 256, 256, 64, 512)
        std = 0.02
        return {'x': jax.random.normal(ks[0], (B, T, C), jnp.float32), 'router_w': jax.random.normal(ks[1], (E, C), jnp.float32) * std, 'correction_bias': jnp.zeros((E,), jnp.float32), 'gate_w': jax.random.normal(ks[2], (E, C, H), jnp.float32) * std, 'up_w': jax.random.normal(ks[3], (E, C, H), jnp.float32) * std, 'down_w': jax.random.normal(ks[4], (E, H, C), jnp.float32) * std, 'shared_gate_w': jax.random.normal(ks[5], (HS, C), jnp.float32) * std, 'shared_up_w': jax.random.normal(ks[6], (HS, C), jnp.float32) * std, 'shared_down_w': jax.random.normal(ks[7], (C, HS), jnp.float32) * std}
    _L0_ffn_in = _L0_ffn_setup()
    _d = {'L0_attn_x': _L0_attn_in['x'], 'L0_attn_qW': _L0_attn_in['qW'], 'L0_attn_qb': _L0_attn_in['qb'], 'L0_attn_kW': _L0_attn_in['kW'], 'L0_attn_kb': _L0_attn_in['kb'], 'L0_attn_vW': _L0_attn_in['vW'], 'L0_attn_vb': _L0_attn_in['vb'], 'L0_attn_oW': _L0_attn_in['oW'], 'L0_attn_ob': _L0_attn_in['ob'], 'L0_attn_J': _L0_attn_in['J'], 'L0_ffn_router_w': _L0_ffn_in['router_w'], 'L0_ffn_correction_bias': _L0_ffn_in['correction_bias'], 'L0_ffn_gate_w': _L0_ffn_in['gate_w'], 'L0_ffn_up_w': _L0_ffn_in['up_w'], 'L0_ffn_down_w': _L0_ffn_in['down_w'], 'L0_ffn_shared_gate_w': _L0_ffn_in['shared_gate_w'], 'L0_ffn_shared_up_w': _L0_ffn_in['shared_up_w'], 'L0_ffn_shared_down_w': _L0_ffn_in['shared_down_w']}
    _x0 = _d['L0_attn_x']
    _d['L0_attn_x'] = jax.random.normal(jax.random.fold_in(jax.random.key(seed), 1), (16, 1024, 256), dtype=_x0.dtype)
    del _x0
    return _d

def reference(L0_attn_x, L0_attn_qW, L0_attn_qb, L0_attn_kW, L0_attn_kb, L0_attn_vW, L0_attn_vb, L0_attn_oW, L0_attn_ob, L0_attn_J, L0_ffn_router_w, L0_ffn_correction_bias, L0_ffn_gate_w, L0_ffn_up_w, L0_ffn_down_w, L0_ffn_shared_gate_w, L0_ffn_shared_up_w, L0_ffn_shared_down_w):

    def _L0_attn_ref(x, qW, qb, kW, kb, vW, vb, oW, ob, J):
        import jax, jax.numpy as jnp
        import numpy as np
        EMBED_DIM = 256
        NUM_HEADS = 16

        def quat_norm(q, eps=1e-06):
            r, i, j, k = jnp.split(q, 4, axis=-1)
            n = jnp.sqrt(r * r + i * i + j * j + k * k + eps)
            return jnp.concatenate([r / n, i / n, j / n, k / n], axis=-1)

        def quat_linear(x, W, b):
            B, T, D = x.shape
            D4 = D // 4
            xs = x.reshape(B, T, 4, D4)
            A = jnp.einsum('btcd,wdo->btcwo', xs, W) + b
            r = A[:, :, 0, 0] - A[:, :, 1, 1] - A[:, :, 2, 2] - A[:, :, 3, 3]
            i = A[:, :, 1, 0] + A[:, :, 0, 1] + A[:, :, 3, 2] - A[:, :, 2, 3]
            j = A[:, :, 2, 0] - A[:, :, 3, 1] + A[:, :, 0, 2] + A[:, :, 1, 3]
            k = A[:, :, 3, 0] + A[:, :, 2, 1] - A[:, :, 1, 2] + A[:, :, 0, 3]
            return jnp.concatenate([r, i, j, k], axis=-1)
        B, T, D = x.shape
        H = NUM_HEADS
        Dh = D // H
        scale = Dh ** (-0.5)
        q = quat_norm(quat_linear(x, qW, qb))
        k = quat_norm(quat_linear(x, kW, kb))
        v = quat_linear(x, vW, vb)
        q_ = q.reshape(B, T, H, Dh)
        k_ = k.reshape(B, T, H, Dh)
        v_ = v.reshape(B, T, H, Dh)
        scores = jnp.einsum('bthd,bshd->bhts', q_, k_) * scale
        scores = scores + jnp.mean(jnp.sin(J[:T])) * 0.1
        attn = jax.nn.softmax(scores, axis=-1)
        out = jnp.einsum('bhts,bshd->bthd', attn, v_).reshape(B, T, D)
        return quat_linear(out, oW, ob)

    def _L0_ffn_ref(x, router_w, correction_bias, gate_w, up_w, down_w, shared_gate_w, shared_up_w, shared_down_w):
        import jax, jax.numpy as jnp
        import numpy as np
        E = 16
        G = 4
        EPG = E // G
        K = 4
        TOPK_GROUP = 2
        PER_GROUP_K = K // TOPK_GROUP

        def _route(xf, router_w, correction_bias):
            S = xf.shape[0]
            logits = xf @ router_w.T
            scores = jax.nn.sigmoid(logits)
            sb = scores + correction_bias
            grp_top = jax.lax.top_k(sb.reshape(S, G, EPG), PER_GROUP_K)[0]
            group_scores = grp_top.sum(axis=-1)
            _, group_idx = jax.lax.top_k(group_scores, TOPK_GROUP)
            group_mask = jnp.zeros((S, G), sb.dtype).at[jnp.arange(S)[:, None], group_idx].set(1.0)
            score_mask = jnp.broadcast_to(group_mask[:, :, None], (S, G, EPG)).reshape(S, E)
            masked = jnp.where(score_mask > 0, sb, -jnp.inf)
            _, topk_idx = jax.lax.top_k(masked, K)
            w = jnp.take_along_axis(scores, topk_idx, axis=1)
            w = w / (w.sum(axis=-1, keepdims=True) + 1e-20)
            return (topk_idx, w, scores)
        B, T, C = x.shape
        S = B * T
        xf = x.reshape(S, C)
        sg = xf @ shared_gate_w.T
        su = xf @ shared_up_w.T
        shared_out = jax.nn.silu(sg) * su @ shared_down_w.T
        topk_idx, w, _scores = _route(xf, router_w, correction_bias)
        combine = jnp.zeros((S, E), xf.dtype).at[jnp.arange(S)[:, None], topk_idx].add(w)
        g = jnp.einsum('sc,ech->esh', xf, gate_w)
        u = jnp.einsum('sc,ech->esh', xf, up_w)
        h = jax.nn.silu(g) * u
        hw = h * combine.T[:, :, None]
        routed = jnp.einsum('esh,ehc->sc', hw, down_w)
        return (shared_out + routed).reshape(B, T, C)
    x = L0_attn_x
    x = _layernorm(x + _L0_attn_ref(x, L0_attn_qW, L0_attn_qb, L0_attn_kW, L0_attn_kb, L0_attn_vW, L0_attn_vb, L0_attn_oW, L0_attn_ob, L0_attn_J), axis=-1)
    x = _layernorm(x + _L0_ffn_ref(x, L0_ffn_router_w, L0_ffn_correction_bias, L0_ffn_gate_w, L0_ffn_up_w, L0_ffn_down_w, L0_ffn_shared_gate_w, L0_ffn_shared_up_w, L0_ffn_shared_down_w), axis=-1)
    return x

_drawn_inputs = setup_inputs


def setup_inputs(seed=0):
    import zlib

    import numpy as np

    out = dict(_drawn_inputs(seed))
    spreads = {'L0_ffn_correction_bias': (0.0, 0.8)}
    factors = {'L0_attn_qW': 8.0,
     'L0_attn_qb': 27.069,
     'L0_attn_kW': 8.0,
     'L0_attn_kb': 59.987,
     'L0_attn_vW': 8.0,
     'L0_attn_vb': 4.179,
     'L0_attn_oW': 4.023,
     'L0_ffn_router_w': 8.0,
     'L0_ffn_gate_w': 8.0,
     'L0_ffn_up_w': 8.0,
     'L0_ffn_down_w': 8.0,
     'L0_attn_J': 64.0,
     'L0_ffn_shared_gate_w': 7.5,
     'L0_ffn_shared_up_w': 7.475,
     'L0_ffn_shared_down_w': 7.505}
    for name, (base, spread) in spreads.items():
        noise = np.random.default_rng([zlib.crc32(name.encode()), seed]).standard_normal(out[name].shape)
        drawn = base * np.exp(spread * noise) if base else spread * noise
        out[name] = jnp.asarray(drawn.astype(out[name].dtype))
    for name, factor in factors.items():
        out[name] = (out[name] * factor).astype(out[name].dtype)
    return out
```

```python
from contextlib import ExitStack

import concourse.bass as bass
import numpy as np
from concourse import mybir

ALU = mybir.AluOpType
ACT = mybir.ActivationFunctionType
F32 = mybir.dt.float32
F16 = mybir.dt.float16
BF16 = mybir.dt.bfloat16
AX = mybir.AxisListType.X

P = 128
B, T, D = 16, 1024, 256
HEADS, DH, COMP = 16, 16, 64
NHG = 4
ST = T // P
QS = 256.0
SIGN = {(1, 0): -1.0, (2, 0): -1.0, (3, 0): -1.0, (2, 1): -1.0, (3, 2): -1.0, (1, 3): -1.0}
NTOK = B * T
TB = 512
NTB = NTOK // TB
SUB = TB // P
E, EH, HS = 16, 64, 512
CR, CS = E * EH // P, HS // P
CH = CR + CS
TAKEN = -3e38
XS = 256.0


RSQRT = ("x", "half", "y0", "u1", "v1", "y1", "u2", "v2", "y2", "u3", "v3", "y3")


def rsqrt(dve, V, S, rnd, last, y, x, u, eps, scale):
    def step(ins):
        ins.then_inc(S.sem, 1)
    I32 = mybir.dt.int32
    S.wait(dve, rnd, last)
    step(V.tensor_scalar(u, x, eps, scale, ALU.add, ALU.mult))
    S.wait(dve, rnd, "x")
    step(V.tensor_scalar(y.bitcast(I32), u.bitcast(I32), 1, None, ALU.logical_shift_right))
    S.wait(dve, rnd, "half")
    step(V.tensor_scalar(y.bitcast(I32), y.bitcast(I32), -1.0, float(0x5f3759df), ALU.mult, ALU.add))
    for n in (1, 2, 3):
        S.wait(dve, rnd, f"y{n - 1}")
        step(V.tensor_tensor(x, y, y, ALU.mult))
        S.wait(dve, rnd, f"u{n}")
        step(V.scalar_tensor_tensor(out=x, in0=x, scalar=-0.5, in1=u, op0=ALU.mult, op1=ALU.mult))
        S.wait(dve, rnd, f"v{n}")
        step(V.scalar_tensor_tensor(out=y, in0=x, scalar=1.5, in1=y, op0=ALU.add, op1=ALU.mult))


class Steps:

    def __init__(self, sem, names):
        self.sem, self.at, self.n = sem, {s: i + 1 for i, s in enumerate(names)}, len(names)

    def wait(self, eng, rnd, step):
        eng.wait_ge(self.sem, rnd * self.n + self.at[step])


def small_math(eng, nc, sem):
    count = [0]

    def link(ins):
        ins.then_inc(sem, 1)
        count[0] += 1
        eng.wait_ge(sem, count[0])
    return link, count


def attention(nc, x, qW, qb, kW, kb, vW, vb, oW, ob, J, x1):
    xrows = x.rearrange("b t d -> (b t) d")
    with ExitStack() as ctx:
        def sb(name, shape, dt=F32):
            return ctx.enter_context(nc.sbuf_tensor(name, shape, dt))

        def sem(name):
            return ctx.enter_context(nc.semaphore(name))

        kst = sb("k_stat", [P, 2, HEADS // 2, 2, T], F16)
        qmv = sb("q_mov", [P, 2, HEADS // 2, T], F16)
        vall = sb("v_all", [P, 2, ST, D])
        vstat = sb("v_stat", [P, ST, 4, 2, DH])
        prob = sb("prob", [P, 8, T])
        osb = sb("osb", [P, T])
        rden = sb("rden", [P, 2, 16])
        ot = sb("ot", [P, T])
        ysb = sb("y", [P, 2, ST, D])
        xt = sb("x_tile", [P, 2, D])
        xT = sb("xT", [P, 2, P])
        qkb = sb("qkb", [P, 2, 4, COMP])
        qkn = sb("qkn", [P, 2, 4, COMP])
        n2 = sb("n2", [P, 2, COMP])
        rn = sb("rn", [P, 2, COMP])
        nu = sb("nu", [P, 2, COMP])
        parts = sb("parts", [P, 2, HEADS, 4, DH], F16)
        wqkv = sb("wqkv", [P, 2, 3, D])
        wo = sb("wo", [P, NHG, D])
        bqkv = sb("bqkv", [P, 3, D])
        bo = sb("bo", [P, D])
        id32 = sb("id32", [P, P])
        id16 = sb("id16", [P, P], F16)
        jt = sb("jt", [P, 4])
        st6 = sb("st6", [P, ST, 6])
        mv = sb("mv", [P, ST, 2])
        rstd = sb("rstd", [P, ST])
        ru = sb("ru", [P, ST])
        spare = sb("spare", [P, 1])
        pspare = sb("pspare", [P, ST])
        base = prob[:, 0:3, :].rearrange("p a b -> p (a b)")
        wbase = base[:, 0:768].rearrange("p (m w o) -> p m w o", m=3, w=4)
        wobase = base[:, 768:1024].rearrange("p (w o) -> p w o", w=4)
        bbase = base[:, 1024:2048].rearrange("p (m w o) -> p m w o", m=4, w=4)
        jrow = base[:, 2048:2304]
        jk = base[:, 2304:2560]

        psS = ctx.enter_context(nc.psum_tensor("psS", [P, 2, T], F32))
        psO = ctx.enter_context(nc.psum_tensor("psO", [P, 2, 512], F32))
        pr0 = ctx.enter_context(nc.psum_tensor("pr0", [P, 512], F32))
        pr1 = ctx.enter_context(nc.psum_tensor("pr1", [P, 512], F32))
        pr0h = pr0[:].bitcast(F16)
        pr1h = pr1[:].bitcast(F16)

        w_loaded = sem("w_loaded")
        pool_setup = sem("pool_setup")
        dve_setup = sem("dve_setup")
        act_setup = sem("act_setup")
        x_loaded = [sem(f"x_loaded{k}") for k in range(2)]
        y_loaded = sem("y_loaded")
        y_biased = sem("y_biased")
        x1_stored = sem("x1_stored")
        scores_done = sem("scores_done")
        exp_done = sem("exp_done")
        pv_done = sem("pv_done")
        v_staged = sem("v_staged")
        proj_done = sem("proj_done")
        proj_added = sem("proj_added")
        PE_X = Steps(sem("pe_x"), ["xT"])
        PE_QKV = Steps(sem("pe_qkv"), ["qk", "v"])
        PE_T = Steps(sem("pe_t"), ["qT", "kT"])
        DV_X = Steps(sem("dve_x"), ["xT"])
        DV_QKV = Steps(sem("dve_qkv"), ["qk", "v", "sq", "n2", *RSQRT, "norm", "qhi", "khi0", "khi1", "qlo", "klo0", "klo1"])
        DV_T = Steps(sem("dve_t"), ["qT", "kT0", "kT1"])
        DV_LN = Steps(sem("dve_ln"), [f"stats{s}" for s in range(ST)] + [f"mean{s}" for s in range(ST)] + [*RSQRT]
                      + [f"out{s}" for s in range(ST)])
        DV_NORM = Steps(sem("dve_norm"), ["o0", "o1", "r0", "m0", "n0", "r1", "m1", "n1"])

        NW = 6 + 4 + 4 + 1
        block = ctx.enter_context(nc.Block())

        def each_iteration(eng, prologue, body, tail, batch_end=lambda b, par: None):
            def batch(b, par, edge):
                body(b * 4, 0, b, par, edge)
                with eng.Fori(1, NHG) as hg:
                    body(b * 4 + hg, hg, b, par, edge)
                batch_end(b, par)
            prologue()
            batch(0, 0, "first")
            with eng.Fori(0, (B - 2) // 2) as b2:
                for odd in range(2):
                    batch(b2 * 2 + 1 + odd, 1 - odd, "")
            batch(B - 1, 1, "last")
            tail()

        def is_first(hg):
            return isinstance(hg, int)

        OGROUPS = [(5, 0, 0), (6, 1, 2), (11, 0, 4), (12, 1, 6)]
        NOG = len(OGROUPS)

        @block.sync
        def _(sp):
            for m, w in enumerate((qW, kW, vW)):
                for half in range(2):
                    sp.dma_start(wbase[64 * half:64 * half + 64, m], w.rearrange("w d o -> d w o")).then_inc(w_loaded, 16)
            for j in range(4):
                sp.dma_start(wobase[32 * j:32 * j + DH], oW[:, DH * j:DH * j + DH].rearrange("w d o -> d w o")).then_inc(w_loaded, 16)
            for m, v in enumerate((qb, kb, vb, ob)):
                sp.dma_start(bbase[:, m], v.partition_broadcast(P)).then_inc(w_loaded, 16)
            sp.dma_start(jrow, J.partition_broadcast(P)).then_inc(w_loaded, 16)

            def load_x(r, k, u, wait):
                if wait:
                    PE_X.wait(sp, u - 2, "xT")
                sp.dma_start(xt[:, k, :], xrows[bass.ds(u * P, P), :]).then_inc(x_loaded[k], 16)

            def prologue():
                for k in range(2):
                    load_x(0, k, k, False)
                with sp.Fori(1, 4) as r:
                    for k in range(2):
                        load_x(r, k, r * 2 + k, True)

            def body(g, hg, b, par, edge):
                if edge != "last":
                    for k in range(2):
                        load_x(g + 4, k, (g + 4) * 2 + k, True)
                if is_first(hg):
                    if edge != "first":
                        sp.wait_ge(x1_stored, b * 16)
                    sp.dma_start(ysb[:, par], token_tiles(xrows, b)).then_inc(y_loaded, 16)

            def token_tiles(rows, b):
                return rows[bass.ds(b * T, T), :].rearrange("(s p) d -> p s d", p=P)

            def store(b, par):
                DV_LN.wait(sp, b, f"out{ST - 1}")
                sp.dma_start(token_tiles(x1, b), ysb[:, par]).then_inc(x1_stored, 16)

            def batch_end(b, par):
                if isinstance(b, int) and b == 0:
                    sp.sem_inc(x1_stored, 16)
                else:
                    store(b - 1, 1 - par)

            def tail():
                store(B - 1, 1)
                sp.wait_ge(x1_stored, 16 * (B + 1))
            each_iteration(sp, prologue, body, tail, batch_end)

        @block.gpsimd
        def _(pool):
            link, _c = small_math(pool, nc, pool_setup)
            link(nc.gpsimd.memset(id32[:], 0.0))
            link(nc.gpsimd.affine_select(out=id32[:], in_=id32[:], compare_op=ALU.not_equal, fill=1.0, base=0,
                                         pattern=[[-1, P]], channel_multiplier=1))
            link(nc.gpsimd.tensor_copy(id16[:], id32[:]))
            for par in range(2):
                link(nc.gpsimd.memset(kst[64:128, par, :, 0, :].bitcast(F32), 0.0))
                link(nc.gpsimd.memset(kst[0:64, par, :, 1, :].bitcast(F32), 0.0))
            assert _c[0] == POOL_SETUP
            pool.wait_ge(dve_setup, DVE_SETUP)

            def stage_v(g, hg, par, s, first):
                if not first:
                    pool.wait_ge(pv_done, (g - 1) * 2 * ST + 2 * s + 2)
                    nc.gpsimd.tensor_tensor(pspare[:, s:s + 1], id32[:, 0:1], id32[:, 0:1], ALU.mult)
                src = vall[:, par, s, bass.ds(hg * COMP, COMP)].rearrange("p (j d) -> p j d", j=4)
                nc.gpsimd.tensor_copy(vstat[:, s, :, 0, :], src).then_inc(v_staged, 1)

            def body(g, hg, b, par, edge):
                if is_first(hg):
                    DV_QKV.wait(pool, b * ST + ST - 1, "v")
                for s in range(ST):
                    stage_v(g, hg, par, s, is_first(hg) and edge == "first")
                if is_first(hg):
                    pool.wait_ge(y_loaded, b * 16 + 16)
                    for s in range(ST):
                        nc.gpsimd.tensor_tensor(ysb[:, par, s], ysb[:, par, s], bo[:], ALU.add).then_inc(y_biased, 1)

            each_iteration(pool, lambda: None, body, lambda: None)

        @block.scalar
        def _(act):
            act.wait_ge(dve_setup, J_REDUCED)
            nc.scalar.activation(jk, jrow, ACT.Sin).then_inc(act_setup, 1)
            act.wait_ge(dve_setup, J_SUMMED)
            nc.scalar.activation(jt[:, 1:2], jt[:, 0:1], ACT.Exp, scale=0.1 / D).then_inc(act_setup, 1)

            def body(g, hg, b, par, edge):
                for n in range(4 * ST):
                    act.wait_ge(scores_done, g * 32 + n + 1)
                    if n % 4 == 0 and not (is_first(hg) and edge == "first" and n < 8):
                        act.wait_ge(pv_done, g * 2 * ST + (n // 4) * 2 - 2)
                    nc.scalar.activation(prob[:, n % 8, :], psS[:, n % 2, :], ACT.Exp,
                                         scale=DH ** -0.5 / (QS * QS)).then_inc(exp_done, 1)
            each_iteration(act, lambda: None, body, lambda: None)

        @block.vector
        def _(dve):
            V = nc.vector
            link, c = small_math(dve, nc, dve_setup)
            dve.wait_ge(w_loaded, 16 * NW)
            TWO_PI, MAGIC = float(2 * np.pi), 12582912.0
            link(V.tensor_scalar(jk, jrow, 1.0 / TWO_PI, MAGIC, ALU.mult, ALU.add))
            link(V.tensor_scalar(jk, jk, MAGIC, None, ALU.subtract))
            link(V.scalar_tensor_tensor(out=jrow, in0=jk, scalar=-6.28125, in1=jrow, op0=ALU.mult, op1=ALU.add))
            link(V.scalar_tensor_tensor(out=jrow, in0=jk, scalar=-(TWO_PI - 6.28125), in1=jrow, op0=ALU.mult, op1=ALU.add))
            link(V.tensor_scalar(jrow, jrow, 3.1415925, -3.1415925, ALU.min, ALU.max))
            assert c[0] == J_REDUCED
            dve.wait_ge(act_setup, 1)
            link(V.tensor_reduce(jt[:, 0:1], jk, AX, ALU.add))
            assert c[0] == J_SUMMED
            dve.wait_ge(act_setup, 2)
            ec = jt[:, 1:2]
            for i in range(4):
                rows = slice(64 * (i % 2), 64 * (i % 2) + 64)
                for o in range(4):
                    sgn = SIGN.get((i, o), 1.0)
                    cols = slice(o * COMP, o * COMP + COMP)
                    link(V.tensor_scalar(wqkv[rows, i // 2, :, cols], wbase[rows, :, o ^ i, :], sgn, None, ALU.mult))
                    if i == 0 and o == 0:
                        link(V.memset(wo[:], 0.0))
                    for j in range(4):
                        r = slice(32 * j, 32 * j + DH)
                        link(V.tensor_scalar(wo[r, i, cols], wobase[r, o ^ i, :], sgn, None, ALU.mult))
                    for dst, src in ((bqkv[:, :, cols], bbase[:, 0:3, o ^ i, :]), (bo[:, cols], bbase[:, 3, o ^ i, :])):
                        if i == 0:
                            link(V.tensor_copy(dst, src))
                        else:
                            link(V.tensor_tensor(dst, dst, src, ALU.add if sgn > 0 else ALU.subtract))
            link(V.tensor_scalar(bqkv[:, 2], bqkv[:, 2], ec, None, ALU.mult))
            link(V.memset(vstat[:], 1.0))
            link(V.tensor_scalar(vstat[:, :, :, 1, :].rearrange("p s j d -> p (s j) d"), vstat[:, :, :, 1, :].rearrange("p s j d -> p (s j) d"), ec, None, ALU.mult))
            assert c[0] == DVE_SETUP, c[0]
            dve.sem_inc(proj_added, 1)

            def step(S, ins):
                ins.then_inc(S.sem, 1)

            S = DV_QKV
            hi_q = parts[:, 0, :, 0:2, :]
            lo_q = parts[:, 0, :, 2:4, :]

            def by_head(a, m):
                return a[:, m].rearrange("p c (j d) -> p (c j) d", j=4)

            def take_x(u):
                PE_X.wait(dve, u, "xT")
                step(DV_X, V.tensor_copy(xT[:], pr0[:, 0:256].rearrange("p (a b) -> p a b", a=2)))

            def take_qk(u):
                PE_QKV.wait(dve, u, "qk")
                step(S, V.tensor_tensor(qkb[:].rearrange("p m c o -> p (m c o)"), pr1[:], bqkv[:, 0:2].rearrange("p m o -> p (m o)"), ALU.add))

            def take_v(u, par, s, staged):
                PE_QKV.wait(dve, u, "v")
                if staged is not None:
                    dve.wait_ge(v_staged, staged)
                step(S, V.scalar_tensor_tensor(out=vall[:, par, s, :], in0=pr0[:, 0:256], scalar=ec, in1=bqkv[:, 2],
                                               op0=ALU.mult, op1=ALU.add))

            def normalise_and_split(u):
                S.wait(dve, u, "qk")
                step(S, V.tensor_tensor(qkn[:], qkb[:], qkb[:], ALU.mult))
                S.wait(dve, u, "sq")
                step(S, V.tensor_reduce(n2[:], qkn[:].rearrange("p m c o -> p m o c"), AX, ALU.add))
                rsqrt(dve, V, S, u, "n2", rn[:], n2[:], nu[:], 1e-6, 1.0 / (QS * QS))
                S.wait(dve, u, RSQRT[-1])
                for_m = rn[:].unsqueeze(2).to_broadcast([P, 2, 4, COMP])
                step(S, V.tensor_tensor(qkn[:], qkb[:], for_m, ALU.mult))
                S.wait(dve, u, "norm")
                q, k = by_head(qkn, 0), by_head(qkn, 1)
                step(S, V.tensor_copy(hi_q, q.unsqueeze(2).to_broadcast([P, HEADS, 2, DH])))
                for t in (0, 2):
                    step(S, V.tensor_copy(parts[:, 1, :, t, :], k))
                S.wait(dve, u, "khi1")
                step(S, V.tensor_tensor(lo_q, q.unsqueeze(2).to_broadcast([P, HEADS, 2, DH]), hi_q, ALU.subtract))
                for t in (1, 3):
                    step(S, V.tensor_tensor(parts[:, 1, :, t, :], k, parts[:, 1, :, 0, :], ALU.subtract))

            def take_transposes(u, par, s):
                tok = bass.ds(s * P, P)
                PE_T.wait(dve, u, "qT")
                step(DV_T, V.tensor_copy(qmv[:, par, :, tok], pr1h.rearrange("p (a t) -> p a t", t=P)))
                PE_T.wait(dve, u, "kT")
                for e in range(2):
                    r = slice(64 * e, 64 * e + 64)
                    step(DV_T, V.tensor_copy(kst[r, par, :, e, tok], pr0h[r].rearrange("p (a t) -> p a t", t=P)))

            def norm(g):
                N = DV_NORM
                def turn(h):
                    dve.wait_ge(pv_done, g * 2 * ST + 2 * ST - 1 + h)
                    step(N, V.transpose(osb[:, 512 * h:512 * h + 512], psO[:, h, :]))

                def divide(h):
                    cols = slice(512 * h, 512 * h + 512)
                    blocks = osb[:, cols].rearrange("p (b r) -> p b r", r=32)
                    N.wait(dve, g, f"o{h}")
                    step(N, V.reciprocal(rden[:, h], blocks[:, :, DH]))
                    N.wait(dve, g, f"r{h}")
                    step(N, V.tensor_tensor(blocks, blocks, rden[:, h].unsqueeze(2).to_broadcast([P, 16, 32]), ALU.mult))
                    N.wait(dve, g, f"m{h}")
                    step(N, V.transpose(ot[:, cols], osb[:, cols]))
                return turn, divide

            def add_proj(g, par, i):
                _, bank, t = OGROUPS[i]
                dve.wait_ge(proj_done, g * NOG + i + 1)
                dst = ysb[:, par, t:t + 2].rearrange("p s d -> p (s d)")
                V.tensor_tensor(dst, dst, (pr1 if bank else pr0)[:], ALU.add).then_inc(proj_added, 1)

            def ln(n, par):
                dve.wait_ge(proj_added, (n + 1) * NHG * NOG + 1)
                for s in range(ST):
                    step(DV_LN, V.bn_stats(st6[:, s, :], ysb[:, par, s, :]))
                DV_LN.wait(dve, n, f"stats{ST - 1}")
                V.memset(spare[:], 0.0)
                for s in range(ST):
                    step(DV_LN, V.bn_aggr(mv[:, s, :], st6[:, s, :]))
                rsqrt(dve, V, DV_LN, n, f"mean{ST - 1}", rstd[:], mv[:, :, 1], ru[:], 1e-5, 1.0)
                DV_LN.wait(dve, n, RSQRT[-1])
                for s in range(ST):
                    step(DV_LN, V.tensor_scalar(ysb[:, par, s, :], ysb[:, par, s, :], mv[:, s, 0:1], rstd[:, s:s + 1],
                                                ALU.subtract, ALU.mult))

            def prologue():
                with dve.Fori(0, 4) as r:
                    a, b = r * 2, r * 2 + 1
                    take_x(a)
                    take_qk(a)
                    take_v(a, 0, a, None)
                    take_x(b)
                    normalise_and_split(a)
                    take_transposes(a, 0, a)
                    take_qk(b)
                    take_v(b, 0, b, None)
                    normalise_and_split(b)
                    take_transposes(b, 0, b)

            def body(g, hg, b, par, edge):
                po = 1 - par if is_first(hg) else par
                nxt = 1 - par
                prep, proj = edge != "last", not (is_first(hg) and edge == "first")
                ua, ub = (g + 4) * 2, (g + 4) * 2 + 1
                staged = None if edge == "first" else b * NHG * ST
                if proj:
                    turn, divide = norm(g - 1)
                    turn(0)
                if prep:
                    take_x(ua)
                if proj:
                    turn(1)
                    divide(0)
                if prep:
                    take_qk(ua)
                    take_v(ua, nxt, hg * 2, staged)
                    take_x(ub)
                    normalise_and_split(ua)
                if proj:
                    if not is_first(hg):
                        dve.wait_ge(y_biased, b * ST + ST)
                    add_proj(g - 1, po, 0)
                    add_proj(g - 1, po, 1)
                    divide(1)
                if prep:
                    take_transposes(ua, nxt, hg * 2)
                    take_qk(ub)
                    take_v(ub, nxt, hg * 2 + 1, staged)
                    normalise_and_split(ub)
                if proj:
                    add_proj(g - 1, po, 2)
                    add_proj(g - 1, po, 3)
                if prep:
                    take_transposes(ub, nxt, hg * 2 + 1)
                if is_first(hg) and proj:
                    ln(b - 1, po)

            def tail():
                turn, divide = norm(4 * B - 1)
                for h in range(2):
                    turn(h)
                for h in range(2):
                    divide(h)
                for i in range(NOG):
                    add_proj(4 * B - 1, 1, i)
                ln(B - 1, 1)
            each_iteration(dve, prologue, body, tail)

        @block.tensor
        def _(pe):
            pe.wait_ge(dve_setup, DVE_SETUP)
            pe.wait_ge(pool_setup, POOL_SETUP)

            def transposes_x(u, k, r):
                pe.wait_ge(x_loaded[k], r * 16 + 16)
                for a in range(2):
                    mm = pe.transpose(pr0[:, P * a:P * a + P], xt[:, k, P * a:P * a + P], id32[:])
                mm.then_inc(PE_X.sem, 1)

            def project_qk(u):
                DV_X.wait(pe, u, "xT")
                for a in range(2):
                    mm = pe.matmul(pr1[:], xT[:, a, :], wqkv[:, a, 0:2, :].rearrange("p m o -> p (m o)"), start=(a == 0), stop=(a == 1))
                mm.then_inc(PE_QKV.sem, 1)

            def project_v(u):
                for a in range(2):
                    mm = pe.matmul(pr0[:, 0:256], xT[:, a, :], wqkv[:, a, 2, :], start=(a == 0), stop=(a == 1))
                mm.then_inc(PE_QKV.sem, 1)

            def transposes_qk(u):
                DV_QKV.wait(pe, u, "klo1")
                for m, dst in ((0, pr1h), (1, pr0h)):
                    for a in range(HEADS // 2):
                        blk = parts[:, m, 2 * a:2 * a + 2].rearrange("p h s d -> p (h s d)")
                        mm = pe.transpose(dst[:, P * a:P * a + P], blk, id16[:])
                    mm.then_inc(PE_T.sem, 1)

            def out_proj(g, hp, i):
                _, bank, t0 = OGROUPS[i]
                DV_NORM.wait(pe, g, "n0" if t0 < 4 else "n1")
                for t in (t0, t0 + 1):
                    mm = pe.matmul((pr1 if bank else pr0)[:, 256 * (t - t0):256 * (t - t0) + 256], ot[:, P * t:P * t + P],
                                   wo[:, bass.ds(hp, 1), :].rearrange("p a o -> p (a o)"), start=True, stop=True)
                mm.then_inc(proj_done, 1)

            def added(g, i):
                pe.wait_ge(proj_added, g * NOG + i + 2)

            def scores(g, hg, par, s, j, first):
                n = 4 * s + j
                if not (first and n < 2):
                    pe.wait_ge(exp_done, g * 32 + n - 1)
                pair = hg * 2 + j // 2
                for h in range(2):
                    lhsT = kst[:, par, bass.ds(pair, 1), j % 2, P * s:P * s + P].rearrange("p a t -> p (a t)")
                    rhs = qmv[:, par, bass.ds(pair, 1), 512 * h:512 * h + 512].rearrange("p a t -> p (a t)")
                    mm = pe.matmul(psS[:, n % 2, 512 * h:512 * h + 512], lhsT, rhs, start=True, stop=True)
                mm.then_inc(scores_done, 1)

            def pv(g, s, h):
                if h == 0:
                    pe.wait_ge(exp_done, g * 32 + 4 * s + 4)
                    pe.wait_ge(v_staged, g * 8 + s + 1)
                if s == 0 and not (isinstance(g, int) and g == 0):
                    DV_NORM.wait(pe, g - 1, f"o{h}")
                for j in range(4):
                    mm = pe.matmul(psO[32 * j:32 * j + 32, h, :], vstat[:, s, j].rearrange("p a d -> p (a d)"),
                                   prob[:, (4 * s + j) % 8, 512 * h:512 * h + 512], start=(s == 0), stop=(s == ST - 1),
                                   tile_position=(0, 32 * j))
                mm.then_inc(pv_done, 1)

            def prologue():
                with pe.Fori(0, 4) as r:
                    a, b = r * 2, r * 2 + 1
                    transposes_x(a, 0, r)
                    project_qk(a)
                    project_v(a)
                    DV_QKV.wait(pe, a, "v")
                    transposes_x(b, 1, r)
                    DV_X.wait(pe, b, "xT")
                    transposes_qk(a)
                    DV_T.wait(pe, a, "kT1")
                    project_qk(b)
                    project_v(b)
                    transposes_qk(b)
                    DV_T.wait(pe, b, "kT1")

            def filler(g, hg, edge, slot):
                prep, proj = edge != "last", not (is_first(hg) and edge == "first")
                hp = 3 if is_first(hg) else hg - 1
                ua, ub = (g + 4) * 2, (g + 4) * 2 + 1
                if prep and slot == 0:
                    DV_T.wait(pe, ua - 1, "kT1")
                    transposes_x(ua, 0, g + 4)
                if prep and slot == 2:
                    project_qk(ua)
                if prep and slot == 3:
                    project_v(ua)
                if prep and slot == 4:
                    DV_QKV.wait(pe, ua, "v")
                    transposes_x(ub, 1, g + 4)
                if proj and slot == 5:
                    if prep:
                        DV_X.wait(pe, ub, "xT")
                    else:
                        added(g - 2, 2)
                    out_proj(g - 1, hp, 0)
                if proj and slot == 6:
                    if not prep:
                        added(g - 2, 3)
                    out_proj(g - 1, hp, 1)
                if prep and slot == 8:
                    if proj:
                        added(g - 1, 1)
                    else:
                        DV_X.wait(pe, ub, "xT")
                    transposes_qk(ua)
                if prep and slot == 9:
                    DV_T.wait(pe, ua, "kT1")
                    project_qk(ub)
                if prep and slot == 10:
                    project_v(ub)
                if proj and slot == 11:
                    if prep:
                        DV_QKV.wait(pe, ub, "v")
                    else:
                        added(g - 1, 0)
                    out_proj(g - 1, hp, 2)
                if proj and slot == 12:
                    if not prep:
                        added(g - 1, 1)
                    out_proj(g - 1, hp, 3)
                if prep and slot == 14:
                    if proj:
                        added(g - 1, 3)
                    transposes_qk(ub)

            def body(g, hg, b, par, edge):
                first = is_first(hg) and edge == "first"
                if is_first(hg):
                    DV_T.wait(pe, b * ST + ST - 1, "kT1")
                for s in range(ST):
                    for j in range(4):
                        scores(g, hg, par, s, j, first)
                        if j in (1, 2) and not (first and s == 0):
                            if s == 0:
                                pv(g - 1, ST - 1, j - 1)
                            else:
                                pv(g, s - 1, j - 1)
                        if j in (1, 3):
                            filler(g, hg, edge, 2 * s + j // 2)

            def tail():
                g = 4 * B - 1
                for h in range(2):
                    pv(g, ST - 1, h)
                for i in range(NOG):
                    if i < 2:
                        added(g - 1, i + 2)
                    else:
                        added(g, i - 2)
                    out_proj(g, 3, i)
            each_iteration(pe, prologue, body, tail)


J_REDUCED, J_SUMMED = 5, 6
DVE_SETUP = 6 + 16 * 7 + 1 + 3
POOL_SETUP = 3 + 4




def feed_forward(nc, x1, rw, cb, gw, uw, dw, sgw, suw, sdw, out):
    with ExitStack() as ctx:
        def sb(name, shape, dt=F32):
            return ctx.enter_context(nc.sbuf_tensor(name, shape, dt))

        def ps(name, shape):
            return ctx.enter_context(nc.psum_tensor(name, shape, F32))

        def sem(name):
            return ctx.enter_context(nc.semaphore(name))

        wf = sb("w_f32", [P, 3, CH * D])
        wg, wu = (wf[:, m].rearrange("p (a c h) -> p a c h", a=2, c=CH) for m in (0, 1))
        wd = wf[:, 2].rearrange("p (c o) -> p c o", c=CH)
        wh = sb("w_f16", [P, 3, 2, CH * D], F16)
        wg16, wu16 = (wh[:, m].rearrange("p t (a c h) -> p t a c h", a=2, c=CH) for m in (0, 1))
        wd16 = wh[:, 2].rearrange("p t (c o) -> p t c o", c=CH)
        wmax = sb("w_max", [P, 3])
        wall = sb("w_all", [P, 3])
        wscale = sb("w_scale", [P, 3])
        unscale = sb("unscale", [P, 3])
        wr = sb("w_router", [P, 2, E])
        sgl = sb("sg_load", [P, CS, D])
        sul = sb("su_load", [P, CS, D])
        sdl = sb("sd_load", [P, 2, HS])
        rl = sb("r_load", [P, D])
        cbias = sb("c_bias", [P, E])
        id32 = sb("id32b", [P, P])
        idb = sb("idb", [P, P], BF16)
        lower = sb("lower", [P, 4, 4])
        pick = sb("pick", [P, CR, P], BF16)
        xb = sb("xb", [P, 2, SUB, D])
        xT = sb("xTb", [P, 2, 2, TB])
        cT = sb("cT", [P, 2, TB], BF16)
        sig = sb("sig", [P, 2, TB])
        hid = sb("hid", [P, 2, TB])
        hid16 = sb("hid16", [P, 4, 2, TB], F16)
        xT16 = sb("xT16", [P, 2, 2, 2, TB], F16)
        sc = sb("sc", [P, SUB, E])
        sbias = sb("sbias", [P, SUB, E])
        masked = sb("masked", [P, SUB, E])
        w = sb("w", [P, SUB, E])
        mx = sb("mx", [P, SUB * 4, 2])
        mn = sb("mn", [P, SUB * 4, 2])
        tp = sb("tp", [P, 4, SUB * 4])
        gsum = sb("gsum", [P, SUB, 4])
        gmask = sb("gmask", [P, SUB, 4])
        gpen = sb("gpen", [P, SUB, 4])
        cg = sb("cg", [P, 2, SUB, 4, 4])
        best = sb("best", [P, SUB, 8])
        sel = sb("sel", [P, SUB, E])
        wsum = sb("wsum", [P, SUB])
        comb = sb("comb", [P, SUB, P], BF16)
        y = sb("yb", [P, SUB, D])
        st6 = sb("st6b", [P, SUB, 6])
        mv = sb("mvb", [P, SUB, 2])
        rstd = sb("rstdb", [P, SUB])
        ru = sb("rub", [P, SUB])
        spare = sb("spareb", [P, 1])

        psG, psU, psD = ps("psG", [P, 2, TB]), ps("psU", [P, 2, TB]), ps("psD", [P, 2, TB])
        psC, psF = ps("psC", [P, TB]), ps("psF", [P, TB])
        psFh = psF[:].bitcast(BF16)

        loads = [sem(n) for n in ("gate_loaded", "up_loaded", "down_loaded")]
        shared_loaded = sem("shared_loaded")
        high_setup = sem("high_setup")
        pool_setup, pe_setup, dve_setup = sem("fpool_setup"), sem("fpe_setup"), sem("fdve_setup")
        x_loaded = [sem(f"fx_loaded{k}") for k in range(2)]
        stored = sem("stored")
        wmax_all = sem("wmax_all")
        PE_F = Steps(sem("pe_front"), ["x0", "x1", "logits", "comb"])
        AC_F = Steps(sem("act_front"), ["x0", "h0", "x1", "h1", "sigmoid"])
        DV_X = Steps(sem("fdve_x"), ["l0", "l1"])
        RSTEPS = ["sb", "mx", "mn", "top1", "t2a", "t2b", "top2", "gsum", "ggt", "geq", "gtie", "gall", "grank",
                  "gmask", "gpen", "m1", "masked", *[f"best{s}" for s in range(SUB)], "spent",
                  *[f"taken{s}" for s in range(SUB)], "esel", "w", "ws", "wr", "rec",
                  "comb", "c1", "r1", "c2", "r2", "c3", "cT"]
        DV_F = Steps(sem("dve_front"), RSTEPS)
        PE_C = Steps(sem("pe_chunk"), [f"{n}{c}" for c in range(CH) for n in ("gate", "up", "comb")[:3 if c < CR else 2]])
        down_done = sem("down_done")
        sig_done = sem("sig_done")
        high_done, low_done = sem("high_done"), sem("low_done")
        DV_C = Steps(sem("dve_chunk"), [f"{n}{c}" for c in range(CH) for n in ("g", "u", "h")[:3 if c < CR else 2]])
        DV_L = Steps(sem("dve_lnb"), ["y"] + [f"s{i}" for i in range(SUB)] + [f"a{i}" for i in range(SUB)] + [*RSQRT]
                     + [f"n{i}" for i in range(SUB)])
        NLOADS = (2, 2, 1)
        NS = 7

        block = ctx.enter_context(nc.Block())

        def tiles(eng, prologue, main, tail):
            prologue()
            main(0, 0, "first")
            with eng.Fori(0, (NTB - 2) // 2) as h:
                for odd in range(2):
                    main(h * 2 + 1 + odd, 1 - odd, "")
            main(NTB - 1, 1, "last")
            tail()

        def rows(a, i):
            return a[bass.ds(i * TB, TB), :].rearrange("(s p) d -> p s d", p=P)

        def step(S, ins):
            ins.then_inc(S.sem, 1)

        def last_of(c):
            return f"h{c}" if c < CR else f"u{c}"

        @block.sync
        def _(sp):
            def load(i, k):
                sp.dma_start(xb[:, k], rows(x1, i)).then_inc(x_loaded[k], 16)

            def prologue():
                load(0, 0)
                sp.dma_start(rl[0:E], rw).then_inc(shared_loaded, 16)
                sp.dma_start(cbias[:], cb.partition_broadcast(P)).then_inc(shared_loaded, 16)
                for half in range(2):
                    sp.dma_start(wg[:, half, 0:CR, :].rearrange("p c (e h) -> p (c e) h", e=2),
                                 gw[:, P * half:P * half + P, :].rearrange("e c h -> c e h")).then_inc(loads[0], 16)
                sp.dma_start(wd[:, 0:CR, :], dw.rearrange("(c e) h o -> (e h) c o", e=2)).then_inc(loads[2], 16)
                sp.sem_inc(stored, 16)

            def store(i):
                DV_L.wait(sp, i, f"n{SUB - 1}")
                sp.dma_start(rows(out, i), y[:]).then_inc(stored, 16)

            def main(i, k, edge):
                if edge != "last":
                    if edge != "first":
                        DV_L.wait(sp, i - 1, "y")
                    load(i + 1, 1 - k)
                if edge != "first":
                    store(i - 1)

            def tail():
                store(NTB - 1)
                sp.wait_ge(stored, 16 * (NTB + 1))
            tiles(sp, prologue, main, tail)

        @block.gpsimd
        def _(pool):
            link, c = small_math(pool, nc, pool_setup)
            link(nc.gpsimd.memset(id32[:], 0.0))
            link(nc.gpsimd.affine_select(out=id32[:], in_=id32[:], compare_op=ALU.not_equal, fill=1.0, base=0,
                                         pattern=[[-1, P]], channel_multiplier=1))
            link(nc.gpsimd.tensor_copy(idb[:], id32[:]))
            link(nc.gpsimd.memset(lower[:], 1.0))
            link(nc.gpsimd.affine_select(out=lower[:], in_=lower[:], compare_op=ALU.is_gt, fill=0.0, base=0,
                                         pattern=[[1, 4], [-1, 4]], channel_multiplier=0))
            link(nc.gpsimd.memset(pick[:], 0.0))
            for part in range(3):
                v = pick[:].rearrange("p c (e h) -> p c e h", e=2)
                link(nc.gpsimd.affine_select(out=v, in_=v, compare_op=ALU.not_equal, fill=1.0, base=-E * part,
                                             pattern=[[-2, CR], [-1, 2], [0, EH]], channel_multiplier=1))
            link(nc.gpsimd.memset(comb[:], 0.0))
            assert c[0] == FPOOL_SETUP
            pool.wait_ge(dve_setup, MAXIMA)
            nc.gpsimd.partition_all_reduce(wall[:], wmax[:], P, bass.bass_isa.ReduceOp.max).then_inc(wmax_all, 1)

        @block.scalar
        def _(act):
            def front(i, k, what):
                if what < 2:
                    PE_F.wait(act, i, f"x{what}")
                    step(AC_F, nc.scalar.mul(xT[:, k, what, :], psF[:], XS))
                    step(AC_F, nc.scalar.mul(xT16[:, k, 0, what, :], psF[:], XS))
                else:
                    PE_F.wait(act, i, "logits")
                    step(AC_F, nc.scalar.activation(sc[:].rearrange("p s e -> p (s e)"), psF[:, 0:SUB * E], ACT.Sigmoid,
                                                    scale=1.0 / XS))

            def high(i, c, edge):
                if not (edge == "first" and c < 4):
                    act.wait_ge(down_done, i * CH + c - 3)
                DV_C.wait(act, i, last_of(c))
                nc.scalar.copy(hid16[:, c % 4, 0, :], hid[:, c % 2, :]).then_inc(high_done, 1)

            def prologue():
                for src, dst in ((sgw, sgl), (suw, sul), (sdw, sdl)):
                    act.dma_start(dst[:], src.rearrange("(s p) d -> p s d", p=P)).then_inc(shared_loaded, 16)
                for half in range(2):
                    act.dma_start(wu[:, half, 0:CR, :].rearrange("p c (e h) -> p (c e) h", e=2),
                                  uw[:, P * half:P * half + P, :].rearrange("e c h -> c e h")).then_inc(loads[1], 16)
                for what in range(3):
                    front(0, 0, what)
                act.wait_ge(dve_setup, SCALES)
                for m in range(3):
                    nc.scalar.activation(wh[:, m, 0], wf[:, m], ACT.Identity, scale=wscale[:, m:m + 1]).then_inc(high_setup, 1)

            def main(i, k, edge):
                for c in range(CH):
                    PE_C.wait(act, i, f"gate{c}")
                    if c >= 2:
                        DV_C.wait(act, i, f"u{c - 2}")
                    elif edge != "first":
                        DV_C.wait(act, i - 1, f"u{CH - 2 + c}")
                    nc.scalar.activation(sig[:, c % 2, :], psG[:, c % 2, :], ACT.Sigmoid,
                                         scale=unscale[:, 0:1]).then_inc(sig_done, 1)
                    if c:
                        high(i, c - 1, edge)
                    elif edge != "first":
                        high(i - 1, CH - 1, "")
                    if edge != "last" and c in (3, 4, 6):
                        front(i + 1, 1 - k, (3, 4, 6).index(c))
            tiles(act, prologue, main, lambda: high(NTB - 1, CH - 1, ""))

        @block.vector
        def _(dve):
            V = nc.vector
            banks = [psG[:, 0], psG[:, 1], psU[:, 0], psU[:, 1], psD[:, 0], psD[:, 1]]
            dsts = [wg[:, 0, CR:], wg[:, 1, CR:], wu[:, 0, CR:], wu[:, 1, CR:], wd[:, CR:, 0:P], wd[:, CR:, P:2 * P]]
            for n, (bank, dst) in enumerate(zip(banks, dsts)):
                dve.wait_ge(pe_setup, n + 2)
                V.tensor_copy(dst, bank.rearrange("p (s t) -> p s t", t=P)).then_inc(dve_setup, 1)
                if n == 0:
                    V.tensor_copy(wr[:], psC[:, 0:2 * E].rearrange("p (a e) -> p a e", a=2)).then_inc(dve_setup, 1)

            def find_maxima(*matrices):
                dve.wait_ge(dve_setup, NS)
                for m in matrices:
                    dve.wait_ge(loads[m], 16 * NLOADS[m])
                    V.tensor_reduce(wmax[:, m:m + 1], wf[:, m], AX, ALU.max, apply_absolute_value=True).then_inc(dve_setup, 1)

            def scale_weights():
                done = MAXIMA

                def link(ins):
                    nonlocal done
                    ins.then_inc(dve_setup, 1)
                    done += 1
                    dve.wait_ge(dve_setup, done)
                I32 = mybir.dt.int32
                dve.wait_ge(wmax_all, 1)
                link(V.tensor_scalar(wall[:], wall[:], 1e-15, None, ALU.max))
                link(V.tensor_scalar(wall[:].bitcast(I32), wall[:].bitcast(I32), 0x7f800000, None, ALU.bitwise_and))
                link(V.reciprocal(wscale[:], wall[:]))
                link(V.tensor_scalar(unscale[:, 1:2], wscale[:, 0:1], 2.0 ** -13 / XS, None, ALU.mult))
                link(V.tensor_scalar(wscale[:], wscale[:], 2.0 ** 10, None, ALU.mult))
                link(V.tensor_scalar(unscale[:, 0:1], wall[:, 0:1], 2.0 ** -10 / XS, None, ALU.mult))
                link(V.scalar_tensor_tensor(out=unscale[:, 2:3], in0=wall[:, 0:1], scalar=2.0 ** -7, in1=wall[:, 1:2], op0=ALU.mult, op1=ALU.mult))
                link(V.tensor_tensor(unscale[:, 2:3], unscale[:, 2:3], wall[:, 2:3], ALU.mult))
                assert done == SCALES
                for m in range(3):
                    dve.wait_ge(high_setup, m + 1)
                    V.scalar_tensor_tensor(out=wh[:, m, 1], in0=wf[:, m], scalar=wscale[:, m:m + 1], in1=wh[:, m, 0],
                                           op0=ALU.mult, op1=ALU.subtract).then_inc(dve_setup, 1)

            def low_x(i, k):
                for a in range(2):
                    AC_F.wait(dve, i, f"h{a}")
                    step(DV_X, V.tensor_tensor(xT16[:, k, 1, a, :], xT[:, k, a, :], xT16[:, k, 0, a, :], ALU.subtract))

            def low(i, c):
                dve.wait_ge(high_done, i * CH + c + 1)
                V.tensor_tensor(hid16[:, c % 4, 1, :], hid[:, c % 2, :], hid16[:, c % 4, 0, :], ALU.subtract).then_inc(low_done, 1)

            def tt(i, name, out_, a, b, op, after=None):
                if after:
                    DV_F.wait(dve, i, after)
                step(DV_F, V.tensor_tensor(out_, a, b, op))

            def router_steps(i, k):
                four = [P, SUB, 4, 4]
                mxv, mnv = mx[:], mn[:]
                g3 = masked[:].rearrange("p s (g m) -> p (s g) m", m=4)
                sb3 = sbias[:].rearrange("p s (g m) -> p (s g) m", m=4)
                gm3 = gmask[:].rearrange("p s g -> p (s g)").unsqueeze(2).to_broadcast([P, SUB * 4, 4])
                gp3 = gpen[:].rearrange("p s g -> p (s g)").unsqueeze(2).to_broadcast([P, SUB * 4, 4])

                def s0():
                    AC_F.wait(dve, i, "sigmoid")
                    tt(i, "sb", sbias[:], sc[:], cbias[:].unsqueeze(1).to_broadcast([P, SUB, E]), ALU.add)
                    tt(i, "mx", mxv, sb3[:, :, 0:4:2], sb3[:, :, 1:4:2], ALU.max, "sb")
                    tt(i, "mn", mnv, sb3[:, :, 0:4:2], sb3[:, :, 1:4:2], ALU.min)
                    tt(i, "top1", tp[:, 0], mxv[:, :, 0], mxv[:, :, 1], ALU.max, "mx")
                    tt(i, "t2a", tp[:, 1], mxv[:, :, 0], mxv[:, :, 1], ALU.min)
                    tt(i, "t2b", tp[:, 2], mnv[:, :, 0], mnv[:, :, 1], ALU.max, "mn")
                    tt(i, "top2", tp[:, 3], tp[:, 1], tp[:, 2], ALU.max, "t2b")
                    tt(i, "gsum", gsum[:].rearrange("p s g -> p (s g)"), tp[:, 0], tp[:, 3], ALU.add, "top2")

                def s1():
                    other, own = gsum[:].unsqueeze(2).to_broadcast(four), gsum[:].unsqueeze(3).to_broadcast(four)
                    tt(i, "ggt", cg[:, 0], other, own, ALU.is_gt, "gsum")
                    tt(i, "geq", cg[:, 1], other, own, ALU.is_equal)
                    tt(i, "gtie", cg[:, 1], cg[:, 1], lower[:].unsqueeze(1).to_broadcast(four), ALU.mult, "geq")
                    tt(i, "gall", cg[:, 0], cg[:, 0], cg[:, 1], ALU.add, "gtie")
                    DV_F.wait(dve, i, "gall")
                    step(DV_F, V.tensor_reduce(gpen[:], cg[:, 0], AX, ALU.add))
                    DV_F.wait(dve, i, "grank")
                    step(DV_F, V.tensor_scalar(gmask[:], gpen[:], 2.0, None, ALU.is_lt))
                    DV_F.wait(dve, i, "gmask")
                    step(DV_F, V.tensor_scalar(gpen[:], gmask[:], 1.0, 1e30, ALU.subtract, ALU.mult))
                    tt(i, "m1", g3, sb3, gm3, ALU.mult, "gpen")
                    tt(i, "masked", g3, g3, gp3, ALU.add, "m1")

                def s2():
                    DV_F.wait(dve, i, "masked")
                    V.memset(spare[:], 0.0)
                    for s in range(SUB):
                        step(DV_F, V.max(best[:, s], masked[:, s]))
                    DV_F.wait(dve, i, f"best{SUB - 1}")
                    step(DV_F, V.memset(best[:, :, 4:8], TAKEN))

                def s3():
                    DV_F.wait(dve, i, "spent")
                    V.memset(spare[:], 0.0)
                    for s in range(SUB):
                        step(DV_F, V.match_replace(sel[:, s], best[:, s], masked[:, s], TAKEN))

                def s4():
                    DV_F.wait(dve, i, f"taken{SUB - 1}")
                    step(DV_F, V.tensor_scalar(sel[:], sel[:], TAKEN, None, ALU.is_equal))
                    tt(i, "w", w[:], sc[:], sel[:], ALU.mult, "esel")
                    DV_F.wait(dve, i, "w")
                    step(DV_F, V.tensor_reduce(wsum[:], w[:], AX, ALU.add))
                    DV_F.wait(dve, i, "ws")
                    step(DV_F, V.tensor_scalar(wsum[:], wsum[:], 1e-20, None, ALU.add))

                def s5():
                    DV_F.wait(dve, i, "wr")
                    step(DV_F, V.reciprocal(wsum[:], wsum[:]))
                return s0, s1, s2, s3, s4, s5

            def combine(i, k):
                c1, c2, c3 = (comb[:, :, E * n:E * n + E] for n in range(3))
                tt(i, "comb", w[:], w[:], wsum[:].unsqueeze(2).to_broadcast([P, SUB, E]), ALU.mult, "rec")
                DV_F.wait(dve, i, "comb")
                step(DV_F, V.tensor_copy(c1, w[:]))
                tt(i, "r1", w[:], w[:], c1, ALU.subtract, "c1")
                DV_F.wait(dve, i, "r1")
                step(DV_F, V.tensor_copy(c2, w[:]))
                tt(i, "r2", w[:], w[:], c2, ALU.subtract, "c2")
                DV_F.wait(dve, i, "r2")
                step(DV_F, V.tensor_copy(c3, w[:]))

            def copy_comb(i, k):
                PE_F.wait(dve, i, "comb")
                step(DV_F, V.tensor_copy(cT[:, k, :], psFh[:, 0:TB]))

            def chunk(i, k, c, edge):
                dve.wait_ge(sig_done, i * CH + c + 1)
                step(DV_C, V.scalar_tensor_tensor(out=sig[:, c % 2], in0=psG[:, c % 2], scalar=unscale[:, 0:1],
                                                  in1=sig[:, c % 2], op0=ALU.mult, op1=ALU.mult))
                if c:
                    low(i, c - 1)
                elif edge != "first":
                    low(i - 1, CH - 1)
                PE_C.wait(dve, i, f"up{c}")
                if c >= 2 or edge != "first":
                    dve.wait_ge(low_done, i * CH + c - 1)
                DV_C.wait(dve, i, f"g{c}")
                step(DV_C, V.scalar_tensor_tensor(out=hid[:, c % 2], in0=psU[:, c % 2], scalar=unscale[:, 1:2],
                                                  in1=sig[:, c % 2], op0=ALU.mult, op1=ALU.mult))
                if c < CR:
                    PE_C.wait(dve, i, f"comb{c}")
                    DV_C.wait(dve, i, f"u{c}")
                    step(DV_C, V.tensor_tensor(hid[:, c % 2], hid[:, c % 2], psC[:], ALU.mult))

            def residual(i, k):
                dve.wait_ge(down_done, i * CH + CH)
                dve.wait_ge(stored, i * 16 + 16)
                step(DV_L, V.scalar_tensor_tensor(out=y[:].rearrange("p s d -> p (s d)"), in0=psD[:].rearrange("p a b -> p (a b)"),
                                                  scalar=unscale[:, 2:3], in1=xb[:, k].rearrange("p s d -> p (s d)"),
                                                  op0=ALU.mult, op1=ALU.add))

            def norm_stats(i):
                DV_L.wait(dve, i, "y")
                for s in range(SUB):
                    step(DV_L, V.bn_stats(st6[:, s, :], y[:, s, :]))
                DV_L.wait(dve, i, f"s{SUB - 1}")
                V.memset(spare[:], 0.0)
                for s in range(SUB):
                    step(DV_L, V.bn_aggr(mv[:, s, :], st6[:, s, :]))

            def norm_out(i):
                rsqrt(dve, V, DV_L, i, f"a{SUB - 1}", rstd[:], mv[:, :, 1], ru[:], 1e-5, 1.0)
                DV_L.wait(dve, i, RSQRT[-1])
                for s in range(SUB):
                    step(DV_L, V.tensor_scalar(y[:, s, :], y[:, s, :], mv[:, s, 0:1], rstd[:, s:s + 1],
                                               ALU.subtract, ALU.mult))

            def prologue():
                low_x(0, 0)
                find_maxima(0)
                for s in router_steps(0, 0):
                    s()
                combine(0, 0)
                find_maxima(2, 1)
                copy_comb(0, 0)
                scale_weights()

            def main(i, k, edge):
                steps = router_steps(i + 1, 1 - k)
                for c in range(CH):
                    chunk(i, k, c, edge)
                    if edge != "first":
                        if c == 1:
                            residual(i - 1, 1 - k)
                        if c == 2:
                            norm_stats(i - 1)
                        if c == 3:
                            norm_out(i - 1)
                    if edge != "last":
                        if c == 5:
                            low_x(i + 1, 1 - k)
                        if c == 6:
                            steps[0]()
                            steps[1]()
                        if c == 7:
                            steps[2]()
                        if c == 8:
                            steps[3]()
                        if c == 9:
                            steps[4]()
                            steps[5]()
                            combine(i + 1, 1 - k)
                if edge != "last":
                    copy_comb(i + 1, 1 - k)

            def tail():
                low(NTB - 1, CH - 1)
                residual(NTB - 1, 1)
                norm_stats(NTB - 1)
                norm_out(NTB - 1)
            tiles(dve, prologue, main, tail)

        @block.tensor
        def _(pe):
            pe.wait_ge(pool_setup, FPOOL_SETUP)
            pe.wait_ge(shared_loaded, 16 * 5)
            for a in range(2):
                mm = pe.transpose(psC[:, E * a:E * a + E], rl[0:E, P * a:P * a + P], id32[0:E, 0:E])
            mm.then_inc(pe_setup, 1)
            for src, dst in ((sgl, psG), (sul, psU)):
                for a in range(2):
                    for s in range(CS):
                        mm = pe.transpose(dst[:, a, P * s:P * s + P], src[:, s, P * a:P * a + P], id32[:])
                    mm.then_inc(pe_setup, 1)
            for r in range(2):
                for s in range(CS):
                    mm = pe.transpose(psD[:, r, P * s:P * s + P], sdl[:, r, P * s:P * s + P], id32[:])
                mm.then_inc(pe_setup, 1)

            def front_x(i, k, a, load):
                if a == 0:
                    pe.wait_ge(x_loaded[k], load * 16 + 16)
                else:
                    AC_F.wait(pe, i, "h0")
                for s in range(SUB):
                    mm = pe.transpose(psF[:, P * s:P * s + P], xb[:, k, s, P * a:P * a + P], id32[:])
                step(PE_F, mm)

            def front_logits(i, k):
                AC_F.wait(pe, i, "h1")
                for s in range(SUB):
                    for a in range(2):
                        mm = pe.matmul(psF[:, E * s:E * s + E], xT[:, k, a, P * s:P * s + P], wr[:, a, :], start=(a == 0), stop=(a == 1))
                step(PE_F, mm)

            def front_comb(i, k):
                DV_F.wait(pe, i, "c3")
                for s in range(SUB):
                    mm = pe.transpose(psFh[:, P * s:P * s + P], comb[:, s, :], idb[:])
                step(PE_F, mm)

            def gate_up(i, k, c, edge):
                for w_, ps_, name in ((wg16, psG, "gate"), (wu16, psU, "up")):
                    if name == "gate":
                        if c >= 2:
                            DV_C.wait(pe, i, f"u{c - 2}")
                        elif edge != "first":
                            DV_C.wait(pe, i - 1, f"u{CH - 2 + c}")
                    for a in range(2):
                        for wp, xp in ((0, 0), (0, 1), (1, 0)):
                            mm = pe.matmul(ps_[:, c % 2, :], w_[:, wp, a, c, :], xT16[:, k, xp, a, :],
                                           start=(a == 0 and wp == xp), stop=(a == 1 and wp == 1))
                    step(PE_C, mm)
                if c < CR:
                    if c:
                        DV_C.wait(pe, i, f"h{c - 1}")
                    elif edge != "first":
                        DV_C.wait(pe, i - 1, f"h{CR - 1}")
                    step(PE_C, pe.matmul(psC[:], pick[:, c, :], cT[:, k, :], start=True, stop=True))

            def down(i, c, first_tile):
                pe.wait_ge(low_done, i * CH + c + 1)
                if c == 0 and first_tile:
                    pe.wait_ge(dve_setup, SCALES + 3)
                elif c == 0:
                    DV_L.wait(pe, i - 1, "y")
                for s in range(SUB):
                    for hp, wp in ((0, 0), (0, 1), (1, 0)):
                        mm = pe.matmul(psD[:, s // 2, D * (s % 2):D * (s % 2) + D], hid16[:, c % 4, hp, P * s:P * s + P],
                                       wd16[:, wp, c, :], start=(c == 0 and s % 2 == 0 and hp == wp),
                                       stop=(c == CH - 1 and hp == 1), skip_group_check=True)
                mm.then_inc(down_done, 1)

            def prologue():
                pe.wait_ge(dve_setup, NS)
                front_x(0, 0, 0, 0)
                front_x(0, 0, 1, 0)
                front_logits(0, 0)
                front_comb(0, 0)
                pe.wait_ge(dve_setup, SCALES + 2)

            def main(i, k, edge, load):
                for c in range(CH):
                    if c == 0:
                        DV_X.wait(pe, i, "l1")
                        DV_F.wait(pe, i, "cT")
                    gate_up(i, k, c, edge)
                    if c >= 2:
                        down(i, c - 2, edge == "first")
                    elif edge != "first":
                        down(i - 1, CH - 2 + c, False)
                    if edge != "last":
                        if c in (2, 3):
                            front_x(i + 1, 1 - k, c - 2, load)
                        if c == 5:
                            front_logits(i + 1, 1 - k)
                        if c == 11:
                            front_comb(i + 1, 1 - k)

            prologue()
            main(0, 0, "first", 0)
            with pe.Fori(0, (NTB - 2) // 2) as h:
                for odd in range(2):
                    main(h * 2 + 1 + odd, 1 - odd, "", h + 1)
            main(NTB - 1, 1, "last", None)
            for c in (CH - 2, CH - 1):
                down(NTB - 1, c, False)


FPOOL_SETUP = 10
MAXIMA = 7 + 3
SCALES = MAXIMA + 8

_INS = ["L0_attn_x", "L0_attn_qW", "L0_attn_qb", "L0_attn_kW", "L0_attn_kb", "L0_attn_vW", "L0_attn_vb", "L0_attn_oW",
        "L0_attn_ob", "L0_attn_J", "L0_ffn_router_w", "L0_ffn_correction_bias", "L0_ffn_gate_w", "L0_ffn_up_w",
        "L0_ffn_down_w", "L0_ffn_shared_gate_w", "L0_ffn_shared_up_w", "L0_ffn_shared_down_w"]


def program(nc, ins, out):
    x, qW, qb, kW, kb, vW, vb, oW, ob, J, rw, cb, gw, uw, dw, sgw, suw, sdw = ins
    x1 = nc.dram_tensor("x1", (NTOK, D), F32, kind="Internal").ap()
    attention(nc, x, qW, qb, kW, kb, vW, vb, oW, ob, J, x1)
    feed_forward(nc, x1, rw, cb, gw, uw, dw, sgw, suw, sdw, out.rearrange("b t d -> (b t) d"))


def kernel(**inputs):
    import concourse.bacc as _bacc
    from concourse.bass_utils import run_bass_kernel_spmd as _run

    nc = _bacc.Bacc("TRN2", target_bir_lowering=False, num_devices=1)
    arrays, ins = {}, []
    for name in _INS:
        a = np.ascontiguousarray(inputs[name])
        arrays[f"in_{name}"] = a
        ins.append(nc.dram_tensor(f"in_{name}", a.shape, mybir.dt.from_np(a.dtype), kind="ExternalInput").ap())
    out = nc.dram_tensor("out", (B, T, D), F32, kind="ExternalOutput").ap()
    program(nc, ins, out)
    return _run(nc, [arrays], core_ids=[0]).results[0]["out"]
```

```python
from contextlib import ExitStack

import concourse.bass as bass
import numpy as np
from concourse import mybir

ALU = mybir.AluOpType
ACT = mybir.ActivationFunctionType
F32 = mybir.dt.float32
F16 = mybir.dt.float16
BF16 = mybir.dt.bfloat16
AX = mybir.AxisListType.X

P = 128
B, T, D = 16, 1024, 256
HEADS, DH, COMP = 16, 16, 64
NHG = 4
ST = T // P
QS = 256.0
SIGN = {(1, 0): -1.0, (2, 0): -1.0, (3, 0): -1.0, (2, 1): -1.0, (3, 2): -1.0, (1, 3): -1.0}
NTOK = B * T
TB = 512
NTB = NTOK // TB
SUB = TB // P
E, EH, HS = 16, 64, 512
CR, CS = E * EH // P, HS // P
CH = CR + CS
TAKEN = -3e38
XS = 256.0


RSQRT = ("x", "half", "y0", "u1", "v1", "y1", "u2", "v2", "y2", "u3", "v3", "y3")


def rsqrt(dve, V, S, rnd, last, y, x, u, eps, scale):
    def step(ins):
        ins.then_inc(S.sem, 1)
    I32 = mybir.dt.int32
    S.wait(dve, rnd, last)
    step(V.tensor_scalar(u, x, eps, scale, ALU.add, ALU.mult))
    S.wait(dve, rnd, "x")
    step(V.tensor_scalar(y.bitcast(I32), u.bitcast(I32), 1, None, ALU.logical_shift_right))
    S.wait(dve, rnd, "half")
    step(V.tensor_scalar(y.bitcast(I32), y.bitcast(I32), -1.0, float(0x5f3759df), ALU.mult, ALU.add))
    for n in (1, 2, 3):
        S.wait(dve, rnd, f"y{n - 1}")
        step(V.tensor_tensor(x, y, y, ALU.mult))
        S.wait(dve, rnd, f"u{n}")
        step(V.scalar_tensor_tensor(out=x, in0=x, scalar=-0.5, in1=u, op0=ALU.mult, op1=ALU.mult))
        S.wait(dve, rnd, f"v{n}")
        step(V.scalar_tensor_tensor(out=y, in0=x, scalar=1.5, in1=y, op0=ALU.add, op1=ALU.mult))


class Steps:

    def __init__(self, sem, names):
        self.sem, self.at, self.n = sem, {s: i + 1 for i, s in enumerate(names)}, len(names)

    def wait(self, eng, rnd, step):
        eng.wait_ge(self.sem, rnd * self.n + self.at[step])


def small_math(eng, nc, sem):
    count = [0]

    def link(ins):
        ins.then_inc(sem, 1)
        count[0] += 1
        eng.wait_ge(sem, count[0])
    return link, count


def attention(nc, x, qW, qb, kW, kb, vW, vb, oW, ob, J, x1):
    xrows = x.rearrange("b t d -> (b t) d")
    with ExitStack() as ctx:
        def sb(name, shape, dt=F32):
            return ctx.enter_context(nc.sbuf_tensor(name, shape, dt))

        def sem(name):
            return ctx.enter_context(nc.semaphore(name))

        kst = sb("k_stat", [P, 2, HEADS // 2, 2, T], F16)
        qmv = sb("q_mov", [P, 2, HEADS // 2, T], F16)
        vall = sb("v_all", [P, 2, ST, D])
        vstat = sb("v_stat", [P, ST, 4, 2, DH])
        prob = sb("prob", [P, 8, T])
        osb = sb("osb", [P, T])
        onorm = sb("o_norm", [P, T])
        rden = sb("rden", [P, 2, 16])
        ot = sb("ot", [P, T])
        ysb = sb("y", [P, 2, ST, D])
        xt = sb("x_tile", [P, 2, D])
        xT = sb("xT", [P, 2, P])
        qkb = sb("qkb", [P, 2, 4, COMP])
        qkn = sb("qkn", [P, 2, 4, COMP])
        n2 = sb("n2", [P, 2, COMP])
        rn = sb("rn", [P, 2, COMP])
        nu = sb("nu", [P, 2, COMP])
        parts = sb("parts", [P, 2, HEADS, 4, DH], F16)
        wqkv = sb("wqkv", [P, 2, 3, D])
        wo = sb("wo", [P, 2, D])
        half = sb("half", [P, 2, 2])
        rows4 = sb("rows4", [P, 4])
        bqkv = sb("bqkv", [P, 3, D])
        bo = sb("bo", [P, D])
        id32 = sb("id32", [P, P])
        id16 = sb("id16", [P, P], F16)
        jt = sb("jt", [P, 4])
        st6 = sb("st6", [P, ST, 6])
        mv = sb("mv", [P, ST, 2])
        rstd = sb("rstd", [P, ST])
        ru = sb("ru", [P, ST])
        spare = sb("spare", [P, 1])
        pspare = sb("pspare", [P, ST])
        base = prob[:, 0:3, :].rearrange("p a b -> p (a b)")
        wbase = base[:, 0:768].rearrange("p (m w o) -> p m w o", m=3, w=4)
        wobase = base[:, 768:1024].rearrange("p (w o) -> p w o", w=4)
        bbase = base[:, 1024:2048].rearrange("p (m w o) -> p m w o", m=4, w=4)
        jrow = base[:, 2048:2304]
        jk = base[:, 2304:2560]
        wtmp = base[:, 2560:3072].rearrange("p (m o) -> p m o", m=2)

        psS = ctx.enter_context(nc.psum_tensor("psS", [P, 2, T], F32))
        psO = ctx.enter_context(nc.psum_tensor("psO", [P, 2, 512], F32))
        pr0 = ctx.enter_context(nc.psum_tensor("pr0", [P, 512], F32))
        pr1 = ctx.enter_context(nc.psum_tensor("pr1", [P, 512], F32))
        pr0h = pr0[:].bitcast(F16)
        pr1h = pr1[:].bitcast(F16)

        j_loaded = sem("j_loaded")
        w_loaded = sem("w_loaded")
        wo_loaded = sem("wo_loaded")
        pool_setup = sem("pool_setup")
        dve_setup = sem("dve_setup")
        act_setup = sem("act_setup")
        x_loaded = [sem(f"x_loaded{k}") for k in range(2)]
        y_loaded = sem("y_loaded")
        y_biased = sem("y_biased")
        x1_stored = sem("x1_stored")
        scores_done = sem("scores_done")
        exp_done = sem("exp_done")
        pv_done = sem("pv_done")
        v_staged = sem("v_staged")
        proj_done = sem("proj_done")
        proj_added = sem("proj_added")
        PE_X = Steps(sem("pe_x"), ["xT"])
        PE_QKV = Steps(sem("pe_qkv"), ["q", "k", "v"])
        PE_T = Steps(sem("pe_t"), ["qT", "kT"])
        DV_X = Steps(sem("x_copied"), ["xT"])
        DV_QKV = Steps(sem("dve_qkv"), ["qk", "sq", "n2", "v", *RSQRT, "norm", "qhi", "khi0", "khi1", "qlo", "klo0", "klo1"])
        DV_T = Steps(sem("t_copied"), ["qT", "kT0", "kT1"])
        DV_LN = Steps(sem("dve_ln"), [f"stats{s}" for s in range(ST)] + [f"mean{s}" for s in range(ST)] + [*RSQRT]
                      + [f"out{s}" for s in range(ST)])
        DV_NORM = Steps(sem("dve_norm"), ["o0", "o1", "r0", "m0", "r1", "m1"])
        DV_OT = Steps(sem("dve_ot"), ["n0", "n1"])

        NW = 6 + 4
        block = ctx.enter_context(nc.Block())

        def each_iteration(eng, prologue, body, tail, batch_end=lambda b, par: None):
            def batch(b, par, edge):
                for hg in range(NHG):
                    body(b * 4 + hg, hg, b, par, edge)
                batch_end(b, par)
            prologue()
            batch(0, 0, "first")
            with eng.Fori(0, (B - 2) // 2) as b2:
                for odd in range(2):
                    batch(b2 * 2 + 1 + odd, 1 - odd, "")
            batch(B - 1, 1, "last")
            tail()

        def products(hg, b, edge):
            if edge == "first" and hg < 2:
                return None, None
            return b * 2 + hg // 2 - 1, (0, 1) if hg % 2 == 0 else (2, 3)

        OGROUPS = [(1, 0), (0, 2), (1, 4), (0, 6)]
        NOG = len(OGROUPS)

        @block.sync
        def _(sp):
            sp.dma_start(jrow, J.partition_broadcast(P)).then_inc(j_loaded, 16)

            def load_x(r, k, u, wait):
                if wait:
                    PE_X.wait(sp, u - 2, "xT")
                sp.dma_start(xt[:, k, :], xrows[bass.ds(u * P, P), :]).then_inc(x_loaded[k], 16)

            def prologue():
                for k in range(2):
                    load_x(0, k, k, False)
                for m, v in enumerate((qb, kb, vb, ob)):
                    sp.dma_start(bbase[:, m], v.partition_broadcast(P)).then_inc(w_loaded, 16)
                for j in range(4):
                    for second in range(2):
                        r = 32 * j + DH * second
                        sp.dma_start(wobase[r:r + DH], oW[:, DH * j:DH * j + DH].rearrange("w d o -> d w o")).then_inc(wo_loaded, 16)
                with sp.Fori(1, 4) as r:
                    for k in range(2):
                        load_x(r, k, r * 2 + k, True)

            def body(g, hg, b, par, edge):
                if edge != "last":
                    for k in range(2):
                        load_x(g + 4, k, (g + 4) * 2 + k, True)
                if hg == 0:
                    if edge != "first":
                        sp.wait_ge(x1_stored, b * 16)
                    sp.dma_start(ysb[:, par], token_tiles(xrows, b)).then_inc(y_loaded, 16)

            def token_tiles(rows, b):
                return rows[bass.ds(b * T, T), :].rearrange("(s p) d -> p s d", p=P)

            def store(b, par):
                DV_LN.wait(sp, b, f"out{ST - 1}")
                sp.dma_start(token_tiles(x1, b), ysb[:, par]).then_inc(x1_stored, 16)

            def batch_end(b, par):
                if isinstance(b, int) and b == 0:
                    sp.sem_inc(x1_stored, 16)
                else:
                    store(b - 1, 1 - par)

            def tail():
                store(B - 1, 1)
                sp.wait_ge(x1_stored, 16 * (B + 1))
            each_iteration(sp, prologue, body, tail, batch_end)

        @block.gpsimd
        def _(pool):
            link, _c = small_math(pool, nc, pool_setup)
            link(nc.gpsimd.memset(id32[:], 0.0))
            link(nc.gpsimd.affine_select(out=id32[:], in_=id32[:], compare_op=ALU.not_equal, fill=1.0, base=0,
                                         pattern=[[-1, P]], channel_multiplier=1))
            link(nc.gpsimd.tensor_copy(id16[:], id32[:]))
            assert _c[0] == POOL_IDS
            link(nc.gpsimd.memset(rows4[:], 1.0))
            link(nc.gpsimd.affine_select(out=rows4[:], in_=rows4[:], compare_op=ALU.is_ge, fill=0.0, base=0,
                                         pattern=[[-32, 4]], channel_multiplier=1))
            link(nc.gpsimd.affine_select(out=rows4[:], in_=rows4[:], compare_op=ALU.is_ge, fill=0.0, base=DH - 1,
                                         pattern=[[32, 4]], channel_multiplier=-1))
            link(nc.gpsimd.tensor_tensor(rows4[:, 0:2], rows4[:, 0:2], rows4[:, 2:4], ALU.add))
            link(nc.gpsimd.tensor_tensor(half[:, 0, 0:1], rows4[:, 0:1], rows4[:, 1:2], ALU.add))
            link(nc.gpsimd.tensor_scalar(half[:, 0, 1:2], half[:, 0, 0:1], -1.0, None, ALU.mult))
            link(nc.gpsimd.tensor_scalar(half[:, 1, 0:1], half[:, 0, 1:2], 1.0, None, ALU.add))
            link(nc.gpsimd.tensor_scalar(half[:, 1, 1:2], half[:, 1, 0:1], -1.0, None, ALU.mult))
            pool.wait_ge(w_loaded, 16 * NW)
            pool.wait_ge(wo_loaded, 16 * 8)
            for i in range(4):
                for o in range(4):
                    minus = (i, o) in SIGN
                    cols = slice(o * COMP, o * COMP + COMP)
                    sign_of_row = half[:, i % 2, minus:minus + 1].to_broadcast([P, COMP])
                    nc.gpsimd.tensor_tensor((wtmp if i % 2 else wo)[:, i // 2, cols], wobase[:, o ^ i, :], sign_of_row,
                                            ALU.mult).then_inc(pool_setup, 1)
                    src = bbase[:, 3, o ^ i, :]
                    if i == 0:
                        nc.gpsimd.tensor_copy(bo[:, cols], src).then_inc(pool_setup, 1)
                    else:
                        nc.gpsimd.tensor_tensor(bo[:, cols], bo[:, cols], src, ALU.subtract if minus else ALU.add).then_inc(pool_setup, 1)
                _c[0] += 8
                pool.wait_ge(pool_setup, _c[0])
            link(nc.gpsimd.tensor_tensor(wo[:], wo[:], wtmp, ALU.add))
            for par in range(2):
                link(nc.gpsimd.memset(kst[64:128, par, :, 0, :].bitcast(F32), 0.0))
                link(nc.gpsimd.memset(kst[0:64, par, :, 1, :].bitcast(F32), 0.0))
            assert _c[0] == POOL_SETUP
            pool.wait_ge(dve_setup, DVE_SETUP)

            def stage_v(g, hg, par, s, first):
                if not first:
                    pool.wait_ge(pv_done, (g - 1) * 2 * ST + 2 * s + 2)
                    nc.gpsimd.tensor_tensor(pspare[:, s:s + 1], id32[:, 0:1], id32[:, 0:1], ALU.mult)
                src = vall[:, par, s, bass.ds(hg * COMP, COMP)].rearrange("p (j d) -> p j d", j=4)
                nc.gpsimd.tensor_copy(vstat[:, s, :, 0, :], src).then_inc(v_staged, 1)

            def body(g, hg, b, par, edge):
                if hg == 0:
                    DV_QKV.wait(pool, b * ST + ST - 1, "v")
                for s in range(ST):
                    stage_v(g, hg, par, s, hg == 0 and edge == "first")
                if hg == 0:
                    pool.wait_ge(y_loaded, b * 16 + 16)
                    for s in range(ST):
                        nc.gpsimd.tensor_tensor(ysb[:, par, s], ysb[:, par, s], bo[:], ALU.add).then_inc(y_biased, 1)

            each_iteration(pool, lambda: None, body, lambda: None)

        @block.scalar
        def _(act):
            for m, w in enumerate((qW, kW, vW)):
                for half in range(2):
                    act.dma_start(wbase[64 * half:64 * half + 64, m], w.rearrange("w d o -> d w o")).then_inc(w_loaded, 16)
            act.wait_ge(dve_setup, J_REDUCED)
            nc.scalar.activation(jk, jrow, ACT.Sin).then_inc(act_setup, 1)
            act.wait_ge(dve_setup, J_SUMMED)
            nc.scalar.activation(jt[:, 1:2], jt[:, 0:1], ACT.Exp, scale=0.1 / D).then_inc(act_setup, 1)

            def body(g, hg, b, par, edge):
                for n in range(4 * ST):
                    act.wait_ge(scores_done, g * 32 + n + 1)
                    if n % 4 == 0 and not (hg == 0 and edge == "first" and n < 8):
                        act.wait_ge(pv_done, g * 2 * ST + (n // 4) * 2 - 2)
                    if hg == 0 and edge == "first" and n == 0:
                        act.wait_ge(pool_setup, POOL_SETUP)
                    nc.scalar.activation(prob[:, n % 8, :], psS[:, n % 2, :], ACT.Exp,
                                         scale=DH ** -0.5 / (QS * QS)).then_inc(exp_done, 1)
            def copy_x(u, k):
                PE_X.wait(act, u, "xT")
                nc.scalar.copy(xT[:], psO[:, k, 0:256].rearrange("p (a b) -> p a b", a=2)).then_inc(DV_X.sem, 1)

            def copy_transposes(u):
                tok = bass.ds(u * P, P)
                PE_T.wait(act, u, "qT")
                nc.scalar.copy(qmv[:, 0, :, tok], pr1h.rearrange("p (a t) -> p a t", t=P)).then_inc(DV_T.sem, 1)
                PE_T.wait(act, u, "kT")
                for e in range(2):
                    r = slice(64 * e, 64 * e + 64)
                    nc.scalar.copy(kst[r, 0, :, e, tok], pr0h[r].rearrange("p (a t) -> p a t", t=P)).then_inc(DV_T.sem, 1)

            def prologue():
                def pair(a, more):
                    PE_QKV.wait(act, a, "v")
                    copy_x(a + 1, 1)
                    copy_transposes(a)
                    PE_QKV.wait(act, a + 1, "v")
                    if more:
                        copy_x(a + 2, 0)
                    copy_transposes(a + 1)
                copy_x(0, 0)
                with act.Fori(0, 3) as r:
                    pair(r * 2, True)
                pair(6, False)
            each_iteration(act, prologue, body, lambda: None)

        @block.vector
        def _(dve):
            V = nc.vector
            link, c = small_math(dve, nc, dve_setup)
            dve.wait_ge(j_loaded, 16)
            TWO_PI, MAGIC = float(2 * np.pi), 12582912.0
            link(V.tensor_scalar(jk, jrow, 1.0 / TWO_PI, MAGIC, ALU.mult, ALU.add))
            link(V.tensor_scalar(jk, jk, MAGIC, None, ALU.subtract))
            link(V.scalar_tensor_tensor(out=jrow, in0=jk, scalar=-6.28125, in1=jrow, op0=ALU.mult, op1=ALU.add))
            link(V.scalar_tensor_tensor(out=jrow, in0=jk, scalar=-(TWO_PI - 6.28125), in1=jrow, op0=ALU.mult, op1=ALU.add))
            link(V.tensor_scalar(jrow, jrow, 3.1415925, -3.1415925, ALU.min, ALU.max))
            assert c[0] == J_REDUCED
            dve.wait_ge(act_setup, 1)
            link(V.tensor_reduce(jt[:, 0:1], jk, AX, ALU.add))
            assert c[0] == J_SUMMED
            dve.wait_ge(w_loaded, 16 * NW)
            V.memset(vstat[:], 1.0).then_inc(dve_setup, 1)
            c[0] += 1
            for i in range(4):
                rows = slice(64 * (i % 2), 64 * (i % 2) + 64)
                for o in range(4):
                    sgn = SIGN.get((i, o), 1.0)
                    cols = slice(o * COMP, o * COMP + COMP)
                    V.tensor_scalar(wqkv[rows, i // 2, :, cols], wbase[rows, :, o ^ i, :], sgn, None, ALU.mult).then_inc(dve_setup, 1)
                    src = bbase[:, 0:3, o ^ i, :]
                    if i == 0:
                        V.tensor_copy(bqkv[:, :, cols], src).then_inc(dve_setup, 1)
                    else:
                        V.tensor_tensor(bqkv[:, :, cols], bqkv[:, :, cols], src, ALU.add if sgn > 0 else ALU.subtract).then_inc(dve_setup, 1)
                c[0] += 8
                dve.wait_ge(dve_setup, c[0])
            assert c[0] == WEIGHTS
            dve.wait_ge(act_setup, 2)
            ec = jt[:, 1:2]
            link(V.tensor_scalar(bqkv[:, 2], bqkv[:, 2], ec, None, ALU.mult))
            ones = vstat[:, :, :, 1, :].rearrange("p s j d -> p (s j) d")
            link(V.tensor_scalar(ones, ones, ec, None, ALU.mult))
            assert c[0] == DVE_SETUP, c[0]
            dve.sem_inc(proj_added, 1)

            def step(S, ins):
                ins.then_inc(S.sem, 1)

            S = DV_QKV
            hi_q = parts[:, 0, :, 0:2, :]
            lo_q = parts[:, 0, :, 2:4, :]

            def by_head(a, m):
                return a[:, m].rearrange("p c (j d) -> p (c j) d", j=4)

            def take_x(u):
                PE_X.wait(dve, u, "xT")
                step(DV_X, V.tensor_copy(xT[:], pr0[:, 0:256].rearrange("p (a b) -> p a b", a=2)))

            def take_qk(u, qk=pr1):
                PE_QKV.wait(dve, u, "k")
                step(S, V.tensor_tensor(qkb[:].rearrange("p m c o -> p (m c o)"), qk[:, 0:512], bqkv[:, 0:2].rearrange("p m o -> p (m o)"), ALU.add))

            def take_v(u, par, s, staged, v=pr0):
                PE_QKV.wait(dve, u, "v")
                if staged is not None:
                    dve.wait_ge(v_staged, staged)
                step(S, V.scalar_tensor_tensor(out=vall[:, par, s, :], in0=v[:, 0:256], scalar=ec, in1=bqkv[:, 2],
                                               op0=ALU.mult, op1=ALU.add))

            def squares(u):
                S.wait(dve, u, "qk")
                step(S, V.tensor_tensor(qkn[:], qkb[:], qkb[:], ALU.mult))
                S.wait(dve, u, "sq")
                step(S, V.tensor_reduce(n2[:], qkn[:].rearrange("p m c o -> p m o c"), AX, ALU.add))

            def inverse_norms(u):
                rsqrt(dve, V, S, u, "n2", rn[:], n2[:], nu[:], 1e-6, 1.0 / (QS * QS))

            def normalise_and_split(u):
                S.wait(dve, u, RSQRT[-1])
                for_m = rn[:].unsqueeze(2).to_broadcast([P, 2, 4, COMP])
                step(S, V.tensor_tensor(qkn[:], qkb[:], for_m, ALU.mult))
                S.wait(dve, u, "norm")
                q, k = by_head(qkn, 0), by_head(qkn, 1)
                step(S, V.tensor_copy(hi_q, q.unsqueeze(2).to_broadcast([P, HEADS, 2, DH])))
                for t in (0, 2):
                    step(S, V.tensor_copy(parts[:, 1, :, t, :], k))
                S.wait(dve, u, "khi1")
                step(S, V.tensor_tensor(lo_q, q.unsqueeze(2).to_broadcast([P, HEADS, 2, DH]), hi_q, ALU.subtract))
                for t in (1, 3):
                    step(S, V.tensor_tensor(parts[:, 1, :, t, :], k, parts[:, 1, :, 0, :], ALU.subtract))

            def take_transposes(u, par, s):
                tok = bass.ds(s * P, P)
                PE_T.wait(dve, u, "qT")
                step(DV_T, V.tensor_copy(qmv[:, par, :, tok], pr1h.rearrange("p (a t) -> p a t", t=P)))
                PE_T.wait(dve, u, "kT")
                for e in range(2):
                    r = slice(64 * e, 64 * e + 64)
                    step(DV_T, V.tensor_copy(kst[r, par, :, e, tok], pr0h[r].rearrange("p (a t) -> p a t", t=P)))

            def norm(g, second):
                N = DV_NORM
                def turn(h):
                    dve.wait_ge(pv_done, g * 2 * ST + 2 * ST - 1 + h)
                    if not (isinstance(g, int) and g == 0):
                        N.wait(dve, g - 1, f"m{h}")
                    step(N, V.transpose(osb[:, 512 * h:512 * h + 512], psO[:, h, :]))

                def divide(h):
                    cols = slice(512 * h, 512 * h + 512)
                    turned = osb[:, cols].rearrange("p (b r) -> p b r", r=32)
                    mine = onorm[:, cols].rearrange("p (b r) -> p b r", r=32)[:, :, DH * second:DH * second + DH]
                    N.wait(dve, g, f"o{h}")
                    step(N, V.reciprocal(rden[:, h], turned[:, :, DH]))
                    N.wait(dve, g, f"r{h}")
                    step(N, V.tensor_tensor(mine, turned[:, :, 0:DH], rden[:, h].unsqueeze(2).to_broadcast([P, 16, DH]), ALU.mult))
                    if second:
                        N.wait(dve, g, f"m{h}")
                        step(DV_OT, V.transpose(ot[:, cols], onorm[:, cols]))
                return turn, divide

            def add_proj(pr, par, i):
                bank, t = OGROUPS[i]
                dve.wait_ge(proj_done, pr * NOG + i + 1)
                dst = ysb[:, par, t:t + 2].rearrange("p s d -> p (s d)")
                V.tensor_tensor(dst, dst, (pr1 if bank else pr0)[:], ALU.add).then_inc(proj_added, 1)

            def ln_stats(n, par):
                dve.wait_ge(proj_added, (n + 1) * 2 * NOG + 1)
                for s in range(ST):
                    step(DV_LN, V.bn_stats(st6[:, s, :], ysb[:, par, s, :]))

            def ln_rstd(n):
                DV_LN.wait(dve, n, f"stats{ST - 1}")
                V.memset(spare[:], 0.0)
                for s in range(ST):
                    step(DV_LN, V.bn_aggr(mv[:, s, :], st6[:, s, :]))
                rsqrt(dve, V, DV_LN, n, f"mean{ST - 1}", rstd[:], mv[:, :, 1], ru[:], 1e-5, 1.0)

            def ln_out(n, par):
                DV_LN.wait(dve, n, RSQRT[-1])
                for s in range(ST):
                    step(DV_LN, V.tensor_scalar(ysb[:, par, s, :], ysb[:, par, s, :], mv[:, s, 0:1], rstd[:, s:s + 1],
                                                ALU.subtract, ALU.mult))

            def prologue():
                def tile(u, k, parts_in_use):
                    take_qk(u, psS[:, 0, 512 * k:])
                    squares(u)
                    take_v(u, 0, u, None, psS[:, 1, 512 * k:])
                    inverse_norms(u)
                    if parts_in_use:
                        PE_T.wait(dve, u - 1, "kT")
                    normalise_and_split(u)
                tile(0, 0, False)
                with dve.Fori(0, 3) as r:
                    tile(r * 2 + 1, 1, True)
                    tile(r * 2 + 2, 0, True)
                tile(7, 1, True)

            def body(g, hg, b, par, edge):
                nxt, prep = 1 - par, edge != "last"
                ua, ub = (g + 4) * 2, (g + 4) * 2 + 1
                norm_group = not (edge == "first" and hg == 0)
                pr, two = products(hg, b, edge)
                po = 1 - par if hg < 2 else par
                norm_before = edge != "first" and hg == 2
                staged = None if edge == "first" else b * NHG * ST
                if norm_group:
                    turn, divide = norm(g - 1, hg % 2 == 0)
                    turn(0)
                if prep:
                    take_x(ua)
                if norm_group:
                    turn(1)
                    divide(0)
                if norm_before:
                    ln_stats(b - 1, 1 - par)
                if prep:
                    take_qk(ua)
                    squares(ua)
                    take_v(ua, nxt, hg * 2, staged)
                    inverse_norms(ua)
                    take_x(ub)
                if two:
                    if hg == 2:
                        dve.wait_ge(y_biased, b * ST + ST)
                    add_proj(pr, po, two[0])
                if prep:
                    normalise_and_split(ua)
                if norm_group:
                    divide(1)
                if prep:
                    take_transposes(ua, nxt, hg * 2)
                if norm_before:
                    ln_rstd(b - 1)
                if prep:
                    take_qk(ub)
                    squares(ub)
                    take_v(ub, nxt, hg * 2 + 1, staged)
                    inverse_norms(ub)
                    normalise_and_split(ub)
                if two:
                    add_proj(pr, po, two[1])
                if norm_before:
                    ln_out(b - 1, 1 - par)
                if prep:
                    take_transposes(ub, nxt, hg * 2 + 1)

            def tail():
                turn, divide = norm(4 * B - 1, True)
                for h in range(2):
                    turn(h)
                for h in range(2):
                    divide(h)
                for i in range(NOG):
                    add_proj(2 * B - 1, 1, i)
                ln_stats(B - 1, 1)
                ln_rstd(B - 1)
                ln_out(B - 1, 1)
            each_iteration(dve, prologue, body, tail)

        @block.tensor
        def _(pe):
            pe.wait_ge(pool_setup, POOL_IDS)

            def transposes_x(u, k, r, xt_bank=pr0):
                pe.wait_ge(x_loaded[k], r * 16 + 16)
                for a in range(2):
                    mm = pe.transpose(xt_bank[:, P * a:P * a + P], xt[:, k, P * a:P * a + P], id32[:])
                mm.then_inc(PE_X.sem, 1)

            def project_qk(u, m, qk=pr1):
                if m == 0:
                    DV_X.wait(pe, u, "xT")
                for a in range(2):
                    mm = pe.matmul(qk[:, D * m:D * m + D], xT[:, a, :], wqkv[:, a, m, :], start=(a == 0), stop=(a == 1),
                                   skip_group_check=True)
                mm.then_inc(PE_QKV.sem, 1)

            def project_v(u, v=pr0):
                for a in range(2):
                    mm = pe.matmul(v[:, 0:256], xT[:, a, :], wqkv[:, a, 2, :], start=(a == 0), stop=(a == 1))
                mm.then_inc(PE_QKV.sem, 1)

            def transposes_qk(u, m):
                DV_QKV.wait(pe, u, "klo1" if m else "qlo")
                for a in range(HEADS // 2):
                    blk = parts[:, m, 2 * a:2 * a + 2].rearrange("p h s d -> p (h s d)")
                    mm = pe.transpose((pr0h if m else pr1h)[:, P * a:P * a + P], blk, id16[:])
                mm.then_inc(PE_T.sem, 1)

            def out_proj(pr, hp, i, tiles=(0, 1)):
                bank, t0 = OGROUPS[i]
                if 0 in tiles:
                    DV_OT.wait(pe, pr, "n0" if t0 < 4 else "n1")
                for t in tiles:
                    mm = pe.matmul((pr1 if bank else pr0)[:, D * t:D * t + D], ot[:, P * (t0 + t):P * (t0 + t) + P],
                                   wo[:, hp, :], start=True, stop=True, skip_group_check=True)
                if 1 in tiles:
                    mm.then_inc(proj_done, 1)

            def added(pr, i):
                pe.wait_ge(proj_added, pr * NOG + i + 2)

            def scores(g, hg, par, s, j, first):
                n = 4 * s + j
                if not (first and n < 2):
                    pe.wait_ge(exp_done, g * 32 + n - 1)
                pair = hg * 2 + j // 2
                for h in range(2):
                    lhsT = kst[:, par, bass.ds(pair, 1), j % 2, P * s:P * s + P].rearrange("p a t -> p (a t)")
                    rhs = qmv[:, par, bass.ds(pair, 1), 512 * h:512 * h + 512].rearrange("p a t -> p (a t)")
                    mm = pe.matmul(psS[:, n % 2, 512 * h:512 * h + 512], lhsT, rhs, start=True, stop=True)
                mm.then_inc(scores_done, 1)

            def pv(g, s, h):
                if h == 0:
                    pe.wait_ge(exp_done, g * 32 + 4 * s + 4)
                    pe.wait_ge(v_staged, g * 8 + s + 1)
                if s == 0 and not (isinstance(g, int) and g == 0):
                    DV_NORM.wait(pe, g - 1, f"o{h}")
                for j in range(4):
                    mm = pe.matmul(psO[32 * j:32 * j + 32, h, :], vstat[:, s, j].rearrange("p a d -> p (a d)"),
                                   prob[:, (4 * s + j) % 8, 512 * h:512 * h + 512], start=(s == 0), stop=(s == ST - 1),
                                   tile_position=(0, 32 * j))
                mm.then_inc(pv_done, 1)

            def prologue():
                def project(u, k):
                    project_qk(u, 0, psS[:, 0, 512 * k:])
                    project_qk(u, 1, psS[:, 0, 512 * k:])
                    project_v(u, psS[:, 1, 512 * k:])

                def pair(a, r, more):
                    transposes_x(a + 1, 1, r, psO[:, 1])
                    project(a + 1, 1)
                    transposes_qk(a, 0)
                    transposes_qk(a, 1)
                    if more:
                        transposes_x(a + 2, 0, r + 1, psO[:, 0])
                        project(a + 2, 0)
                    DV_T.wait(pe, a, "kT1")
                    transposes_qk(a + 1, 0)
                    transposes_qk(a + 1, 1)
                    DV_T.wait(pe, a + 1, "kT1")
                transposes_x(0, 0, 0, psO[:, 0])
                pe.wait_ge(dve_setup, WEIGHTS)
                project(0, 0)
                with pe.Fori(0, 3) as r:
                    pair(r * 2, r, True)
                pair(6, 3, False)
                pe.wait_ge(pool_setup, POOL_SETUP)

            def filler(g, hg, b, edge, slot):
                prep = edge != "last"
                pr, two = products(hg, b, edge)
                hp = (hg // 2 - 1) % 2
                ua, ub = (g + 4) * 2, (g + 4) * 2 + 1
                if prep and slot == 0:
                    DV_T.wait(pe, ua - 1, "kT1")
                    transposes_x(ua, 0, g + 4)
                if prep and slot in (1, 2):
                    project_qk(ua, slot - 1)
                if prep and slot == 3:
                    project_v(ua)
                if two and slot == 4:
                    if prep:
                        DV_QKV.wait(pe, ua, "qk")
                    else:
                        added(pr, two[0] - 2)
                    out_proj(pr, hp, two[0], (0,))
                if slot == 5:
                    if prep:
                        DV_QKV.wait(pe, ua, "v")
                        transposes_x(ub, 1, g + 4)
                    if two:
                        out_proj(pr, hp, two[0], (1,))
                if prep and slot == 7:
                    if two:
                        added(pr, two[0])
                    transposes_qk(ua, 0)
                if prep and slot == 8:
                    DV_X.wait(pe, ub, "xT")
                    transposes_qk(ua, 1)
                if prep and slot in (9, 10):
                    if slot == 9:
                        DV_T.wait(pe, ua, "qT")
                    project_qk(ub, slot - 9)
                if prep and slot == 11:
                    DV_T.wait(pe, ua, "kT1")
                    project_v(ub)
                if two and slot == 13:
                    if prep:
                        DV_QKV.wait(pe, ub, "v")
                    else:
                        added(pr, two[1] - 2)
                    out_proj(pr, hp, two[1])
                if prep and slot == 14:
                    transposes_qk(ub, 0)
                if prep and slot == 15:
                    if two:
                        added(pr, two[1])
                    else:
                        DV_QKV.wait(pe, ub, "v")
                    transposes_qk(ub, 1)

            def body(g, hg, b, par, edge):
                first = hg == 0 and edge == "first"
                if hg == 0:
                    DV_T.wait(pe, b * ST + ST - 1, "qT")
                for s in range(ST):
                    if hg == 0 and s == ST - 1:
                        DV_T.wait(pe, b * ST + ST - 1, "kT1")
                    for j in range(4):
                        scores(g, hg, par, s, j, first)
                        if j in (1, 2) and not (first and s == 0):
                            if s == 0:
                                pv(g - 1, ST - 1, j - 1)
                            else:
                                pv(g, s - 1, j - 1)
                        if j in (1, 3):
                            filler(g, hg, b, edge, 2 * s + j // 2)

            def tail():
                g = 4 * B - 1
                for h in range(2):
                    pv(g, ST - 1, h)
                for i in range(NOG):
                    added(2 * B - 1, i - 2)
                    out_proj(2 * B - 1, 1, i)
            each_iteration(pe, prologue, body, tail)


J_REDUCED, J_SUMMED = 5, 6
WEIGHTS = J_SUMMED + 1 + 4 * 8
DVE_SETUP = WEIGHTS + 2
POOL_IDS = 3
POOL_SETUP = POOL_IDS + 8 + 4 * 8 + 1 + 4




def feed_forward(nc, x1, rw, cb, gw, uw, dw, sgw, suw, sdw, out):
    with ExitStack() as ctx:
        def sb(name, shape, dt=F32):
            return ctx.enter_context(nc.sbuf_tensor(name, shape, dt))

        def ps(name, shape):
            return ctx.enter_context(nc.psum_tensor(name, shape, F32))

        def sem(name):
            return ctx.enter_context(nc.semaphore(name))

        wf = sb("w_f32", [P, 3, CH * D])
        wg, wu = (wf[:, m].rearrange("p (a c h) -> p a c h", a=2, c=CH) for m in (0, 1))
        wd = wf[:, 2].rearrange("p (c o) -> p c o", c=CH)
        wh = sb("w_f16", [P, 3, 2, CH * D], F16)
        wg16, wu16 = (wh[:, m].rearrange("p t (a c h) -> p t a c h", a=2, c=CH) for m in (0, 1))
        wd16 = wh[:, 2].rearrange("p t (c o) -> p t c o", c=CH)
        wmax = sb("w_max", [P, 3])
        wall = sb("w_all", [P, 3])
        wscale = sb("w_scale", [P, 3])
        unscale = sb("unscale", [P, 3])
        wr = sb("w_router", [P, 2, E])
        sgl = sb("sg_load", [P, CS, D])
        sul = sb("su_load", [P, CS, D])
        sdl = sb("sd_load", [P, 2, HS])
        rl = sb("r_load", [P, D])
        cbias = sb("c_bias", [P, E])
        id32 = sb("id32b", [P, P])
        idb = sb("idb", [P, P], BF16)
        lower = sb("lower", [P, 4, 4])
        pick = sb("pick", [P, CR, P], BF16)
        xb = sb("xb", [P, 2, SUB, D])
        xT = sb("xTb", [P, 2, 2, TB])
        cT = sb("cT", [P, 2, TB], BF16)
        sig = sb("sig", [P, 2, TB])
        hid = sb("hid", [P, 2, TB])
        hid16 = sb("hid16", [P, 4, 2, TB], F16)
        xT16 = sb("xT16", [P, 2, 2, 2, TB], F16)
        sc = sb("sc", [P, SUB, E])
        sbias = sb("sbias", [P, SUB, E])
        masked = sb("masked", [P, SUB, E])
        w = sb("w", [P, SUB, E])
        mx = sb("mx", [P, SUB * 4, 2])
        mn = sb("mn", [P, SUB * 4, 2])
        tp = sb("tp", [P, 4, SUB * 4])
        gsum = sb("gsum", [P, SUB, 4])
        gmask = sb("gmask", [P, SUB, 4])
        gpen = sb("gpen", [P, SUB, 4])
        cg = sb("cg", [P, 2, SUB, 4, 4])
        best = sb("best", [P, SUB, 8])
        sel = sb("sel", [P, SUB, E])
        wsum = sb("wsum", [P, SUB])
        comb = sb("comb", [P, SUB, P], BF16)
        y = sb("yb", [P, SUB, D])
        st6 = sb("st6b", [P, SUB, 6])
        mv = sb("mvb", [P, SUB, 2])
        rstd = sb("rstdb", [P, SUB])
        ru = sb("rub", [P, SUB])
        spare = sb("spareb", [P, 1])

        psG, psU, psD = ps("psG", [P, 2, TB]), ps("psU", [P, 2, TB]), ps("psD", [P, 2, TB])
        psC, psF = ps("psC", [P, TB]), ps("psF", [P, TB])
        psFh = psF[:].bitcast(BF16)

        loads = [sem(n) for n in ("gate_loaded", "up_loaded", "down_loaded")]
        shared_loaded = sem("shared_loaded")
        high_setup = sem("high_setup")
        pool_setup, pe_setup, dve_setup = sem("fpool_setup"), sem("fpe_setup"), sem("fdve_setup")
        x_loaded = [sem(f"fx_loaded{k}") for k in range(2)]
        stored = sem("stored")
        wmax_all = sem("wmax_all")
        PE_F = Steps(sem("pe_front"), ["x0", "x1", "logits", "comb"])
        AC_F = Steps(sem("act_front"), ["x0", "h0", "x1", "h1", "sigmoid"])
        DV_X = Steps(sem("fdve_x"), ["l0", "l1"])
        RSTEPS = ["sb", "mx", "mn", "top1", "t2a", "t2b", "top2", "gsum", "ggt", "geq", "gtie", "gall", "grank",
                  "gmask", "gpen", "m1", "masked", *[f"best{s}" for s in range(SUB)], "spent",
                  *[f"taken{s}" for s in range(SUB)], "esel", "w", "ws", "wr", "rec",
                  "comb", "c1", "r1", "c2", "r2", "c3", "cT"]
        DV_F = Steps(sem("dve_front"), RSTEPS)
        PE_C = Steps(sem("pe_chunk"), [f"{n}{c}" for c in range(CH) for n in ("gate", "up", "comb")[:3 if c < CR else 2]])
        down_done = sem("down_done")
        sig_done = sem("sig_done")
        high_done, low_done = sem("high_done"), sem("low_done")
        DV_C = Steps(sem("dve_chunk"), [f"{n}{c}" for c in range(CH) for n in ("g", "u", "h")[:3 if c < CR else 2]])
        DV_L = Steps(sem("dve_lnb"), ["y"] + [f"s{i}" for i in range(SUB)] + [f"a{i}" for i in range(SUB)] + [*RSQRT]
                     + [f"n{i}" for i in range(SUB)])
        NLOADS = (2, 2, 1)
        NS = 7

        block = ctx.enter_context(nc.Block())

        def tiles(eng, prologue, main, tail):
            prologue()
            main(0, 0, "first")
            with eng.Fori(0, (NTB - 2) // 2) as h:
                for odd in range(2):
                    main(h * 2 + 1 + odd, 1 - odd, "")
            main(NTB - 1, 1, "last")
            tail()

        def rows(a, i):
            return a[bass.ds(i * TB, TB), :].rearrange("(s p) d -> p s d", p=P)

        def step(S, ins):
            ins.then_inc(S.sem, 1)

        def last_of(c):
            return f"h{c}" if c < CR else f"u{c}"

        @block.sync
        def _(sp):
            def load(i, k):
                sp.dma_start(xb[:, k], rows(x1, i)).then_inc(x_loaded[k], 16)

            def prologue():
                load(0, 0)
                sp.dma_start(rl[0:E], rw).then_inc(shared_loaded, 16)
                sp.dma_start(cbias[:], cb.partition_broadcast(P)).then_inc(shared_loaded, 16)
                for half in range(2):
                    sp.dma_start(wg[:, half, 0:CR, :].rearrange("p c (e h) -> p (c e) h", e=2),
                                 gw[:, P * half:P * half + P, :].rearrange("e c h -> c e h")).then_inc(loads[0], 16)
                sp.dma_start(wd[:, 0:CR, :], dw.rearrange("(c e) h o -> (e h) c o", e=2)).then_inc(loads[2], 16)
                sp.sem_inc(stored, 16)

            def store(i):
                DV_L.wait(sp, i, f"n{SUB - 1}")
                sp.dma_start(rows(out, i), y[:]).then_inc(stored, 16)

            def main(i, k, edge):
                if edge != "last":
                    if edge != "first":
                        DV_L.wait(sp, i - 1, "y")
                    load(i + 1, 1 - k)
                if edge != "first":
                    store(i - 1)

            def tail():
                store(NTB - 1)
                sp.wait_ge(stored, 16 * (NTB + 1))
            tiles(sp, prologue, main, tail)

        @block.gpsimd
        def _(pool):
            link, c = small_math(pool, nc, pool_setup)
            link(nc.gpsimd.memset(id32[:], 0.0))
            link(nc.gpsimd.affine_select(out=id32[:], in_=id32[:], compare_op=ALU.not_equal, fill=1.0, base=0,
                                         pattern=[[-1, P]], channel_multiplier=1))
            link(nc.gpsimd.tensor_copy(idb[:], id32[:]))
            link(nc.gpsimd.memset(lower[:], 1.0))
            link(nc.gpsimd.affine_select(out=lower[:], in_=lower[:], compare_op=ALU.is_gt, fill=0.0, base=0,
                                         pattern=[[1, 4], [-1, 4]], channel_multiplier=0))
            link(nc.gpsimd.memset(pick[:], 0.0))
            for part in range(3):
                v = pick[:].rearrange("p c (e h) -> p c e h", e=2)
                link(nc.gpsimd.affine_select(out=v, in_=v, compare_op=ALU.not_equal, fill=1.0, base=-E * part,
                                             pattern=[[-2, CR], [-1, 2], [0, EH]], channel_multiplier=1))
            link(nc.gpsimd.memset(comb[:], 0.0))
            assert c[0] == FPOOL_SETUP
            pool.wait_ge(dve_setup, MAXIMA)
            nc.gpsimd.partition_all_reduce(wall[:], wmax[:], P, bass.bass_isa.ReduceOp.max).then_inc(wmax_all, 1)

        @block.scalar
        def _(act):
            def front(i, k, what):
                if what < 2:
                    PE_F.wait(act, i, f"x{what}")
                    step(AC_F, nc.scalar.mul(xT[:, k, what, :], psF[:], XS))
                    step(AC_F, nc.scalar.mul(xT16[:, k, 0, what, :], psF[:], XS))
                else:
                    PE_F.wait(act, i, "logits")
                    step(AC_F, nc.scalar.activation(sc[:].rearrange("p s e -> p (s e)"), psF[:, 0:SUB * E], ACT.Sigmoid,
                                                    scale=1.0 / XS))

            def high(i, c, edge):
                if not (edge == "first" and c < 4):
                    act.wait_ge(down_done, i * CH + c - 3)
                DV_C.wait(act, i, last_of(c))
                nc.scalar.copy(hid16[:, c % 4, 0, :], hid[:, c % 2, :]).then_inc(high_done, 1)

            def prologue():
                for src, dst in ((sgw, sgl), (suw, sul), (sdw, sdl)):
                    act.dma_start(dst[:], src.rearrange("(s p) d -> p s d", p=P)).then_inc(shared_loaded, 16)
                for half in range(2):
                    act.dma_start(wu[:, half, 0:CR, :].rearrange("p c (e h) -> p (c e) h", e=2),
                                  uw[:, P * half:P * half + P, :].rearrange("e c h -> c e h")).then_inc(loads[1], 16)
                for what in range(3):
                    front(0, 0, what)
                act.wait_ge(dve_setup, SCALES)
                for m in range(3):
                    nc.scalar.activation(wh[:, m, 0], wf[:, m], ACT.Identity, scale=wscale[:, m:m + 1]).then_inc(high_setup, 1)

            def main(i, k, edge):
                for c in range(CH):
                    PE_C.wait(act, i, f"gate{c}")
                    if c >= 2:
                        DV_C.wait(act, i, f"u{c - 2}")
                    elif edge != "first":
                        DV_C.wait(act, i - 1, f"u{CH - 2 + c}")
                    nc.scalar.activation(sig[:, c % 2, :], psG[:, c % 2, :], ACT.Sigmoid,
                                         scale=unscale[:, 0:1]).then_inc(sig_done, 1)
                    if c:
                        high(i, c - 1, edge)
                    elif edge != "first":
                        high(i - 1, CH - 1, "")
                    if edge != "last" and c in (4, 5, 7):
                        front(i + 1, 1 - k, (4, 5, 7).index(c))
            tiles(act, prologue, main, lambda: high(NTB - 1, CH - 1, ""))

        @block.vector
        def _(dve):
            V = nc.vector
            banks = [psG[:, 0], psG[:, 1], psU[:, 0], psU[:, 1], psD[:, 0], psD[:, 1]]
            dsts = [wg[:, 0, CR:], wg[:, 1, CR:], wu[:, 0, CR:], wu[:, 1, CR:], wd[:, CR:, 0:P], wd[:, CR:, P:2 * P]]
            for n, (bank, dst) in enumerate(zip(banks, dsts)):
                dve.wait_ge(pe_setup, n + 2)
                V.tensor_copy(dst, bank.rearrange("p (s t) -> p s t", t=P)).then_inc(dve_setup, 1)
                if n == 0:
                    V.tensor_copy(wr[:], psC[:, 0:2 * E].rearrange("p (a e) -> p a e", a=2)).then_inc(dve_setup, 1)

            def find_maxima(*matrices):
                dve.wait_ge(dve_setup, NS)
                for m in matrices:
                    dve.wait_ge(loads[m], 16 * NLOADS[m])
                    V.tensor_reduce(wmax[:, m:m + 1], wf[:, m], AX, ALU.max, apply_absolute_value=True).then_inc(dve_setup, 1)

            def scale_weights():
                done = MAXIMA

                def link(ins):
                    nonlocal done
                    ins.then_inc(dve_setup, 1)
                    done += 1
                    dve.wait_ge(dve_setup, done)
                I32 = mybir.dt.int32
                dve.wait_ge(wmax_all, 1)
                link(V.tensor_scalar(wall[:], wall[:], 1e-15, None, ALU.max))
                link(V.tensor_scalar(wall[:].bitcast(I32), wall[:].bitcast(I32), 0x7f800000, None, ALU.bitwise_and))
                link(V.reciprocal(wscale[:], wall[:]))
                link(V.tensor_scalar(unscale[:, 1:2], wscale[:, 0:1], 2.0 ** -13 / XS, None, ALU.mult))
                link(V.tensor_scalar(wscale[:], wscale[:], 2.0 ** 10, None, ALU.mult))
                link(V.tensor_scalar(unscale[:, 0:1], wall[:, 0:1], 2.0 ** -10 / XS, None, ALU.mult))
                link(V.scalar_tensor_tensor(out=unscale[:, 2:3], in0=wall[:, 0:1], scalar=2.0 ** -7, in1=wall[:, 1:2], op0=ALU.mult, op1=ALU.mult))
                link(V.tensor_tensor(unscale[:, 2:3], unscale[:, 2:3], wall[:, 2:3], ALU.mult))
                assert done == SCALES
                for m in range(3):
                    dve.wait_ge(high_setup, m + 1)
                    V.scalar_tensor_tensor(out=wh[:, m, 1], in0=wf[:, m], scalar=wscale[:, m:m + 1], in1=wh[:, m, 0],
                                           op0=ALU.mult, op1=ALU.subtract).then_inc(dve_setup, 1)

            def low_x(i, k):
                for a in range(2):
                    AC_F.wait(dve, i, f"h{a}")
                    step(DV_X, V.tensor_tensor(xT16[:, k, 1, a, :], xT[:, k, a, :], xT16[:, k, 0, a, :], ALU.subtract))

            def low(i, c):
                dve.wait_ge(high_done, i * CH + c + 1)
                V.tensor_tensor(hid16[:, c % 4, 1, :], hid[:, c % 2, :], hid16[:, c % 4, 0, :], ALU.subtract).then_inc(low_done, 1)

            def tt(i, name, out_, a, b, op, after=None):
                if after:
                    DV_F.wait(dve, i, after)
                step(DV_F, V.tensor_tensor(out_, a, b, op))

            def router_steps(i, k):
                four = [P, SUB, 4, 4]
                mxv, mnv = mx[:], mn[:]
                g3 = masked[:].rearrange("p s (g m) -> p (s g) m", m=4)
                sb3 = sbias[:].rearrange("p s (g m) -> p (s g) m", m=4)
                gm3 = gmask[:].rearrange("p s g -> p (s g)").unsqueeze(2).to_broadcast([P, SUB * 4, 4])
                gp3 = gpen[:].rearrange("p s g -> p (s g)").unsqueeze(2).to_broadcast([P, SUB * 4, 4])

                def s0():
                    AC_F.wait(dve, i, "sigmoid")
                    tt(i, "sb", sbias[:], sc[:], cbias[:].unsqueeze(1).to_broadcast([P, SUB, E]), ALU.add)
                    tt(i, "mx", mxv, sb3[:, :, 0:4:2], sb3[:, :, 1:4:2], ALU.max, "sb")
                    tt(i, "mn", mnv, sb3[:, :, 0:4:2], sb3[:, :, 1:4:2], ALU.min)
                    tt(i, "top1", tp[:, 0], mxv[:, :, 0], mxv[:, :, 1], ALU.max, "mx")
                    tt(i, "t2a", tp[:, 1], mxv[:, :, 0], mxv[:, :, 1], ALU.min)
                    tt(i, "t2b", tp[:, 2], mnv[:, :, 0], mnv[:, :, 1], ALU.max, "mn")
                    tt(i, "top2", tp[:, 3], tp[:, 1], tp[:, 2], ALU.max, "t2b")
                    tt(i, "gsum", gsum[:].rearrange("p s g -> p (s g)"), tp[:, 0], tp[:, 3], ALU.add, "top2")

                def s1():
                    other, own = gsum[:].unsqueeze(2).to_broadcast(four), gsum[:].unsqueeze(3).to_broadcast(four)
                    tt(i, "ggt", cg[:, 0], other, own, ALU.is_gt, "gsum")
                    tt(i, "geq", cg[:, 1], other, own, ALU.is_equal)
                    tt(i, "gtie", cg[:, 1], cg[:, 1], lower[:].unsqueeze(1).to_broadcast(four), ALU.mult, "geq")
                    tt(i, "gall", cg[:, 0], cg[:, 0], cg[:, 1], ALU.add, "gtie")
                    DV_F.wait(dve, i, "gall")
                    step(DV_F, V.tensor_reduce(gpen[:], cg[:, 0], AX, ALU.add))
                    DV_F.wait(dve, i, "grank")
                    step(DV_F, V.tensor_scalar(gmask[:], gpen[:], 2.0, None, ALU.is_lt))
                    DV_F.wait(dve, i, "gmask")
                    step(DV_F, V.tensor_scalar(gpen[:], gmask[:], 1.0, 1e30, ALU.subtract, ALU.mult))
                    tt(i, "m1", g3, sb3, gm3, ALU.mult, "gpen")
                    tt(i, "masked", g3, g3, gp3, ALU.add, "m1")

                def s2():
                    DV_F.wait(dve, i, "masked")
                    V.memset(spare[:], 0.0)
                    for s in range(SUB):
                        step(DV_F, V.max(best[:, s], masked[:, s]))
                    DV_F.wait(dve, i, f"best{SUB - 1}")
                    step(DV_F, V.memset(best[:, :, 4:8], TAKEN))

                def s3():
                    DV_F.wait(dve, i, "spent")
                    V.memset(spare[:], 0.0)
                    for s in range(SUB):
                        step(DV_F, V.match_replace(sel[:, s], best[:, s], masked[:, s], TAKEN))

                def s4():
                    DV_F.wait(dve, i, f"taken{SUB - 1}")
                    step(DV_F, V.tensor_scalar(sel[:], sel[:], TAKEN, None, ALU.is_equal))
                    tt(i, "w", w[:], sc[:], sel[:], ALU.mult, "esel")
                    DV_F.wait(dve, i, "w")
                    step(DV_F, V.tensor_reduce(wsum[:], w[:], AX, ALU.add))
                    DV_F.wait(dve, i, "ws")
                    step(DV_F, V.tensor_scalar(wsum[:], wsum[:], 1e-20, None, ALU.add))

                def s5():
                    DV_F.wait(dve, i, "wr")
                    step(DV_F, V.reciprocal(wsum[:], wsum[:]))
                return s0, s1, s2, s3, s4, s5

            def combine(i, k):
                c1, c2, c3 = (comb[:, :, E * n:E * n + E] for n in range(3))
                tt(i, "comb", w[:], w[:], wsum[:].unsqueeze(2).to_broadcast([P, SUB, E]), ALU.mult, "rec")
                DV_F.wait(dve, i, "comb")
                step(DV_F, V.tensor_copy(c1, w[:]))
                tt(i, "r1", w[:], w[:], c1, ALU.subtract, "c1")
                DV_F.wait(dve, i, "r1")
                step(DV_F, V.tensor_copy(c2, w[:]))
                tt(i, "r2", w[:], w[:], c2, ALU.subtract, "c2")
                DV_F.wait(dve, i, "r2")
                step(DV_F, V.tensor_copy(c3, w[:]))

            def copy_comb(i, k):
                PE_F.wait(dve, i, "comb")
                step(DV_F, V.tensor_copy(cT[:, k, :], psFh[:, 0:TB]))

            def chunk(i, k, c, edge):
                dve.wait_ge(sig_done, i * CH + c + 1)
                step(DV_C, V.scalar_tensor_tensor(out=sig[:, c % 2], in0=psG[:, c % 2], scalar=unscale[:, 0:1],
                                                  in1=sig[:, c % 2], op0=ALU.mult, op1=ALU.mult))
                if c:
                    low(i, c - 1)
                elif edge != "first":
                    low(i - 1, CH - 1)
                PE_C.wait(dve, i, f"up{c}")
                if c >= 2 or edge != "first":
                    dve.wait_ge(low_done, i * CH + c - 1)
                DV_C.wait(dve, i, f"g{c}")
                step(DV_C, V.scalar_tensor_tensor(out=hid[:, c % 2], in0=psU[:, c % 2], scalar=unscale[:, 1:2],
                                                  in1=sig[:, c % 2], op0=ALU.mult, op1=ALU.mult))
                if c < CR:
                    PE_C.wait(dve, i, f"comb{c}")
                    DV_C.wait(dve, i, f"u{c}")
                    step(DV_C, V.tensor_tensor(hid[:, c % 2], hid[:, c % 2], psC[:], ALU.mult))

            def residual(i, k):
                dve.wait_ge(down_done, i * CH + CH)
                dve.wait_ge(stored, i * 16 + 16)
                step(DV_L, V.scalar_tensor_tensor(out=y[:].rearrange("p s d -> p (s d)"), in0=psD[:].rearrange("p a b -> p (a b)"),
                                                  scalar=unscale[:, 2:3], in1=xb[:, k].rearrange("p s d -> p (s d)"),
                                                  op0=ALU.mult, op1=ALU.add))

            def norm_stats(i):
                DV_L.wait(dve, i, "y")
                for s in range(SUB):
                    step(DV_L, V.bn_stats(st6[:, s, :], y[:, s, :]))
                DV_L.wait(dve, i, f"s{SUB - 1}")
                V.memset(spare[:], 0.0)
                for s in range(SUB):
                    step(DV_L, V.bn_aggr(mv[:, s, :], st6[:, s, :]))

            def norm_out(i):
                rsqrt(dve, V, DV_L, i, f"a{SUB - 1}", rstd[:], mv[:, :, 1], ru[:], 1e-5, 1.0)
                DV_L.wait(dve, i, RSQRT[-1])
                for s in range(SUB):
                    step(DV_L, V.tensor_scalar(y[:, s, :], y[:, s, :], mv[:, s, 0:1], rstd[:, s:s + 1],
                                               ALU.subtract, ALU.mult))

            def prologue():
                low_x(0, 0)
                find_maxima(0)
                for s in router_steps(0, 0):
                    s()
                combine(0, 0)
                find_maxima(2, 1)
                copy_comb(0, 0)
                scale_weights()

            def main(i, k, edge):
                steps = router_steps(i + 1, 1 - k)
                for c in range(CH):
                    chunk(i, k, c, edge)
                    if edge != "first":
                        if c == 1:
                            residual(i - 1, 1 - k)
                        if c == 2:
                            norm_stats(i - 1)
                        if c == 3:
                            norm_out(i - 1)
                    if edge != "last":
                        if c == 6:
                            low_x(i + 1, 1 - k)
                        if c == 7:
                            steps[0]()
                            steps[1]()
                        if c == 8:
                            steps[2]()
                        if c == 9:
                            steps[3]()
                            steps[4]()
                            steps[5]()
                        if c == 10:
                            combine(i + 1, 1 - k)
                if edge != "last":
                    copy_comb(i + 1, 1 - k)

            def tail():
                low(NTB - 1, CH - 1)
                residual(NTB - 1, 1)
                norm_stats(NTB - 1)
                norm_out(NTB - 1)
            tiles(dve, prologue, main, tail)

        @block.tensor
        def _(pe):
            pe.wait_ge(pool_setup, FPOOL_SETUP)
            pe.wait_ge(shared_loaded, 16 * 5)
            for a in range(2):
                mm = pe.transpose(psC[:, E * a:E * a + E], rl[0:E, P * a:P * a + P], id32[0:E, 0:E])
            mm.then_inc(pe_setup, 1)
            for src, dst in ((sgl, psG), (sul, psU)):
                for a in range(2):
                    for s in range(CS):
                        mm = pe.transpose(dst[:, a, P * s:P * s + P], src[:, s, P * a:P * a + P], id32[:])
                    mm.then_inc(pe_setup, 1)
            for r in range(2):
                for s in range(CS):
                    mm = pe.transpose(psD[:, r, P * s:P * s + P], sdl[:, r, P * s:P * s + P], id32[:])
                mm.then_inc(pe_setup, 1)

            def front_x(i, k, a, load):
                if a == 0:
                    pe.wait_ge(x_loaded[k], load * 16 + 16)
                else:
                    AC_F.wait(pe, i, "h0")
                for s in range(SUB):
                    mm = pe.transpose(psF[:, P * s:P * s + P], xb[:, k, s, P * a:P * a + P], id32[:])
                step(PE_F, mm)

            def front_logits(i, k):
                AC_F.wait(pe, i, "h1")
                for s in range(SUB):
                    for a in range(2):
                        mm = pe.matmul(psF[:, E * s:E * s + E], xT[:, k, a, P * s:P * s + P], wr[:, a, :], start=(a == 0), stop=(a == 1))
                step(PE_F, mm)

            def front_comb(i, k):
                DV_F.wait(pe, i, "c3")
                for s in range(SUB):
                    mm = pe.transpose(psFh[:, P * s:P * s + P], comb[:, s, :], idb[:])
                step(PE_F, mm)

            def gate_up(i, k, c, edge):
                for w_, ps_, name in ((wg16, psG, "gate"), (wu16, psU, "up")):
                    if name == "gate":
                        if c >= 2:
                            DV_C.wait(pe, i, f"u{c - 2}")
                        elif edge != "first":
                            DV_C.wait(pe, i - 1, f"u{CH - 2 + c}")
                    for a in range(2):
                        for wp, xp in ((0, 0), (0, 1), (1, 0)):
                            mm = pe.matmul(ps_[:, c % 2, :], w_[:, wp, a, c, :], xT16[:, k, xp, a, :],
                                           start=(a == 0 and wp == xp), stop=(a == 1 and wp == 1))
                    step(PE_C, mm)
                if c == 0:
                    DV_F.wait(pe, i, "cT")
                if c < CR:
                    if c:
                        DV_C.wait(pe, i, f"h{c - 1}")
                    elif edge != "first":
                        DV_C.wait(pe, i - 1, f"h{CR - 1}")
                    step(PE_C, pe.matmul(psC[:], pick[:, c, :], cT[:, k, :], start=True, stop=True))

            def down(i, c, first_tile):
                pe.wait_ge(low_done, i * CH + c + 1)
                if c == 0 and first_tile:
                    pe.wait_ge(dve_setup, SCALES + 3)
                elif c == 0:
                    DV_L.wait(pe, i - 1, "y")
                for s in range(SUB):
                    for hp, wp in ((0, 0), (0, 1), (1, 0)):
                        mm = pe.matmul(psD[:, s // 2, D * (s % 2):D * (s % 2) + D], hid16[:, c % 4, hp, P * s:P * s + P],
                                       wd16[:, wp, c, :], start=(c == 0 and s % 2 == 0 and hp == wp),
                                       stop=(c == CH - 1 and hp == 1), skip_group_check=True)
                mm.then_inc(down_done, 1)

            def prologue():
                pe.wait_ge(dve_setup, NS)
                front_x(0, 0, 0, 0)
                front_x(0, 0, 1, 0)
                front_logits(0, 0)
                front_comb(0, 0)
                pe.wait_ge(dve_setup, SCALES + 2)

            def main(i, k, edge, load):
                for c in range(CH):
                    if c == 0:
                        DV_X.wait(pe, i, "l1")
                    gate_up(i, k, c, edge)
                    if c >= 2:
                        down(i, c - 2, edge == "first")
                    elif edge != "first":
                        down(i - 1, CH - 2 + c, False)
                    if edge != "last":
                        if c in (3, 4):
                            front_x(i + 1, 1 - k, c - 3, load)
                        if c == 6:
                            front_logits(i + 1, 1 - k)
                        if c == 11:
                            front_comb(i + 1, 1 - k)

            prologue()
            main(0, 0, "first", 0)
            with pe.Fori(0, (NTB - 2) // 2) as h:
                for odd in range(2):
                    main(h * 2 + 1 + odd, 1 - odd, "", h + 1)
            main(NTB - 1, 1, "last", None)
            for c in (CH - 2, CH - 1):
                down(NTB - 1, c, False)


FPOOL_SETUP = 10
MAXIMA = 7 + 3
SCALES = MAXIMA + 8

_INS = ["L0_attn_x", "L0_attn_qW", "L0_attn_qb", "L0_attn_kW", "L0_attn_kb", "L0_attn_vW", "L0_attn_vb", "L0_attn_oW",
        "L0_attn_ob", "L0_attn_J", "L0_ffn_router_w", "L0_ffn_correction_bias", "L0_ffn_gate_w", "L0_ffn_up_w",
        "L0_ffn_down_w", "L0_ffn_shared_gate_w", "L0_ffn_shared_up_w", "L0_ffn_shared_down_w"]


def program(nc, ins, out):
    x, qW, qb, kW, kb, vW, vb, oW, ob, J, rw, cb, gw, uw, dw, sgw, suw, sdw = ins
    x1 = nc.dram_tensor("x1", (NTOK, D), F32, kind="Internal").ap()
    attention(nc, x, qW, qb, kW, kb, vW, vb, oW, ob, J, x1)
    feed_forward(nc, x1, rw, cb, gw, uw, dw, sgw, suw, sdw, out.rearrange("b t d -> (b t) d"))


def kernel(**inputs):
    import concourse.bacc as _bacc
    from concourse.bass_utils import run_bass_kernel_spmd as _run

    nc = _bacc.Bacc("TRN2", target_bir_lowering=False, num_devices=1)
    arrays, ins = {}, []
    for name in _INS:
        a = np.ascontiguousarray(inputs[name])
        arrays[f"in_{name}"] = a
        ins.append(nc.dram_tensor(f"in_{name}", a.shape, mybir.dt.from_np(a.dtype), kind="ExternalInput").ap())
    out = nc.dram_tensor("out", (B, T, D), F32, kind="ExternalOutput").ap()
    program(nc, ins, out)
    return _run(nc, [arrays], core_ids=[0]).results[0]["out"]
```

```python
from contextlib import ExitStack

import concourse.bass as bass
import numpy as np
from concourse import mybir

ALU = mybir.AluOpType
ACT = mybir.ActivationFunctionType
F32 = mybir.dt.float32
F16 = mybir.dt.float16
BF16 = mybir.dt.bfloat16
AX = mybir.AxisListType.X

P = 128
B, T, D = 16, 1024, 256
HEADS, DH, COMP = 16, 16, 64
NHG = 4
ST = T // P
QS = 256.0
SIGN = {(1, 0): -1.0, (2, 0): -1.0, (3, 0): -1.0, (2, 1): -1.0, (3, 2): -1.0, (1, 3): -1.0}
NTOK = B * T
TB = 512
NTB = NTOK // TB
SUB = TB // P
E, EH, HS = 16, 64, 512
CR, CS = E * EH // P, HS // P
CH = CR + CS
TAKEN = -3e38
XS = 256.0


RSQRT = ("x", "half", "y0", "u1", "v1", "y1", "u2", "v2", "y2", "u3", "v3", "y3")


def rsqrt(dve, V, S, rnd, last, y, x, u, eps, scale):
    def step(ins):
        ins.then_inc(S.sem, 1)
    I32 = mybir.dt.int32
    S.wait(dve, rnd, last)
    step(V.tensor_scalar(u, x, eps, scale, ALU.add, ALU.mult))
    S.wait(dve, rnd, "x")
    step(V.tensor_scalar(y.bitcast(I32), u.bitcast(I32), 1, None, ALU.logical_shift_right))
    S.wait(dve, rnd, "half")
    step(V.tensor_scalar(y.bitcast(I32), y.bitcast(I32), -1.0, float(0x5f3759df), ALU.mult, ALU.add))
    for n in (1, 2, 3):
        S.wait(dve, rnd, f"y{n - 1}")
        step(V.tensor_tensor(x, y, y, ALU.mult))
        S.wait(dve, rnd, f"u{n}")
        step(V.scalar_tensor_tensor(out=x, in0=x, scalar=-0.5, in1=u, op0=ALU.mult, op1=ALU.mult))
        S.wait(dve, rnd, f"v{n}")
        step(V.scalar_tensor_tensor(out=y, in0=x, scalar=1.5, in1=y, op0=ALU.add, op1=ALU.mult))


class Steps:

    def __init__(self, sem, names):
        self.sem, self.at, self.n = sem, {s: i + 1 for i, s in enumerate(names)}, len(names)

    def wait(self, eng, rnd, step):
        eng.wait_ge(self.sem, rnd * self.n + self.at[step])


def small_math(eng, nc, sem):
    count = [0]

    def link(ins):
        ins.then_inc(sem, 1)
        count[0] += 1
        eng.wait_ge(sem, count[0])
    return link, count


def attention(nc, x, qW, qb, kW, kb, vW, vb, oW, ob, J, x1):
    xrows = x.rearrange("b t d -> (b t) d")
    with ExitStack() as ctx:
        def sb(name, shape, dt=F32):
            return ctx.enter_context(nc.sbuf_tensor(name, shape, dt))

        def sem(name):
            return ctx.enter_context(nc.semaphore(name))

        kst = sb("k_stat", [P, 2, HEADS // 2, 2, T], F16)
        qmv = sb("q_mov", [P, 2, HEADS // 2, T], F16)
        vall = sb("v_all", [P, 2, ST, D])
        vstat = sb("v_stat", [P, ST, 4, 2, DH])
        prob = sb("prob", [P, 8, T])
        osb = sb("osb", [P, T])
        onorm = sb("o_norm", [P, T])
        rden = sb("rden", [P, 2, 16])
        ot = sb("ot", [P, T])
        ysb = sb("y", [P, 2, ST, D])
        xt = sb("x_tile", [P, 2, D])
        x16 = sb("x_parts", [P, 2, 2, D], F16)
        xT = sb("xT", [P, 2, 2, P], F16)
        xpow, xinv, xun, xunv = (sb(n, [P, 2, 2]) for n in ("x_pow", "x_inv", "x_un", "x_unv"))
        wpow, wall, wun, wunv = (sb(n, [P, 1]) for n in ("wq_pow", "wq_all", "wq_un", "wq_unv"))
        qkb = sb("qkb", [P, 2, 4, COMP])
        qkn = sb("qkn", [P, 2, 4, COMP])
        n2 = sb("n2", [P, 2, COMP])
        rn = sb("rn", [P, 2, COMP])
        nu = sb("nu", [P, 2, COMP])
        parts = sb("parts", [P, 2, HEADS, 4, DH], F16)
        wqkv = sb("wqkv", [P, 2, 2, 3, D], F16)
        wo = sb("wo", [P, 2, D])
        half = sb("half", [P, 2, 2])
        rows4 = sb("rows4", [P, 4])
        bqkv = sb("bqkv", [P, 3, D])
        bo = sb("bo", [P, D])
        id32 = sb("id32", [P, P])
        id16 = sb("id16", [P, P], F16)
        jt = sb("jt", [P, 4])
        st6 = sb("st6", [P, ST, 6])
        mv = sb("mv", [P, ST, 2])
        rstd = sb("rstd", [P, ST])
        ru = sb("ru", [P, ST])
        spare = sb("spare", [P, 1])
        pspare = sb("pspare", [P, ST])
        base = prob[:, 0:3, :].rearrange("p a b -> p (a b)")
        wbase = base[:, 0:768].rearrange("p (m w o) -> p m w o", m=3, w=4)
        wobase = base[:, 768:1024].rearrange("p (w o) -> p w o", w=4)
        bbase = base[:, 1024:2048].rearrange("p (m w o) -> p m w o", m=4, w=4)
        jrow = base[:, 2048:2304]
        jk = base[:, 2304:2560]
        wtmp = base[:, 2560:3072].rearrange("p (m o) -> p m o", m=2)
        wfull = prob[:, 3:5, :].rearrange("p a b -> p (a b)")[:, 0:1536].rearrange("p (a m o) -> p a m o", a=2, m=3)

        psS = ctx.enter_context(nc.psum_tensor("psS", [P, 2, T], F32))
        psO = ctx.enter_context(nc.psum_tensor("psO", [P, 2, 512], F32))
        pr0 = ctx.enter_context(nc.psum_tensor("pr0", [P, 512], F32))
        pr1 = ctx.enter_context(nc.psum_tensor("pr1", [P, 512], F32))
        pr0h = pr0[:].bitcast(F16)
        pr1h = pr1[:].bitcast(F16)
        psOh = psO[:].bitcast(F16)

        j_loaded = sem("j_loaded")
        w_loaded = sem("w_loaded")
        wo_loaded = sem("wo_loaded")
        pool_setup = sem("pool_setup")
        dve_setup = sem("dve_setup")
        act_setup = sem("act_setup")
        w_max = sem("w_max")
        x_loaded = sem("x_loaded")
        y_loaded = sem("y_loaded")
        y_biased = sem("y_biased")
        x1_stored = sem("x1_stored")
        scores_done = sem("scores_done")
        exp_done = sem("exp_done")
        pv_done = sem("pv_done")
        v_staged = sem("v_staged")
        proj_done = sem("proj_done")
        proj_added = sem("proj_added")
        DV_S = Steps(sem("dve_scale"), ["max", "clamp", "pow", "inv", "un", "unv"])
        PL_X = Steps(sem("pool_x"), ["hi", "xs", "lo"])
        PE_X = Steps(sem("pe_x"), ["xT"])
        PE_QKV = Steps(sem("pe_qkv"), ["q", "k", "v"])
        PE_T = Steps(sem("pe_t"), ["qT", "kT"])
        X_COPIED = Steps(sem("x_copied"), ["xT"])
        DV_QKV = Steps(sem("dve_qkv"), ["qk", "sq", "n2", *RSQRT, "v", "norm", "qhi", "khi0", "khi1", "qlo", "klo0", "klo1"])
        T_COPIED = Steps(sem("t_copied"), ["qT", "kT0", "kT1"])
        DV_LN = Steps(sem("dve_ln"), [f"stats{s}" for s in range(ST)] + [f"mean{s}" for s in range(ST)] + [*RSQRT]
                      + [f"out{s}" for s in range(ST)])
        DV_NORM = Steps(sem("dve_norm"), ["o0", "o1", "r0", "m0", "r1", "m1"])
        DV_OT = Steps(sem("dve_ot"), ["n0", "n1"])

        NW = 6 + 4
        block = ctx.enter_context(nc.Block())

        def each_iteration(eng, prologue, body, tail, batch_end=lambda b, par: None):
            def batch(b, par, edge):
                for hg in range(NHG):
                    body(b * 4 + hg, hg, b, par, edge)
                batch_end(b, par)
            prologue()
            batch(0, 0, "first")
            with eng.Fori(0, (B - 4) // 2) as b2:
                for odd in range(2):
                    batch(b2 * 2 + 1 + odd, 1 - odd, "")
            batch(B - 3, 1, "")
            batch(B - 2, 0, "last but one")
            batch(B - 1, 1, "last")
            tail()

        def products(hg, b, edge):
            if edge == "first" and hg < 2:
                return None, None
            return b * 2 + hg // 2 - 1, (0, 1) if hg % 2 == 0 else (2, 3)

        def pairs_ahead(hg, edge):
            return {"last": 0, "last but one": min(NHG - 1 - hg, 2)}.get(edge, 2)

        OGROUPS = [(0, 0), (1, 2), (0, 4), (1, 6)]
        NOG = len(OGROUPS)
        SLOT = {"x^T a": 0, "q a": 1, "k a": 3, "v a": 5, "x^T b": 6, "out 0": 7, "q^T a": 8, "q b": 9,
                "k^T a": 9, "k b": 10, "v b": 11, "out 1": 13, "q^T b": 15, "k^T b": 15}

        @block.sync
        def _(sp):
            sp.dma_start(jrow, J.partition_broadcast(P)).then_inc(j_loaded, 16)

            def load_x(w):
                if not (isinstance(w, int) and w == 0):
                    PL_X.wait(sp, w - 1, "lo")
                sp.dma_start(xt[:], xrows[bass.ds(w * 2 * P, 2 * P), :].rearrange("(k p) d -> p k d", p=P)).then_inc(x_loaded, 16)

            def prologue():
                load_x(0)
                for m, v in enumerate((qb, kb, vb, ob)):
                    sp.dma_start(bbase[:, m], v.partition_broadcast(P)).then_inc(w_loaded, 16)
                for j in range(4):
                    for second in range(2):
                        r = 32 * j + DH * second
                        sp.dma_start(wobase[r:r + DH], oW[:, DH * j:DH * j + DH].rearrange("w d o -> d w o")).then_inc(wo_loaded, 16)
                for w in range(1, 6):
                    load_x(w)

            def body(g, hg, b, par, edge):
                if hg == 0:
                    if edge != "first":
                        sp.wait_ge(x1_stored, b * 16)
                    sp.dma_start(ysb[:, par], token_tiles(xrows, b)).then_inc(y_loaded, 16)
                if pairs_ahead(hg, edge) > 1:
                    load_x(g + 6)

            def token_tiles(rows, b):
                return rows[bass.ds(b * T, T), :].rearrange("(s p) d -> p s d", p=P)

            def store(b, par):
                DV_LN.wait(sp, b, f"out{ST - 1}")
                sp.dma_start(token_tiles(x1, b), ysb[:, par]).then_inc(x1_stored, 16)

            def batch_end(b, par):
                if isinstance(b, int) and b == 0:
                    sp.sem_inc(x1_stored, 16)
                else:
                    store(b - 1, 1 - par)

            def tail():
                store(B - 1, 1)
                sp.wait_ge(x1_stored, 16 * (B + 1))
            each_iteration(sp, prologue, body, tail, batch_end)

        @block.gpsimd
        def _(pool):
            link, count = small_math(pool, nc, pool_setup)
            link(nc.gpsimd.memset(id32[:], 0.0))
            link(nc.gpsimd.affine_select(out=id32[:], in_=id32[:], compare_op=ALU.not_equal, fill=1.0, base=0,
                                         pattern=[[-1, P]], channel_multiplier=1))
            link(nc.gpsimd.tensor_copy(id16[:], id32[:]))
            assert count[0] == POOL_IDS

            def split_x(w, k):
                G, by = nc.gpsimd, xinv[:, k].unsqueeze(2).to_broadcast([P, 2, D])
                DV_S.wait(pool, w, "inv")
                if not (isinstance(w, int) and w == 0):
                    PE_X.wait(pool, w * 2 - 1, "xT")
                G.tensor_tensor(x16[:, :, 0], xt[:], by, ALU.mult).then_inc(PL_X.sem, 1)
                PL_X.wait(pool, w, "hi")
                G.tensor_tensor(xt[:], xt[:], by, ALU.mult).then_inc(PL_X.sem, 1)
                PL_X.wait(pool, w, "xs")
                G.tensor_tensor(x16[:, :, 1], xt[:], x16[:, :, 0], ALU.subtract).then_inc(PL_X.sem, 1)
            split_x(0, 0)
            pool.wait_ge(w_max, 1)
            nc.gpsimd.partition_all_reduce(wall[:], wpow[:], P, bass.bass_isa.ReduceOp.max).then_inc(w_max, 1)
            split_x(1, 1)
            link(nc.gpsimd.memset(rows4[:], 1.0))
            link(nc.gpsimd.affine_select(out=rows4[:], in_=rows4[:], compare_op=ALU.is_ge, fill=0.0, base=0,
                                         pattern=[[-32, 4]], channel_multiplier=1))
            link(nc.gpsimd.affine_select(out=rows4[:], in_=rows4[:], compare_op=ALU.is_ge, fill=0.0, base=DH - 1,
                                         pattern=[[32, 4]], channel_multiplier=-1))
            link(nc.gpsimd.tensor_tensor(rows4[:, 0:2], rows4[:, 0:2], rows4[:, 2:4], ALU.add))
            link(nc.gpsimd.tensor_tensor(half[:, 0, 0:1], rows4[:, 0:1], rows4[:, 1:2], ALU.add))
            link(nc.gpsimd.tensor_scalar(half[:, 0, 1:2], half[:, 0, 0:1], -1.0, None, ALU.mult))
            link(nc.gpsimd.tensor_scalar(half[:, 1, 0:1], half[:, 0, 1:2], 1.0, None, ALU.add))
            link(nc.gpsimd.tensor_scalar(half[:, 1, 1:2], half[:, 1, 0:1], -1.0, None, ALU.mult))
            pool.wait_ge(w_loaded, 16 * NW)
            pool.wait_ge(wo_loaded, 16 * 8)
            for i in range(4):
                for o in range(4):
                    minus = (i, o) in SIGN
                    cols = slice(o * COMP, o * COMP + COMP)
                    sign_of_row = half[:, i % 2, minus:minus + 1].to_broadcast([P, COMP])
                    nc.gpsimd.tensor_tensor((wtmp if i % 2 else wo)[:, i // 2, cols], wobase[:, o ^ i, :], sign_of_row,
                                            ALU.mult).then_inc(pool_setup, 1)
                    src = bbase[:, 3, o ^ i, :]
                    if i == 0:
                        nc.gpsimd.tensor_copy(bo[:, cols], src).then_inc(pool_setup, 1)
                    else:
                        nc.gpsimd.tensor_tensor(bo[:, cols], bo[:, cols], src, ALU.subtract if minus else ALU.add).then_inc(pool_setup, 1)
                count[0] += 8
                pool.wait_ge(pool_setup, count[0])
            link(nc.gpsimd.tensor_tensor(wo[:], wo[:], wtmp, ALU.add))
            for par in range(2):
                split_x(2 + par, par)
                PL_X.wait(pool, 2 + par, "lo")
                link(nc.gpsimd.memset(kst[64:128, par, :, 0, :].bitcast(F32), 0.0))
                link(nc.gpsimd.memset(kst[0:64, par, :, 1, :].bitcast(F32), 0.0))
            assert count[0] == POOL_SETUP
            split_x(4, 0)
            pool.wait_ge(dve_setup, DVE_SETUP)

            def stage_v(g, hg, par, s, first):
                if not first:
                    pool.wait_ge(pv_done, (g - 1) * 2 * ST + 2 * s + 2)
                    nc.gpsimd.tensor_tensor(pspare[:, s:s + 1], id32[:, 0:1], id32[:, 0:1], ALU.mult)
                src = vall[:, par, s, bass.ds(hg * COMP, COMP)].rearrange("p (j d) -> p j d", j=4)
                nc.gpsimd.tensor_copy(vstat[:, s, :, 0, :], src).then_inc(v_staged, 1)

            def body(g, hg, b, par, edge):
                if hg == 0:
                    DV_QKV.wait(pool, b * ST + ST - 1, "v")
                for s in range(ST):
                    stage_v(g, hg, par, s, hg == 0 and edge == "first")
                if pairs_ahead(hg, edge):
                    split_x(g + 5, (hg + 1) % 2)
                if hg == 0:
                    pool.wait_ge(y_loaded, b * 16 + 16)
                    for s in range(ST):
                        nc.gpsimd.tensor_tensor(ysb[:, par, s], ysb[:, par, s], bo[:], ALU.add).then_inc(y_biased, 1)

            each_iteration(pool, lambda: None, body, lambda: None)

        @block.scalar
        def _(act):
            for m, w in enumerate((qW, kW, vW)):
                for half in range(2):
                    act.dma_start(wbase[64 * half:64 * half + 64, m], w.rearrange("w d o -> d w o")).then_inc(w_loaded, 16)
            act.wait_ge(dve_setup, J_REDUCED)
            nc.scalar.activation(jk, jrow, ACT.Sin).then_inc(act_setup, 1)
            act.wait_ge(dve_setup, J_SUMMED)
            nc.scalar.activation(jt[:, 1:2], jt[:, 0:1], ACT.Exp, scale=0.1 / D).then_inc(act_setup, 1)

            def body(g, hg, b, par, edge):
                for n in range(4 * ST):
                    act.wait_ge(scores_done, g * 32 + n + 1)
                    if n % 4 == 0 and not (hg == 0 and edge == "first" and n < 8):
                        act.wait_ge(pv_done, g * 2 * ST + (n // 4) * 2 - 2)
                    if hg == 0 and edge == "first" and n == 0:
                        act.wait_ge(pool_setup, POOL_SETUP)
                    nc.scalar.activation(prob[:, n % 8, :], psS[:, n % 2, :], ACT.Exp,
                                         scale=DH ** -0.5 / (QS * QS)).then_inc(exp_done, 1)

            def copy_x(u, k):
                PE_X.wait(act, u, "xT")
                nc.scalar.copy(xT[:].rearrange("p t a b -> p (t a b)"), psOh[:, k, 0:512]).then_inc(X_COPIED.sem, 1)

            def copy_transposes(u):
                tok = bass.ds(u * P, P)
                PE_T.wait(act, u, "qT")
                nc.scalar.copy(qmv[:, 0, :, tok], pr1h.rearrange("p (a t) -> p a t", t=P)).then_inc(T_COPIED.sem, 1)
                PE_T.wait(act, u, "kT")
                for e in range(2):
                    r = slice(64 * e, 64 * e + 64)
                    nc.scalar.copy(kst[r, 0, :, e, tok], pr0h[r].rearrange("p (a t) -> p a t", t=P)).then_inc(T_COPIED.sem, 1)

            def prologue():
                def pair(a, more):
                    PE_QKV.wait(act, a, "v")
                    copy_x(a + 1, 1)
                    copy_transposes(a)
                    PE_QKV.wait(act, a + 1, "v")
                    if more:
                        copy_x(a + 2, 0)
                    copy_transposes(a + 1)
                copy_x(0, 0)
                with act.Fori(0, 3) as r:
                    pair(r * 2, True)
                pair(6, False)
            each_iteration(act, prologue, body, lambda: None)

        @block.vector
        def _(dve):
            V = nc.vector
            link, c = small_math(dve, nc, dve_setup)
            dve.wait_ge(j_loaded, 16)
            TWO_PI, MAGIC = float(2 * np.pi), 12582912.0
            link(V.tensor_scalar(jk, jrow, 1.0 / TWO_PI, MAGIC, ALU.mult, ALU.add))
            link(V.tensor_scalar(jk, jk, MAGIC, None, ALU.subtract))
            link(V.scalar_tensor_tensor(out=jrow, in0=jk, scalar=-6.28125, in1=jrow, op0=ALU.mult, op1=ALU.add))
            link(V.scalar_tensor_tensor(out=jrow, in0=jk, scalar=-(TWO_PI - 6.28125), in1=jrow, op0=ALU.mult, op1=ALU.add))
            link(V.tensor_scalar(jrow, jrow, 3.1415925, -3.1415925, ALU.min, ALU.max))
            assert c[0] == J_REDUCED

            def step(S, ins):
                ins.then_inc(S.sem, 1)

            def scale_of_x(w, k):
                I32, p = mybir.dt.int32, xpow[:, k]
                dve.wait_ge(x_loaded, w * 16 + 16)
                step(DV_S, V.tensor_reduce(p, xt[:], AX, ALU.max, apply_absolute_value=True))
                DV_S.wait(dve, w, "max")
                step(DV_S, V.tensor_scalar(p, p, 1e-15, 2.0 ** -10, ALU.max, ALU.mult))
                DV_S.wait(dve, w, "clamp")
                step(DV_S, V.tensor_scalar(p.bitcast(I32), p.bitcast(I32), 0x7f800000, None, ALU.bitwise_and))
                DV_S.wait(dve, w, "pow")
                step(DV_S, V.reciprocal(xinv[:, k], p))

            def unscale_of_x(w, k):
                DV_S.wait(dve, w, "pow")
                step(DV_S, V.tensor_scalar(xun[:, k], xpow[:, k], wun[:, 0:1], None, ALU.mult))
                step(DV_S, V.tensor_scalar(xunv[:, k], xpow[:, k], wunv[:, 0:1], None, ALU.mult))
            scale_of_x(0, 0)
            V.memset(vstat[:], 1.0).then_inc(dve_setup, 1)
            c[0] += 1
            dve.wait_ge(act_setup, 1)
            link(V.tensor_reduce(jt[:, 0:1], jk, AX, ALU.add))
            assert c[0] == J_SUMMED
            dve.wait_ge(w_loaded, 16 * NW)
            for i in range(4):
                rows = slice(64 * (i % 2), 64 * (i % 2) + 64)
                for o in range(4):
                    sgn = SIGN.get((i, o), 1.0)
                    cols = slice(o * COMP, o * COMP + COMP)
                    V.tensor_scalar(wfull[rows, i // 2, :, cols], wbase[rows, :, o ^ i, :], sgn, None, ALU.mult).then_inc(dve_setup, 1)
                    src = bbase[:, 0:3, o ^ i, :]
                    if i == 0:
                        V.tensor_copy(bqkv[:, :, cols], src).then_inc(dve_setup, 1)
                    else:
                        V.tensor_tensor(bqkv[:, :, cols], bqkv[:, :, cols], src, ALU.add if sgn > 0 else ALU.subtract).then_inc(dve_setup, 1)
                c[0] += 8
                dve.wait_ge(dve_setup, c[0])
            dve.wait_ge(act_setup, 2)
            ec = jt[:, 1:2]
            flat = wfull.rearrange("p a m o -> p (a m o)")
            hi, lo = (wqkv[:, t].rearrange("p a m o -> p (a m o)") for t in range(2))
            V.tensor_reduce(wpow[:], flat, AX, ALU.max, apply_absolute_value=True).then_inc(w_max, 1)
            link(V.tensor_scalar(bqkv[:, 2], bqkv[:, 2], ec, None, ALU.mult))
            ones = vstat[:, :, :, 1, :].rearrange("p s j d -> p (s j) d")
            link(V.tensor_scalar(ones, ones, ec, None, ALU.mult))
            dve.wait_ge(w_max, 2)
            link(V.tensor_scalar(wun[:], wall[:], 1e-15, 2.0 ** -10, ALU.max, ALU.mult))
            link(V.tensor_scalar(wun[:].bitcast(mybir.dt.int32), wun[:].bitcast(mybir.dt.int32), 0x7f800000, None, ALU.bitwise_and))
            link(V.reciprocal(wpow[:], wun[:]))
            link(V.tensor_scalar(hi, flat, wpow[:, 0:1], None, ALU.mult))
            link(V.scalar_tensor_tensor(out=lo, in0=flat, scalar=wpow[:, 0:1], in1=hi, op0=ALU.mult, op1=ALU.subtract))
            link(V.tensor_tensor(wunv[:], wun[:], ec, ALU.mult))
            assert c[0] == DVE_SETUP, c[0]
            dve.sem_inc(proj_added, 1)
            unscale_of_x(0, 0)

            S = DV_QKV
            hi_q = parts[:, 0, :, 0:2, :]
            lo_q = parts[:, 0, :, 2:4, :]

            def by_head(a, m):
                return a[:, m].rearrange("p c (j d) -> p (c j) d", j=4)

            def take_x(u):
                PE_X.wait(dve, u, "xT")
                step(X_COPIED, V.tensor_copy(xT[:].rearrange("p t a b -> p (t a b)"), pr0h[:, 0:512]))

            def take_qk(u, k, pair, qk=pr1):
                PE_QKV.wait(dve, u, "k")
                step(S, V.scalar_tensor_tensor(out=qkb[:].rearrange("p m c o -> p (m c o)"), in0=qk[:, 0:512],
                                               scalar=xun[:, pair, k:k + 1], in1=bqkv[:, 0:2].rearrange("p m o -> p (m o)"),
                                               op0=ALU.mult, op1=ALU.add))

            def take_v(u, k, pair, par, s, staged, v=pr0):
                PE_QKV.wait(dve, u, "v")
                if staged is not None:
                    dve.wait_ge(v_staged, staged)
                step(S, V.scalar_tensor_tensor(out=vall[:, par, s, :], in0=v[:, 0:256], scalar=xunv[:, pair, k:k + 1],
                                               in1=bqkv[:, 2], op0=ALU.mult, op1=ALU.add))

            def squares(u):
                S.wait(dve, u, "qk")
                step(S, V.tensor_tensor(qkn[:], qkb[:], qkb[:], ALU.mult))
                S.wait(dve, u, "sq")
                step(S, V.tensor_reduce(n2[:], qkn[:].rearrange("p m c o -> p m o c"), AX, ALU.add))

            def inverse_norms(u):
                rsqrt(dve, V, S, u, "n2", rn[:], n2[:], nu[:], 1e-6, 1.0 / (QS * QS))

            def normalise(u):
                S.wait(dve, u, RSQRT[-1])
                for_m = rn[:].unsqueeze(2).to_broadcast([P, 2, 4, COMP])
                step(S, V.tensor_tensor(qkn[:], qkb[:], for_m, ALU.mult))
                S.wait(dve, u, "norm")
                q, k = by_head(qkn, 0), by_head(qkn, 1)
                step(S, V.tensor_copy(hi_q, q.unsqueeze(2).to_broadcast([P, HEADS, 2, DH])))
                for t in (0, 2):
                    step(S, V.tensor_copy(parts[:, 1, :, t, :], k))

            def low_parts(u):
                S.wait(dve, u, "khi1")
                q, k = by_head(qkn, 0), by_head(qkn, 1)
                step(S, V.tensor_tensor(lo_q, q.unsqueeze(2).to_broadcast([P, HEADS, 2, DH]), hi_q, ALU.subtract))
                for t in (1, 3):
                    step(S, V.tensor_tensor(parts[:, 1, :, t, :], k, parts[:, 1, :, 0, :], ALU.subtract))

            def take_qT(u, par, s):
                PE_T.wait(dve, u, "qT")
                step(T_COPIED, V.tensor_copy(qmv[:, par, :, bass.ds(s * P, P)], pr1h.rearrange("p (a t) -> p a t", t=P)))

            def take_kT(u, par, s):
                PE_T.wait(dve, u, "kT")
                for e in range(2):
                    r = slice(64 * e, 64 * e + 64)
                    step(T_COPIED, V.tensor_copy(kst[r, par, :, e, bass.ds(s * P, P)], pr0h[r].rearrange("p (a t) -> p a t", t=P)))

            def norm(g, second):
                N = DV_NORM
                def turn(h):
                    dve.wait_ge(pv_done, g * 2 * ST + 2 * ST - 1 + h)
                    if not (isinstance(g, int) and g == 0):
                        N.wait(dve, g - 1, f"m{h}")
                    step(N, V.transpose(osb[:, 512 * h:512 * h + 512], psO[:, h, :]))

                def divide(h):
                    cols = slice(512 * h, 512 * h + 512)
                    turned = osb[:, cols].rearrange("p (b r) -> p b r", r=32)
                    mine = onorm[:, cols].rearrange("p (b r) -> p b r", r=32)[:, :, DH * second:DH * second + DH]
                    N.wait(dve, g, f"o{h}")
                    step(N, V.reciprocal(rden[:, h], turned[:, :, DH]))
                    N.wait(dve, g, f"r{h}")
                    step(N, V.tensor_tensor(mine, turned[:, :, 0:DH], rden[:, h].unsqueeze(2).to_broadcast([P, 16, DH]), ALU.mult))
                    if second:
                        N.wait(dve, g, f"m{h}")
                        step(DV_OT, V.transpose(ot[:, cols], onorm[:, cols]))
                return turn, divide

            def add_proj(pr, par, i):
                bank, t = OGROUPS[i]
                dve.wait_ge(proj_done, pr * NOG + i + 1)
                dst = ysb[:, par, t:t + 2].rearrange("p s d -> p (s d)")
                V.tensor_tensor(dst, dst, (pr1 if bank else pr0)[:], ALU.add).then_inc(proj_added, 1)

            def ln_stats(n, par):
                dve.wait_ge(proj_added, (n + 1) * 2 * NOG + 1)
                for s in range(ST):
                    step(DV_LN, V.bn_stats(st6[:, s, :], ysb[:, par, s, :]))

            def ln_mean(n):
                DV_LN.wait(dve, n, f"stats{ST - 1}")
                V.memset(spare[:], 0.0)
                for s in range(ST):
                    step(DV_LN, V.bn_aggr(mv[:, s, :], st6[:, s, :]))

            def ln_rstd(n):
                rsqrt(dve, V, DV_LN, n, f"mean{ST - 1}", rstd[:], mv[:, :, 1], ru[:], 1e-5, 1.0)

            def ln_out(n, par, tiles=range(ST)):
                DV_LN.wait(dve, n, RSQRT[-1])
                for s in tiles:
                    step(DV_LN, V.tensor_scalar(ysb[:, par, s, :], ysb[:, par, s, :], mv[:, s, 0:1], rstd[:, s:s + 1],
                                                ALU.subtract, ALU.mult))

            def prologue():
                for u in range(ST):
                    k, w = u % 2, u // 2
                    if k == 0:
                        scale_of_x(w + 1, (w + 1) % 2)
                        unscale_of_x(w + 1, (w + 1) % 2)
                    take_qk(u, k, w % 2, psS[:, 0, 512 * k:])
                    squares(u)
                    inverse_norms(u)
                    take_v(u, k, w % 2, 0, u, None, psS[:, 1, 512 * k:])
                    if u:
                        PE_T.wait(dve, u - 1, "kT")
                    normalise(u)
                    low_parts(u)

            def body(g, hg, b, par, edge):
                nxt, prep = 1 - par, edge != "last"
                ua, ub = (g + 4) * 2, (g + 4) * 2 + 1
                norm_group = not (edge == "first" and hg == 0)
                pr, two = products(hg, b, edge)
                po = 1 - par if hg < 2 else par
                norm_1, norm_2 = (edge != "first" and hg == h for h in (2, 3))
                staged = None if edge == "first" else b * NHG * ST

                def scale_next():
                    if pairs_ahead(hg, edge):
                        scale_of_x(g + 5, 1 - hg % 2)
                        unscale_of_x(g + 5, 1 - hg % 2)
                if norm_group:
                    turn, divide = norm(g - 1, hg % 2 == 0)
                    turn(0)
                if prep:
                    take_x(ua)
                if norm_group:
                    turn(1)
                    divide(0)
                if norm_1:
                    ln_stats(b - 1, 1 - par)
                if hg != 2:
                    scale_next()
                if norm_2:
                    ln_rstd(b - 1)
                if prep:
                    take_qk(ua, 0, hg % 2)
                    squares(ua)
                    inverse_norms(ua)
                    take_v(ua, 0, hg % 2, nxt, hg * 2, staged)
                    normalise(ua)
                    take_x(ub)
                    low_parts(ua)
                if two:
                    if hg == 2:
                        dve.wait_ge(y_biased, b * ST + ST)
                    add_proj(pr, po, two[0])
                if prep:
                    take_qT(ua, nxt, hg * 2)
                if norm_group:
                    divide(1)
                if hg == 2:
                    scale_next()
                if norm_1:
                    ln_mean(b - 1)
                if norm_2:
                    ln_out(b - 1, 1 - par, range(ST // 2))
                if prep:
                    take_kT(ua, nxt, hg * 2)
                    take_qk(ub, 1, hg % 2)
                    squares(ub)
                    inverse_norms(ub)
                    take_v(ub, 1, hg % 2, nxt, hg * 2 + 1, staged)
                if two:
                    add_proj(pr, po, two[1])
                if prep:
                    normalise(ub)
                    low_parts(ub)
                if norm_2:
                    ln_out(b - 1, 1 - par, range(ST // 2, ST))
                if prep:
                    take_qT(ub, nxt, hg * 2 + 1)
                    take_kT(ub, nxt, hg * 2 + 1)

            def tail():
                turn, divide = norm(4 * B - 1, True)
                for h in range(2):
                    turn(h)
                for h in range(2):
                    divide(h)
                for i in range(NOG):
                    add_proj(2 * B - 1, 1, i)
                ln_stats(B - 1, 1)
                ln_mean(B - 1)
                ln_rstd(B - 1)
                ln_out(B - 1, 1)
            each_iteration(dve, prologue, body, tail)

        @block.tensor
        def _(pe):
            pe.wait_ge(pool_setup, POOL_IDS)

            def transposes_x(u, k, w, bank=pr0h):
                PL_X.wait(pe, w, "lo")
                for t in range(2):
                    for a in range(2):
                        mm = pe.transpose(bank[:, P * (2 * t + a):P * (2 * t + a) + P], x16[:, k, t, P * a:P * a + P], id16[:])
                mm.then_inc(PE_X.sem, 1)

            def project(m, out_):
                for a in range(2):
                    for xp, wp in ((0, 0), (1, 0), (0, 1)):
                        mm = pe.matmul(out_, xT[:, xp, a, :], wqkv[:, wp, a, m, :], start=(a == 0 and xp == wp),
                                       stop=(a == 1 and wp == 1), skip_group_check=True)
                mm.then_inc(PE_QKV.sem, 1)

            def project_qk(u, m, qk=pr1):
                if m == 0:
                    X_COPIED.wait(pe, u, "xT")
                project(m, qk[:, D * m:D * m + D])

            def project_v(u, v=pr0):
                project(2, v[:, 0:D])

            def transposes_qk(u, m):
                DV_QKV.wait(pe, u, "klo1" if m else "qlo")
                for a in range(HEADS // 2):
                    blk = parts[:, m, 2 * a:2 * a + 2].rearrange("p h s d -> p (h s d)")
                    mm = pe.transpose((pr0h if m else pr1h)[:, P * a:P * a + P], blk, id16[:])
                mm.then_inc(PE_T.sem, 1)

            def out_proj(pr, hp, i):
                bank, t0 = OGROUPS[i]
                DV_OT.wait(pe, pr, "n0" if t0 < 4 else "n1")
                for t in range(2):
                    mm = pe.matmul((pr1 if bank else pr0)[:, D * t:D * t + D], ot[:, P * (t0 + t):P * (t0 + t) + P],
                                   wo[:, hp, :], start=True, stop=True, skip_group_check=True)
                mm.then_inc(proj_done, 1)

            def added(pr, i):
                pe.wait_ge(proj_added, pr * NOG + i + 2)

            def scores(g, hg, par, s, j, first):
                n = 4 * s + j
                if not (first and n < 2):
                    pe.wait_ge(exp_done, g * 32 + n - 1)
                pair = hg * 2 + j // 2
                for h in range(2):
                    lhsT = kst[:, par, bass.ds(pair, 1), j % 2, P * s:P * s + P].rearrange("p a t -> p (a t)")
                    rhs = qmv[:, par, bass.ds(pair, 1), 512 * h:512 * h + 512].rearrange("p a t -> p (a t)")
                    mm = pe.matmul(psS[:, n % 2, 512 * h:512 * h + 512], lhsT, rhs, start=True, stop=True)
                mm.then_inc(scores_done, 1)

            def pv(g, s, h):
                if h == 0:
                    pe.wait_ge(exp_done, g * 32 + 4 * s + 4)
                    pe.wait_ge(v_staged, g * 8 + s + 1)
                if s == 0 and not (isinstance(g, int) and g == 0):
                    DV_NORM.wait(pe, g - 1, f"o{h}")
                for j in range(4):
                    mm = pe.matmul(psO[32 * j:32 * j + 32, h, :], vstat[:, s, j].rearrange("p a d -> p (a d)"),
                                   prob[:, (4 * s + j) % 8, 512 * h:512 * h + 512], start=(s == 0), stop=(s == ST - 1),
                                   tile_position=(0, 32 * j))
                mm.then_inc(pv_done, 1)

            def prologue():
                def project_tile(u, k):
                    project_qk(u, 0, psS[:, 0, 512 * k:])
                    project_qk(u, 1, psS[:, 0, 512 * k:])
                    project_v(u, psS[:, 1, 512 * k:])

                def pair(a, r, more):
                    transposes_x(a + 1, 1, r, psOh[:, 1])
                    project_tile(a + 1, 1)
                    transposes_qk(a, 0)
                    transposes_qk(a, 1)
                    if more:
                        transposes_x(a + 2, 0, r + 1, psOh[:, 0])
                        project_tile(a + 2, 0)
                    T_COPIED.wait(pe, a, "kT1")
                    transposes_qk(a + 1, 0)
                    transposes_qk(a + 1, 1)
                    T_COPIED.wait(pe, a + 1, "kT1")
                transposes_x(0, 0, 0, psOh[:, 0])
                pe.wait_ge(dve_setup, DVE_SETUP)
                project_tile(0, 0)
                with pe.Fori(0, 3) as r:
                    pair(r * 2, r, True)
                pair(6, 3, False)
                pe.wait_ge(pool_setup, POOL_SETUP)

            def filler(g, hg, b, edge, slot):
                prep = edge != "last"
                pr, two = products(hg, b, edge)
                hp = (hg // 2 - 1) % 2
                ua, ub = (g + 4) * 2, (g + 4) * 2 + 1
                if prep and slot == SLOT["x^T a"]:
                    T_COPIED.wait(pe, ua - 1, "kT1")
                    transposes_x(ua, 0, g + 4)
                if prep and slot == SLOT["q a"]:
                    project_qk(ua, 0)
                if prep and slot == SLOT["k a"]:
                    project_qk(ua, 1)
                if prep and slot == SLOT["v a"]:
                    project_v(ua)
                if prep and slot == SLOT["x^T b"]:
                    DV_QKV.wait(pe, ua, "v")
                    transposes_x(ub, 1, g + 4)
                if two and slot == SLOT["out 0"]:
                    if prep:
                        X_COPIED.wait(pe, ub, "xT")
                    else:
                        added(pr, two[0] - 2)
                    out_proj(pr, hp, two[0])
                if prep and slot == SLOT["q^T a"]:
                    transposes_qk(ua, 0)
                if prep and slot == SLOT["q b"]:
                    T_COPIED.wait(pe, ua, "qT")
                    project_qk(ub, 0)
                if prep and slot == SLOT["k^T a"]:
                    if two:
                        added(pr, two[0])
                    else:
                        X_COPIED.wait(pe, ub, "xT")
                    transposes_qk(ua, 1)
                if prep and slot == SLOT["k b"]:
                    project_qk(ub, 1)
                if prep and slot == SLOT["v b"]:
                    T_COPIED.wait(pe, ua, "kT1")
                    project_v(ub)
                if two and slot == SLOT["out 1"]:
                    if prep:
                        DV_QKV.wait(pe, ub, "qk")
                    else:
                        added(pr, two[1] - 2)
                    out_proj(pr, hp, two[1])
                if prep and slot == SLOT["q^T b"]:
                    if two:
                        added(pr, two[1])
                    transposes_qk(ub, 0)
                if prep and slot == SLOT["k^T b"]:
                    transposes_qk(ub, 1)

            def body(g, hg, b, par, edge):
                first = hg == 0 and edge == "first"
                halves = (1, 3) if edge == "last" else (1, 2)
                if hg == 0:
                    T_COPIED.wait(pe, b * ST + ST - 1, "qT")
                for s in range(ST):
                    if hg == 0 and s == ST - 1:
                        T_COPIED.wait(pe, b * ST + ST - 1, "kT1")
                    for j in range(4):
                        scores(g, hg, par, s, j, first)
                        if j in halves and not (first and s == 0):
                            if s == 0:
                                pv(g - 1, ST - 1, halves.index(j))
                            else:
                                pv(g, s - 1, halves.index(j))
                        if j in (1, 3):
                            filler(g, hg, b, edge, 2 * s + j // 2)

            def tail():
                g = 4 * B - 1
                for h in range(2):
                    pv(g, ST - 1, h)
                for i in range(NOG):
                    added(2 * B - 1, i - 2)
                    out_proj(2 * B - 1, 1, i)
            each_iteration(pe, prologue, body, tail)


J_REDUCED, J_SUMMED = 5, 7
DVE_SETUP = J_SUMMED + 4 * 8 + 8
POOL_IDS = 3
POOL_SETUP = POOL_IDS + 8 + 4 * 8 + 1 + 4


def feed_forward(nc, x1, rw, cb, gw, uw, dw, sgw, suw, sdw, out):
    with ExitStack() as ctx:
        def sb(name, shape, dt=F32):
            return ctx.enter_context(nc.sbuf_tensor(name, shape, dt))

        def ps(name, shape):
            return ctx.enter_context(nc.psum_tensor(name, shape, F32))

        def sem(name):
            return ctx.enter_context(nc.semaphore(name))

        wf = sb("w_f32", [P, 3, CH * D])
        wg, wu = (wf[:, m].rearrange("p (a c h) -> p a c h", a=2, c=CH) for m in (0, 1))
        wd = wf[:, 2].rearrange("p (c o) -> p c o", c=CH)
        wh = sb("w_f16", [P, 3, 2, CH * D], F16)
        wg16, wu16 = (wh[:, m].rearrange("p t (a c h) -> p t a c h", a=2, c=CH) for m in (0, 1))
        wd16 = wh[:, 2].rearrange("p t (c o) -> p t c o", c=CH)
        wmax = sb("w_max", [P, 3])
        wall = sb("w_all", [P, 3])
        wscale = sb("w_scale", [P, 3])
        unscale = sb("unscale", [P, 3])
        wr = sb("w_router", [P, 2, E])
        sgl = sb("sg_load", [P, CS, D])
        sul = sb("su_load", [P, CS, D])
        sdl = sb("sd_load", [P, 2, HS])
        rl = sb("r_load", [P, D])
        cbias = sb("c_bias", [P, E])
        id32 = sb("id32b", [P, P])
        idb = sb("idb", [P, P], BF16)
        lower = sb("lower", [P, 4, 4])
        pick = sb("pick", [P, CR, P], BF16)
        xb = sb("xb", [P, 2, SUB, D])
        xT = sb("xTb", [P, 2, 2, TB])
        cT = sb("cT", [P, 2, TB], BF16)
        sig = sb("sig", [P, 2, TB])
        hid = sb("hid", [P, 2, TB])
        hid16 = sb("hid16", [P, 4, 2, TB], F16)
        xT16 = sb("xT16", [P, 2, 2, 2, TB], F16)
        sc = sb("sc", [P, SUB, E])
        sbias = sb("sbias", [P, SUB, E])
        masked = sb("masked", [P, SUB, E])
        w = sb("w", [P, SUB, E])
        mx = sb("mx", [P, SUB * 4, 2])
        mn = sb("mn", [P, SUB * 4, 2])
        tp = sb("tp", [P, 4, SUB * 4])
        gsum = sb("gsum", [P, SUB, 4])
        gmask = sb("gmask", [P, SUB, 4])
        gpen = sb("gpen", [P, SUB, 4])
        cg = sb("cg", [P, 2, SUB, 4, 4])
        best = sb("best", [P, SUB, 8])
        sel = sb("sel", [P, SUB, E])
        wsum = sb("wsum", [P, SUB])
        comb = sb("comb", [P, SUB, P], BF16)
        y = sb("yb", [P, SUB, D])
        st6 = sb("st6b", [P, SUB, 6])
        mv = sb("mvb", [P, SUB, 2])
        rstd = sb("rstdb", [P, SUB])
        ru = sb("rub", [P, SUB])
        spare = sb("spareb", [P, 1])

        psG, psU, psD = ps("psG", [P, 2, TB]), ps("psU", [P, 2, TB]), ps("psD", [P, 2, TB])
        psC, psF = ps("psC", [P, TB]), ps("psF", [P, TB])
        psFh = psF[:].bitcast(BF16)

        loads = [sem(n) for n in ("gate_loaded", "up_loaded", "down_loaded")]
        shared_loaded = sem("shared_loaded")
        high_setup = sem("high_setup")
        pool_setup, pe_setup, dve_setup = sem("fpool_setup"), sem("fpe_setup"), sem("fdve_setup")
        x_loaded = [sem(f"fx_loaded{k}") for k in range(2)]
        stored = sem("stored")
        wmax_all = sem("wmax_all")
        PE_F = Steps(sem("pe_front"), ["x0", "x1", "logits", "comb"])
        AC_F = Steps(sem("act_front"), ["x0", "h0", "x1", "h1", "sigmoid"])
        DV_X = Steps(sem("fdve_x"), ["l0", "l1"])
        RSTEPS = ["sb", "mx", "mn", "top1", "t2a", "t2b", "top2", "gsum", "ggt", "geq", "gtie", "gall", "grank",
                  "gmask", "gpen", "m1", "masked", *[f"best{s}" for s in range(SUB)], "spent",
                  *[f"taken{s}" for s in range(SUB)], "esel", "w", "ws", "wr", "rec",
                  "comb", "c1", "r1", "c2", "r2", "c3", "cT"]
        DV_F = Steps(sem("dve_front"), RSTEPS)
        PE_C = Steps(sem("pe_chunk"), [f"{n}{c}" for c in range(CH) for n in ("gate", "up", "comb")[:3 if c < CR else 2]])
        down_done = sem("down_done")
        sig_done = sem("sig_done")
        high_done, low_done = sem("high_done"), sem("low_done")
        DV_C = Steps(sem("dve_chunk"), [f"{n}{c}" for c in range(CH) for n in ("g", "u", "h")[:3 if c < CR else 2]])
        DV_L = Steps(sem("dve_lnb"), ["y"] + [f"s{i}" for i in range(SUB)] + [f"a{i}" for i in range(SUB)] + [*RSQRT]
                     + [f"n{i}" for i in range(SUB)])
        NLOADS = (2, 2, 1)
        NS = 7

        block = ctx.enter_context(nc.Block())

        def tiles(eng, prologue, main, tail):
            prologue()
            main(0, 0, "first")
            with eng.Fori(0, (NTB - 2) // 2) as h:
                for odd in range(2):
                    main(h * 2 + 1 + odd, 1 - odd, "")
            main(NTB - 1, 1, "last")
            tail()

        def rows(a, i):
            return a[bass.ds(i * TB, TB), :].rearrange("(s p) d -> p s d", p=P)

        def step(S, ins):
            ins.then_inc(S.sem, 1)

        def last_of(c):
            return f"h{c}" if c < CR else f"u{c}"

        @block.sync
        def _(sp):
            def load(i, k):
                sp.dma_start(xb[:, k], rows(x1, i)).then_inc(x_loaded[k], 16)

            def prologue():
                load(0, 0)
                sp.dma_start(rl[0:E], rw).then_inc(shared_loaded, 16)
                sp.dma_start(cbias[:], cb.partition_broadcast(P)).then_inc(shared_loaded, 16)
                for half in range(2):
                    sp.dma_start(wg[:, half, 0:CR, :].rearrange("p c (e h) -> p (c e) h", e=2),
                                 gw[:, P * half:P * half + P, :].rearrange("e c h -> c e h")).then_inc(loads[0], 16)
                sp.dma_start(wd[:, 0:CR, :], dw.rearrange("(c e) h o -> (e h) c o", e=2)).then_inc(loads[2], 16)
                sp.sem_inc(stored, 16)

            def store(i):
                DV_L.wait(sp, i, f"n{SUB - 1}")
                sp.dma_start(rows(out, i), y[:]).then_inc(stored, 16)

            def main(i, k, edge):
                if edge != "last":
                    if edge != "first":
                        DV_L.wait(sp, i - 1, "y")
                    load(i + 1, 1 - k)
                if edge != "first":
                    store(i - 1)

            def tail():
                store(NTB - 1)
                sp.wait_ge(stored, 16 * (NTB + 1))
            tiles(sp, prologue, main, tail)

        @block.gpsimd
        def _(pool):
            link, c = small_math(pool, nc, pool_setup)
            link(nc.gpsimd.memset(id32[:], 0.0))
            link(nc.gpsimd.affine_select(out=id32[:], in_=id32[:], compare_op=ALU.not_equal, fill=1.0, base=0,
                                         pattern=[[-1, P]], channel_multiplier=1))
            link(nc.gpsimd.tensor_copy(idb[:], id32[:]))
            link(nc.gpsimd.memset(lower[:], 1.0))
            link(nc.gpsimd.affine_select(out=lower[:], in_=lower[:], compare_op=ALU.is_gt, fill=0.0, base=0,
                                         pattern=[[1, 4], [-1, 4]], channel_multiplier=0))
            link(nc.gpsimd.memset(pick[:], 0.0))
            for part in range(3):
                v = pick[:].rearrange("p c (e h) -> p c e h", e=2)
                link(nc.gpsimd.affine_select(out=v, in_=v, compare_op=ALU.not_equal, fill=1.0, base=-E * part,
                                             pattern=[[-2, CR], [-1, 2], [0, EH]], channel_multiplier=1))
            link(nc.gpsimd.memset(comb[:], 0.0))
            assert c[0] == FPOOL_SETUP
            pool.wait_ge(dve_setup, MAXIMA)
            nc.gpsimd.partition_all_reduce(wall[:], wmax[:], P, bass.bass_isa.ReduceOp.max).then_inc(wmax_all, 1)

        @block.scalar
        def _(act):
            def front(i, k, what):
                if what < 2:
                    PE_F.wait(act, i, f"x{what}")
                    step(AC_F, nc.scalar.mul(xT[:, k, what, :], psF[:], XS))
                    step(AC_F, nc.scalar.mul(xT16[:, k, 0, what, :], psF[:], XS))
                else:
                    PE_F.wait(act, i, "logits")
                    step(AC_F, nc.scalar.activation(sc[:].rearrange("p s e -> p (s e)"), psF[:, 0:SUB * E], ACT.Sigmoid,
                                                    scale=1.0 / XS))

            def high(i, c, edge):
                if not (edge == "first" and c < 4):
                    act.wait_ge(down_done, i * CH + c - 3)
                DV_C.wait(act, i, last_of(c))
                nc.scalar.copy(hid16[:, c % 4, 0, :], hid[:, c % 2, :]).then_inc(high_done, 1)

            def prologue():
                for src, dst in ((sgw, sgl), (suw, sul), (sdw, sdl)):
                    act.dma_start(dst[:], src.rearrange("(s p) d -> p s d", p=P)).then_inc(shared_loaded, 16)
                for half in range(2):
                    act.dma_start(wu[:, half, 0:CR, :].rearrange("p c (e h) -> p (c e) h", e=2),
                                  uw[:, P * half:P * half + P, :].rearrange("e c h -> c e h")).then_inc(loads[1], 16)
                for what in range(3):
                    front(0, 0, what)
                act.wait_ge(dve_setup, SCALES)
                for m in range(3):
                    nc.scalar.activation(wh[:, m, 0], wf[:, m], ACT.Identity, scale=wscale[:, m:m + 1]).then_inc(high_setup, 1)

            def main(i, k, edge):
                for c in range(CH):
                    PE_C.wait(act, i, f"gate{c}")
                    if c >= 2:
                        DV_C.wait(act, i, f"u{c - 2}")
                    elif edge != "first":
                        DV_C.wait(act, i - 1, f"u{CH - 2 + c}")
                    nc.scalar.activation(sig[:, c % 2, :], psG[:, c % 2, :], ACT.Sigmoid,
                                         scale=unscale[:, 0:1]).then_inc(sig_done, 1)
                    if c:
                        high(i, c - 1, edge)
                    elif edge != "first":
                        high(i - 1, CH - 1, "")
                    if edge != "last" and c in (4, 5, 7):
                        front(i + 1, 1 - k, (4, 5, 7).index(c))
            tiles(act, prologue, main, lambda: high(NTB - 1, CH - 1, ""))

        @block.vector
        def _(dve):
            V = nc.vector
            banks = [psG[:, 0], psG[:, 1], psU[:, 0], psU[:, 1], psD[:, 0], psD[:, 1]]
            dsts = [wg[:, 0, CR:], wg[:, 1, CR:], wu[:, 0, CR:], wu[:, 1, CR:], wd[:, CR:, 0:P], wd[:, CR:, P:2 * P]]
            for n, (bank, dst) in enumerate(zip(banks, dsts)):
                dve.wait_ge(pe_setup, n + 2)
                V.tensor_copy(dst, bank.rearrange("p (s t) -> p s t", t=P)).then_inc(dve_setup, 1)
                if n == 0:
                    V.tensor_copy(wr[:], psC[:, 0:2 * E].rearrange("p (a e) -> p a e", a=2)).then_inc(dve_setup, 1)

            def find_maxima(*matrices):
                dve.wait_ge(dve_setup, NS)
                for m in matrices:
                    dve.wait_ge(loads[m], 16 * NLOADS[m])
                    V.tensor_reduce(wmax[:, m:m + 1], wf[:, m], AX, ALU.max, apply_absolute_value=True).then_inc(dve_setup, 1)

            def scale_weights():
                done = MAXIMA

                def link(ins):
                    nonlocal done
                    ins.then_inc(dve_setup, 1)
                    done += 1
                    dve.wait_ge(dve_setup, done)
                I32 = mybir.dt.int32
                dve.wait_ge(wmax_all, 1)
                link(V.tensor_scalar(wall[:], wall[:], 1e-15, None, ALU.max))
                link(V.tensor_scalar(wall[:].bitcast(I32), wall[:].bitcast(I32), 0x7f800000, None, ALU.bitwise_and))
                link(V.reciprocal(wscale[:], wall[:]))
                link(V.tensor_scalar(unscale[:, 1:2], wscale[:, 0:1], 2.0 ** -13 / XS, None, ALU.mult))
                link(V.tensor_scalar(wscale[:], wscale[:], 2.0 ** 10, None, ALU.mult))
                link(V.tensor_scalar(unscale[:, 0:1], wall[:, 0:1], 2.0 ** -10 / XS, None, ALU.mult))
                link(V.scalar_tensor_tensor(out=unscale[:, 2:3], in0=wall[:, 0:1], scalar=2.0 ** -7, in1=wall[:, 1:2], op0=ALU.mult, op1=ALU.mult))
                link(V.tensor_tensor(unscale[:, 2:3], unscale[:, 2:3], wall[:, 2:3], ALU.mult))
                assert done == SCALES
                for m in range(3):
                    dve.wait_ge(high_setup, m + 1)
                    V.scalar_tensor_tensor(out=wh[:, m, 1], in0=wf[:, m], scalar=wscale[:, m:m + 1], in1=wh[:, m, 0],
                                           op0=ALU.mult, op1=ALU.subtract).then_inc(dve_setup, 1)

            def low_x(i, k):
                for a in range(2):
                    AC_F.wait(dve, i, f"h{a}")
                    step(DV_X, V.tensor_tensor(xT16[:, k, 1, a, :], xT[:, k, a, :], xT16[:, k, 0, a, :], ALU.subtract))

            def low(i, c):
                dve.wait_ge(high_done, i * CH + c + 1)
                V.tensor_tensor(hid16[:, c % 4, 1, :], hid[:, c % 2, :], hid16[:, c % 4, 0, :], ALU.subtract).then_inc(low_done, 1)

            def tt(i, name, out_, a, b, op, after=None):
                if after:
                    DV_F.wait(dve, i, after)
                step(DV_F, V.tensor_tensor(out_, a, b, op))

            def router_steps(i, k):
                four = [P, SUB, 4, 4]
                mxv, mnv = mx[:], mn[:]
                g3 = masked[:].rearrange("p s (g m) -> p (s g) m", m=4)
                sb3 = sbias[:].rearrange("p s (g m) -> p (s g) m", m=4)
                gm3 = gmask[:].rearrange("p s g -> p (s g)").unsqueeze(2).to_broadcast([P, SUB * 4, 4])
                gp3 = gpen[:].rearrange("p s g -> p (s g)").unsqueeze(2).to_broadcast([P, SUB * 4, 4])

                def s0():
                    AC_F.wait(dve, i, "sigmoid")
                    tt(i, "sb", sbias[:], sc[:], cbias[:].unsqueeze(1).to_broadcast([P, SUB, E]), ALU.add)
                    tt(i, "mx", mxv, sb3[:, :, 0:4:2], sb3[:, :, 1:4:2], ALU.max, "sb")
                    tt(i, "mn", mnv, sb3[:, :, 0:4:2], sb3[:, :, 1:4:2], ALU.min)
                    tt(i, "top1", tp[:, 0], mxv[:, :, 0], mxv[:, :, 1], ALU.max, "mx")
                    tt(i, "t2a", tp[:, 1], mxv[:, :, 0], mxv[:, :, 1], ALU.min)
                    tt(i, "t2b", tp[:, 2], mnv[:, :, 0], mnv[:, :, 1], ALU.max, "mn")
                    tt(i, "top2", tp[:, 3], tp[:, 1], tp[:, 2], ALU.max, "t2b")
                    tt(i, "gsum", gsum[:].rearrange("p s g -> p (s g)"), tp[:, 0], tp[:, 3], ALU.add, "top2")

                def s1():
                    other, own = gsum[:].unsqueeze(2).to_broadcast(four), gsum[:].unsqueeze(3).to_broadcast(four)
                    tt(i, "ggt", cg[:, 0], other, own, ALU.is_gt, "gsum")
                    tt(i, "geq", cg[:, 1], other, own, ALU.is_equal)
                    tt(i, "gtie", cg[:, 1], cg[:, 1], lower[:].unsqueeze(1).to_broadcast(four), ALU.mult, "geq")
                    tt(i, "gall", cg[:, 0], cg[:, 0], cg[:, 1], ALU.add, "gtie")
                    DV_F.wait(dve, i, "gall")
                    step(DV_F, V.tensor_reduce(gpen[:], cg[:, 0], AX, ALU.add))
                    DV_F.wait(dve, i, "grank")
                    step(DV_F, V.tensor_scalar(gmask[:], gpen[:], 2.0, None, ALU.is_lt))
                    DV_F.wait(dve, i, "gmask")
                    step(DV_F, V.tensor_scalar(gpen[:], gmask[:], 1.0, 1e30, ALU.subtract, ALU.mult))
                    tt(i, "m1", g3, sb3, gm3, ALU.mult, "gpen")
                    tt(i, "masked", g3, g3, gp3, ALU.add, "m1")

                def s2():
                    DV_F.wait(dve, i, "masked")
                    V.memset(spare[:], 0.0)
                    for s in range(SUB):
                        step(DV_F, V.max(best[:, s], masked[:, s]))
                    DV_F.wait(dve, i, f"best{SUB - 1}")
                    step(DV_F, V.memset(best[:, :, 4:8], TAKEN))

                def s3():
                    DV_F.wait(dve, i, "spent")
                    V.memset(spare[:], 0.0)
                    for s in range(SUB):
                        step(DV_F, V.match_replace(sel[:, s], best[:, s], masked[:, s], TAKEN))

                def s4():
                    DV_F.wait(dve, i, f"taken{SUB - 1}")
                    step(DV_F, V.tensor_scalar(sel[:], sel[:], TAKEN, None, ALU.is_equal))
                    tt(i, "w", w[:], sc[:], sel[:], ALU.mult, "esel")
                    DV_F.wait(dve, i, "w")
                    step(DV_F, V.tensor_reduce(wsum[:], w[:], AX, ALU.add))
                    DV_F.wait(dve, i, "ws")
                    step(DV_F, V.tensor_scalar(wsum[:], wsum[:], 1e-20, None, ALU.add))

                def s5():
                    DV_F.wait(dve, i, "wr")
                    step(DV_F, V.reciprocal(wsum[:], wsum[:]))
                return s0, s1, s2, s3, s4, s5

            def combine(i, k):
                c1, c2, c3 = (comb[:, :, E * n:E * n + E] for n in range(3))
                tt(i, "comb", w[:], w[:], wsum[:].unsqueeze(2).to_broadcast([P, SUB, E]), ALU.mult, "rec")
                DV_F.wait(dve, i, "comb")
                step(DV_F, V.tensor_copy(c1, w[:]))
                tt(i, "r1", w[:], w[:], c1, ALU.subtract, "c1")
                DV_F.wait(dve, i, "r1")
                step(DV_F, V.tensor_copy(c2, w[:]))
                tt(i, "r2", w[:], w[:], c2, ALU.subtract, "c2")
                DV_F.wait(dve, i, "r2")
                step(DV_F, V.tensor_copy(c3, w[:]))

            def copy_comb(i, k):
                PE_F.wait(dve, i, "comb")
                step(DV_F, V.tensor_copy(cT[:, k, :], psFh[:, 0:TB]))

            def chunk(i, k, c, edge):
                dve.wait_ge(sig_done, i * CH + c + 1)
                step(DV_C, V.scalar_tensor_tensor(out=sig[:, c % 2], in0=psG[:, c % 2], scalar=unscale[:, 0:1],
                                                  in1=sig[:, c % 2], op0=ALU.mult, op1=ALU.mult))
                if c:
                    low(i, c - 1)
                elif edge != "first":
                    low(i - 1, CH - 1)
                PE_C.wait(dve, i, f"up{c}")
                if c >= 2 or edge != "first":
                    dve.wait_ge(low_done, i * CH + c - 1)
                DV_C.wait(dve, i, f"g{c}")
                step(DV_C, V.scalar_tensor_tensor(out=hid[:, c % 2], in0=psU[:, c % 2], scalar=unscale[:, 1:2],
                                                  in1=sig[:, c % 2], op0=ALU.mult, op1=ALU.mult))
                if c < CR:
                    PE_C.wait(dve, i, f"comb{c}")
                    DV_C.wait(dve, i, f"u{c}")
                    step(DV_C, V.tensor_tensor(hid[:, c % 2], hid[:, c % 2], psC[:], ALU.mult))

            def residual(i, k):
                dve.wait_ge(down_done, i * CH + CH)
                dve.wait_ge(stored, i * 16 + 16)
                step(DV_L, V.scalar_tensor_tensor(out=y[:].rearrange("p s d -> p (s d)"), in0=psD[:].rearrange("p a b -> p (a b)"),
                                                  scalar=unscale[:, 2:3], in1=xb[:, k].rearrange("p s d -> p (s d)"),
                                                  op0=ALU.mult, op1=ALU.add))

            def norm_stats(i):
                DV_L.wait(dve, i, "y")
                for s in range(SUB):
                    step(DV_L, V.bn_stats(st6[:, s, :], y[:, s, :]))
                DV_L.wait(dve, i, f"s{SUB - 1}")
                V.memset(spare[:], 0.0)
                for s in range(SUB):
                    step(DV_L, V.bn_aggr(mv[:, s, :], st6[:, s, :]))

            def norm_out(i):
                rsqrt(dve, V, DV_L, i, f"a{SUB - 1}", rstd[:], mv[:, :, 1], ru[:], 1e-5, 1.0)
                DV_L.wait(dve, i, RSQRT[-1])
                for s in range(SUB):
                    step(DV_L, V.tensor_scalar(y[:, s, :], y[:, s, :], mv[:, s, 0:1], rstd[:, s:s + 1],
                                               ALU.subtract, ALU.mult))

            def prologue():
                low_x(0, 0)
                find_maxima(0)
                for s in router_steps(0, 0):
                    s()
                combine(0, 0)
                find_maxima(2, 1)
                copy_comb(0, 0)
                scale_weights()

            def main(i, k, edge):
                steps = router_steps(i + 1, 1 - k)
                for c in range(CH):
                    chunk(i, k, c, edge)
                    if edge != "first":
                        if c == 1:
                            residual(i - 1, 1 - k)
                        if c == 2:
                            norm_stats(i - 1)
                        if c == 3:
                            norm_out(i - 1)
                    if edge != "last":
                        if c == 6:
                            low_x(i + 1, 1 - k)
                        if c == 7:
                            steps[0]()
                            steps[1]()
                        if c == 8:
                            steps[2]()
                        if c == 9:
                            steps[3]()
                            steps[4]()
                            steps[5]()
                        if c == 10:
                            combine(i + 1, 1 - k)
                if edge != "last":
                    copy_comb(i + 1, 1 - k)

            def tail():
                low(NTB - 1, CH - 1)
                residual(NTB - 1, 1)
                norm_stats(NTB - 1)
                norm_out(NTB - 1)
            tiles(dve, prologue, main, tail)

        @block.tensor
        def _(pe):
            pe.wait_ge(pool_setup, FPOOL_SETUP)
            pe.wait_ge(shared_loaded, 16 * 5)
            for a in range(2):
                mm = pe.transpose(psC[:, E * a:E * a + E], rl[0:E, P * a:P * a + P], id32[0:E, 0:E])
            mm.then_inc(pe_setup, 1)
            for src, dst in ((sgl, psG), (sul, psU)):
                for a in range(2):
                    for s in range(CS):
                        mm = pe.transpose(dst[:, a, P * s:P * s + P], src[:, s, P * a:P * a + P], id32[:])
                    mm.then_inc(pe_setup, 1)
            for r in range(2):
                for s in range(CS):
                    mm = pe.transpose(psD[:, r, P * s:P * s + P], sdl[:, r, P * s:P * s + P], id32[:])
                mm.then_inc(pe_setup, 1)

            def front_x(i, k, a, load):
                if a == 0:
                    pe.wait_ge(x_loaded[k], load * 16 + 16)
                else:
                    AC_F.wait(pe, i, "h0")
                for s in range(SUB):
                    mm = pe.transpose(psF[:, P * s:P * s + P], xb[:, k, s, P * a:P * a + P], id32[:])
                step(PE_F, mm)

            def front_logits(i, k):
                AC_F.wait(pe, i, "h1")
                for s in range(SUB):
                    for a in range(2):
                        mm = pe.matmul(psF[:, E * s:E * s + E], xT[:, k, a, P * s:P * s + P], wr[:, a, :], start=(a == 0), stop=(a == 1))
                step(PE_F, mm)

            def front_comb(i, k):
                DV_F.wait(pe, i, "c3")
                for s in range(SUB):
                    mm = pe.transpose(psFh[:, P * s:P * s + P], comb[:, s, :], idb[:])
                step(PE_F, mm)

            def gate_up(i, k, c, edge):
                for w_, ps_, name in ((wg16, psG, "gate"), (wu16, psU, "up")):
                    if name == "gate":
                        if c >= 2:
                            DV_C.wait(pe, i, f"u{c - 2}")
                        elif edge != "first":
                            DV_C.wait(pe, i - 1, f"u{CH - 2 + c}")
                    for a in range(2):
                        for wp, xp in ((0, 0), (0, 1), (1, 0)):
                            mm = pe.matmul(ps_[:, c % 2, :], w_[:, wp, a, c, :], xT16[:, k, xp, a, :],
                                           start=(a == 0 and wp == xp), stop=(a == 1 and wp == 1))
                    step(PE_C, mm)
                if c == 0:
                    DV_F.wait(pe, i, "cT")
                if c < CR:
                    if c:
                        DV_C.wait(pe, i, f"h{c - 1}")
                    elif edge != "first":
                        DV_C.wait(pe, i - 1, f"h{CR - 1}")
                    step(PE_C, pe.matmul(psC[:], pick[:, c, :], cT[:, k, :], start=True, stop=True))

            def down(i, c, first_tile):
                pe.wait_ge(low_done, i * CH + c + 1)
                if c == 0 and first_tile:
                    pe.wait_ge(dve_setup, SCALES + 3)
                elif c == 0:
                    DV_L.wait(pe, i - 1, "y")
                for s in range(SUB):
                    for hp, wp in ((0, 0), (0, 1), (1, 0)):
                        mm = pe.matmul(psD[:, s // 2, D * (s % 2):D * (s % 2) + D], hid16[:, c % 4, hp, P * s:P * s + P],
                                       wd16[:, wp, c, :], start=(c == 0 and s % 2 == 0 and hp == wp),
                                       stop=(c == CH - 1 and hp == 1), skip_group_check=True)
                mm.then_inc(down_done, 1)

            def prologue():
                pe.wait_ge(dve_setup, NS)
                front_x(0, 0, 0, 0)
                front_x(0, 0, 1, 0)
                front_logits(0, 0)
                front_comb(0, 0)
                pe.wait_ge(dve_setup, SCALES + 2)

            def main(i, k, edge, load):
                for c in range(CH):
                    if c == 0:
                        DV_X.wait(pe, i, "l1")
                    gate_up(i, k, c, edge)
                    if c >= 2:
                        down(i, c - 2, edge == "first")
                    elif edge != "first":
                        down(i - 1, CH - 2 + c, False)
                    if edge != "last":
                        if c in (3, 4):
                            front_x(i + 1, 1 - k, c - 3, load)
                        if c == 6:
                            front_logits(i + 1, 1 - k)
                        if c == 11:
                            front_comb(i + 1, 1 - k)

            prologue()
            main(0, 0, "first", 0)
            with pe.Fori(0, (NTB - 2) // 2) as h:
                for odd in range(2):
                    main(h * 2 + 1 + odd, 1 - odd, "", h + 1)
            main(NTB - 1, 1, "last", None)
            for c in (CH - 2, CH - 1):
                down(NTB - 1, c, False)


FPOOL_SETUP = 10
MAXIMA = 7 + 3
SCALES = MAXIMA + 8

_INS = ["L0_attn_x", "L0_attn_qW", "L0_attn_qb", "L0_attn_kW", "L0_attn_kb", "L0_attn_vW", "L0_attn_vb", "L0_attn_oW",
        "L0_attn_ob", "L0_attn_J", "L0_ffn_router_w", "L0_ffn_correction_bias", "L0_ffn_gate_w", "L0_ffn_up_w",
        "L0_ffn_down_w", "L0_ffn_shared_gate_w", "L0_ffn_shared_up_w", "L0_ffn_shared_down_w"]


def program(nc, ins, out):
    x, qW, qb, kW, kb, vW, vb, oW, ob, J, rw, cb, gw, uw, dw, sgw, suw, sdw = ins
    x1 = nc.dram_tensor("x1", (NTOK, D), F32, kind="Internal").ap()
    attention(nc, x, qW, qb, kW, kb, vW, vb, oW, ob, J, x1)
    feed_forward(nc, x1, rw, cb, gw, uw, dw, sgw, suw, sdw, out.rearrange("b t d -> (b t) d"))


def kernel(**inputs):
    import concourse.bacc as _bacc
    from concourse.bass_utils import run_bass_kernel_spmd as _run

    nc = _bacc.Bacc("TRN2", target_bir_lowering=False, num_devices=1)
    arrays, ins = {}, []
    for name in _INS:
        a = np.ascontiguousarray(inputs[name])
        arrays[f"in_{name}"] = a
        ins.append(nc.dram_tensor(f"in_{name}", a.shape, mybir.dt.from_np(a.dtype), kind="ExternalInput").ap())
    out = nc.dram_tensor("out", (B, T, D), F32, kind="ExternalOutput").ap()
    program(nc, ins, out)
    return _run(nc, [arrays], core_ids=[0]).results[0]["out"]
```
